# Optimizing a Trainium2 kernel written in Bass

```python
import numpy as np
import jax
import jax.numpy as jnp

def _softmax(x, axis=-1):
    return jax.nn.softmax(x, axis=axis)

def _gelu(x):
    return jax.nn.gelu(x, approximate=True)

def _silu(x):
    return jax.nn.silu(x)

def _sigmoid(x):
    return jax.nn.sigmoid(x)

def _layernorm(x, axis=-1, eps=1e-05):
    m = jnp.mean(x, axis=axis, keepdims=True)
    v = jnp.var(x, axis=axis, keepdims=True)
    return (x - m) / jnp.sqrt(v + eps)

def _scatter_add(tgt, idx, src, axis=0):
    return tgt.at[idx].add(src)

def _segment_sum(src, seg, n):
    return jax.ops.segment_sum(src, seg, n)
kernel_name = 'mk_adaln_d1_jaxref_r4_9e13ce'

def setup_inputs(seed: int=0):
    np.random.seed(seed)
    _w = jnp.asarray

    def _L0_attn_setup():
        import jax, jax.numpy as jnp
        import numpy as np
        B, SQ, H = (2, 512, 512)
        NH = 16
        HN = H // NH
        key = jax.random.key(seed)
        ks = jax.random.split(key, 6)
        query = jax.random.normal(ks[0], (B, SQ, H), dtype=jnp.float32)
        k_in = jax.random.normal(ks[1], (B, SQ, H), dtype=jnp.float32)
        v_in = jax.random.normal(ks[2], (B, SQ, H), dtype=jnp.float32)
        Wqkv = jax.random.normal(ks[3], (3 * H, H), dtype=jnp.float32) * (1.0 / np.sqrt(H))
        Wproj = jax.random.normal(ks[4], (H, H), dtype=jnp.float32) * (1.0 / np.sqrt(H))
        bproj = jnp.zeros((H,), dtype=jnp.float32)
        return {'query': query, 'key': k_in, 'value': v_in, 'Wqkv': Wqkv, 'Wproj': Wproj, 'bproj': bproj}
    _L0_attn_in = _L0_attn_setup()

    def _L0_ffn_setup():
        import jax, jax.numpy as jnp
        import numpy as np
        B, S, H = (1, 256, 512)
        E, K = (32, 4)
        F, FS = (352, 1408)
        CAP = 64

        def silu(x):
            return x * jax.nn.sigmoid(x)
        key = jax.random.key(seed)
        ks = jax.random.split(key, 9)
        sc = 0.02
        return {'hidden_states': jax.random.normal(ks[0], (B, S, H), jnp.float32), 'Wr': jax.random.normal(ks[1], (H, E), jnp.float32) * sc, 'Wg': jax.random.normal(ks[2], (E, H, F), jnp.float32) * sc, 'Wu': jax.random.normal(ks[3], (E, H, F), jnp.float32) * sc, 'Wd': jax.random.normal(ks[4], (E, F, H), jnp.float32) * sc, 'Wsg': jax.random.normal(ks[5], (H, FS), jnp.float32) * sc, 'Wsu': jax.random.normal(ks[6], (H, FS), jnp.float32) * sc, 'Wsd': jax.random.normal(ks[7], (FS, H), jnp.float32) * sc, 'Wse': jax.random.normal(ks[8], (H, 1), jnp.float32) * sc}
    _L0_ffn_in = _L0_ffn_setup()
    _L0_c = _w((lambda *s: np.random.randn(*s).astype(np.float32) * 0.05)(2, 512))
    _L0_wmod = _w((lambda *s: np.random.randn(*s).astype(np.float32) * 0.05)(512, 6 * 512) * 512 ** (-0.5))
    _d = {'L0_attn_query': _L0_attn_in['query'], 'L0_attn_key': _L0_attn_in['key'], 'L0_attn_value': _L0_attn_in['value'], 'L0_attn_Wqkv': _L0_attn_in['Wqkv'], 'L0_attn_Wproj': _L0_attn_in['Wproj'], 'L0_attn_bproj': _L0_attn_in['bproj'], 'L0_ffn_Wr': _L0_ffn_in['Wr'], 'L0_ffn_Wg': _L0_ffn_in['Wg'], 'L0_ffn_Wu': _L0_ffn_in['Wu'], 'L0_ffn_Wd': _L0_ffn_in['Wd'], 'L0_ffn_Wsg': _L0_ffn_in['Wsg'], 'L0_ffn_Wsu': _L0_ffn_in['Wsu'], 'L0_ffn_Wsd': _L0_ffn_in['Wsd'], 'L0_ffn_Wse': _L0_ffn_in['Wse'], 'L0_c': _L0_c, 'L0_wmod': _L0_wmod}
    _x0 = _d['L0_attn_query']
    _d['L0_attn_query'] = jax.random.normal(jax.random.fold_in(jax.random.key(seed), 1), (2, 1024, 512), dtype=_x0.dtype)
    del _x0
    return _d

def reference(L0_attn_query, L0_attn_key, L0_attn_value, L0_attn_Wqkv, L0_attn_Wproj, L0_attn_bproj, L0_ffn_Wr, L0_ffn_Wg, L0_ffn_Wu, L0_ffn_Wd, L0_ffn_Wsg, L0_ffn_Wsu, L0_ffn_Wsd, L0_ffn_Wse, L0_c, L0_wmod):

    def _L0_attn_ref(query, key, value, Wqkv, Wproj, bproj):
        import jax, jax.numpy as jnp
        import numpy as np
        B, SQ, H = (2, 512, 512)
        NH = 16
        HN = H // NH
        b, sq, h = query.shape
        nh, hn = (NH, HN)
        norm = 1.0 / jnp.sqrt(jnp.asarray(hn, query.dtype))
        x = jnp.transpose(query, (1, 0, 2)).reshape(sq * b, h)
        mixed = x @ Wqkv.T
        mixed = mixed.reshape(sq, b, nh, 3, hn)
        q = mixed[..., 0, :]
        k = mixed[..., 1, :]
        v = mixed[..., 2, :]
        q = q.reshape(sq, b * nh, hn).transpose(1, 0, 2)
        k = k.reshape(sq, b * nh, hn).transpose(1, 0, 2)
        v = v.reshape(sq, b * nh, hn).transpose(1, 0, 2)
        attn = jnp.einsum('gqd,gkd->gqk', q, k) * norm
        attn = jax.nn.softmax(attn, axis=-1)
        ctx = jnp.einsum('gqk,gkd->gqd', attn, v)
        ctx = ctx.reshape(nh, b, sq, hn)
        ctx = jnp.transpose(ctx, (2, 1, 0, 3)).reshape(sq * b, h)
        out = ctx @ Wproj.T + bproj
        out = out.reshape(sq, b, h)
        return jnp.transpose(out, (1, 0, 2))

    def _L0_ffn_ref(hidden_states, Wr, Wg, Wu, Wd, Wsg, Wsu, Wsd, Wse):
        import jax, jax.numpy as jnp
        import numpy as np
        B, S, H = (1, 256, 512)
        E, K = (32, 4)
        F, FS = (352, 1408)
        CAP = 64

        def silu(x):
            return x * jax.nn.sigmoid(x)
        b, s_len, h = hidden_states.shape
        x = hidden_states.reshape(-1, h)
        T = x.shape[0]
        probs = jax.nn.softmax(x @ Wr, axis=-1)
        topw, topi = jax.lax.top_k(probs, K)
        topw = topw / jnp.sum(topw, axis=-1, keepdims=True)
        shared = silu(x @ Wsg) * (x @ Wsu) @ Wsd
        shared = shared * jax.nn.sigmoid(x @ Wse)
        sel = topi.reshape(-1)
        w = topw.reshape(-1)
        tok = jnp.repeat(jnp.arange(T), K)
        oh = jax.nn.one_hot(sel, E, dtype=jnp.int32)
        pos = (jnp.cumsum(oh, axis=0) * oh).sum(-1) - 1
        valid = (pos < CAP).astype(x.dtype)
        posc = jnp.clip(pos, 0, CAP - 1)
        xe = jnp.zeros((E, CAP, h), x.dtype).at[sel, posc].add(x[tok] * valid[:, None])
        g = silu(jnp.einsum('ech,ehf->ecf', xe, Wg))
        u = jnp.einsum('ech,ehf->ecf', xe, Wu)
        ye = jnp.einsum('ecf,efh->ech', g * u, Wd)
        y_pair = ye[sel, posc] * (w * valid)[:, None]
        out = shared.at[tok].add(y_pair)
        return out.reshape(b, s_len, h)
    x = L0_attn_query
    mod = (_silu(L0_c) @ L0_wmod).reshape(L0_c.shape[0], 6, 1, -1)
    sa, ca, ga, sb, cb, gb = (mod[:, 0], mod[:, 1], mod[:, 2], mod[:, 3], mod[:, 4], mod[:, 5])
    ga = (2 * (ga >= 0) - 1) * jnp.maximum(jnp.abs(ga), 0.25)
    gb = (2 * (gb >= 0) - 1) * jnp.maximum(jnp.abs(gb), 0.25)
    h = _layernorm(x, axis=-1) * (1 + ca) + sa
    x = x + ga * _L0_attn_ref(h, L0_attn_key, L0_attn_value, L0_attn_Wqkv, L0_attn_Wproj, L0_attn_bproj)
    h = _layernorm(x, axis=-1) * (1 + cb) + sb
    x = x + gb * _L0_ffn_ref(h, L0_ffn_Wr, L0_ffn_Wg, L0_ffn_Wu, L0_ffn_Wd, L0_ffn_Wsg, L0_ffn_Wsu, L0_ffn_Wsd, L0_ffn_Wse)
    return x

_drawn_inputs = setup_inputs


def setup_inputs(seed=0):
    import zlib

    import numpy as np

    out = dict(_drawn_inputs(seed))
    spreads = {'L0_attn_bproj': (0.0, 0.334)}
    factors = {'L0_attn_Wqkv': 3.368,
     'L0_attn_Wproj': 3.365,
     'L0_ffn_Wr': 8.0,
     'L0_ffn_Wg': 8.0,
     'L0_ffn_Wu': 8.0,
     'L0_ffn_Wd': 8.0,
     'L0_ffn_Wsg': 5.541,
     'L0_ffn_Wsu': 5.421,
     'L0_ffn_Wsd': 5.42,
     'L0_ffn_Wse': 8.0}
    for name, (base, spread) in spreads.items():
        noise = np.random.default_rng([zlib.crc32(name.encode()), seed]).standard_normal(out[name].shape)
        drawn = base * np.exp(spread * noise) if base else spread * noise
        out[name] = jnp.asarray(drawn.astype(out[name].dtype))
    for name, factor in factors.items():
        out[name] = (out[name] * factor).astype(out[name].dtype)
    return out
```

```python
from contextlib import ExitStack

import concourse.bass as bass
from concourse import mybir

ALU = mybir.AluOpType
ACT = mybir.ActivationFunctionType
AX = mybir.AxisListType
F32 = mybir.dt.float32
F32R = mybir.dt.float32r
BF16 = mybir.dt.bfloat16
U32 = mybir.dt.uint32
I32 = mybir.dt.int32

P = 128
B, S, D = 2, 1024, 512
T = B * S
KT = D // P
NH, HN = 16, 32
PAIRS = B * NH // 2
HALF = 512
TT = T // P
E, TOPK, F, CAP = 32, 4, 352, 64
FS = 1408
FT = FS // P
CH = T // HALF
SLOTS = E * CAP
EPS = 1e-5
F_TILES = [(0, 128), (128, 128), (256, 96)]
PAIR_BYTES = 4


def ge(eng, sem, value):
    if isinstance(value, int) and value <= 0:
        return
    eng.wait_ge(sem, value)


def hold(eng, passed, sem, value):
    ge(eng, sem, value)
    if not isinstance(value, int):
        eng.sem_inc(passed, 1)


def adaln_kernel(nc, x, wqk, wv, wproj, bproj, wr_se, c, wmod, wsh, wgu, wd_a, wd_b, out):
    mod_rows = nc.dram_tensor("mod_rows", (4, B, D), F32).ap()
    gb_rows = nc.dram_tensor("gb_rows", (CH, D), F32).ap()
    ctx_t = nc.dram_tensor("ctx_t", (D, B, S), F32).ap()
    x1_d = nc.dram_tensor("x1_d", (T, D), F32).ap()
    res_d = nc.dram_tensor("res_d", (T, D), F32).ap()
    xe_d = nc.dram_tensor("xe_d", (SLOTS, D), F32).ap()
    ye_d = nc.dram_tensor("ye_d", (SLOTS, D), F32).ap()

    with ExitStack() as top:
        ident = top.enter_context(nc.sbuf_tensor("ident", [P, P], F32))
        prologue_and_attention(nc, x, wqk, wv, c, wmod, mod_rows, gb_rows, ctx_t, xe_d, ident)
        slots = top.enter_context(nc.sbuf_tensor("slots", [P, TT, TOPK], U32))
        wtop = top.enter_context(nc.sbuf_tensor("wtop", [P, TT, TOPK], F32))
        gbt = top.enter_context(nc.sbuf_tensor("gbt", [P, B, D], F32))
        with ExitStack() as mid:
            sgate = mid.enter_context(nc.sbuf_tensor("sgate", [P, TT], F32))
            h2h = mid.enter_context(nc.sbuf_tensor("h2h", [P, KT, T], F32R))
            h2l = mid.enter_context(nc.sbuf_tensor("h2l", [P, KT, T], F32R))
            middle(nc, x, wproj, bproj, wr_se, mod_rows, ctx_t, x1_d, xe_d,
                   ident, slots, wtop, gbt, sgate, h2h, h2l)
            ffn(nc, wsh, wgu, wd_a, wd_b, x1_d, res_d, xe_d, ye_d, gb_rows, ident, sgate, h2h, h2l)
        combine(nc, res_d, ye_d, slots, wtop, gbt, out)


def prologue_and_attention(nc, x, wqk, wv, c, wmod, mod_rows, gb_rows, ctx_t, xe_d, ident):
    with ExitStack() as ctx:
        def sb(name, shape, dt=F32):
            return ctx.enter_context(nc.sbuf_tensor(name, shape, dt))

        hth = sb("hth", [P, KT, T], F32R)
        htl = sb("htl", [P, KT, T], F32R)
        v_all = sb("v_all", [P, TT, D])
        wqk_h = sb("wqk_h", [P, 2, KT, P], F32R)
        wqk_l = sb("wqk_l", [P, 2, KT, P], F32R)
        prologue(nc, x, wv, c, wmod, mod_rows, gb_rows, xe_d, ident, hth, htl, v_all)
        attention(nc, wqk, ctx_t, ident, hth, htl, v_all, wqk_h, wqk_l)


def prologue(nc, x, wv, c, wmod, mod_rows, gb_rows, xe_d, ident, hth, htl, v_all):
    GROUPS = T // HALF
    with ExitStack() as ctx:
        def sb(name, shape, dt=F32):
            return ctx.enter_context(nc.sbuf_tensor(name, shape, dt))

        def sem(name):
            return ctx.enter_context(nc.semaphore(name))

        c_sb = sb("c_sb", [P, KT, B])
        c_e = sb("c_e", [P, KT, B])
        c_silu = sb("c_silu", [P, KT, B])
        wm = sb("wm", [P, 2, 6 * D])
        rows = sb("rows", [P, 2, D])
        gate_s = sb("gate_s", [P, 2, D])
        gate_a = sb("gate_a", [P, 2, D])
        mod_t = sb("mod_t", [P, 2, KT, B])
        zero = sb("zero", [P, D])
        x_sb = sb("x_sb", [P, 4, D])
        xhat = sb("xhat", [P, 4, D])
        stats = sb("stats", [P, 4, 6])
        mv = sb("mv", [P, 4, 2])
        veps = sb("veps", [P, 4])
        rstd = sb("rstd", [P, 4])
        mhalf = sb("mhalf", [P, 4])
        hmod = sb("hmod", [P, 2, HALF])
        wv_raw = sb("wv_raw", [P, KT, D])
        wv_h = sb("wv_h", [P, KT, D], F32R)
        wv_l = sb("wv_l", [P, KT, D], F32R)
        banks = [ctx.enter_context(nc.psum_tensor(f"pro_bank{n}", [P, HALF], F32)) for n in range(8)]
        ps_mod, ps_modt, ps_v, ps_t = banks[0:2], banks[2:4], banks[0:4], banks[4:8]

        s_c = sem("c_loaded")
        s_wm = [sem("wmod_loaded0"), sem("wmod_loaded1")]
        s_wv = sem("wv_loaded")
        s_x = [sem(f"x_loaded{n}") for n in range(4)]
        s_e = sem("c_exp_done")
        s_silu = sem("c_silu_step")
        s_modk = sem("mod_k_done")
        s_rows = sem("rows_step")
        s_modt = sem("mod_t_done")
        s_modc = sem("mod_cols_ready")
        s_rowst = sem("rows_stored")
        s_id = sem("ident_step")
        s_zero = sem("zero_ready")
        s_xe = sem("xe_zeroed")
        s_stat = sem("stats_step")
        s_rstd = sem("rstd_ready")
        s_xh = sem("xhat_ready")
        s_tr = sem("transposed")
        s_hm = sem("hmod_ready")
        s_hh = sem("hth_ready")
        s_hl = sem("htl_ready")
        s_wvs = sem("wv_split")
        s_vps = sem("v_product_done")
        s_vev = sem("v_copied")

        x_t = x.rearrange("b s d -> (b s) d").rearrange("(n p) d -> n p d", p=P)
        wm_t = wmod.rearrange("(k p) n -> k p n", p=P)
        passed = sem("waits_passed")
        block = ctx.enter_context(nc.Block())

        @block.sync
        def _(eng):
            eng.dma_start(c_sb[:], c).then_inc(s_c, 16)
            for k in range(KT):
                if k >= 2:
                    hold(eng, passed, s_modk, k - 1)
                eng.dma_start(wm[:, k % 2], wm_t[k]).then_inc(s_wm[k % 2], 16)
                if k < 2:
                    for n in range(2 * k, 2 * k + 2):
                        eng.dma_start(x_sb[:, n], x_t[n]).then_inc(s_x[n], 16)
            eng.dma_start(wv_raw[:], wv).then_inc(s_wv, 16)
            for t in range(4, TT):
                hold(eng, passed, s_xh, t - 3)
                eng.dma_start(x_sb[:, t % 4], x_t[t]).then_inc(s_x[t % 4], 16)
            eng.wait_ge(s_rows, 7)
            for n, s in enumerate((2, 3, 4, 5)):
                src = rows[32 * (s % 4):32 * (s % 4) + B, s // 4, :]
                eng.dma_start(mod_rows[n], src).then_inc(s_rowst, 16)
            gb_v = gb_rows.rearrange("(b r) d -> r b d", b=B)
            for n in range(CH // B):
                eng.dma_start(gb_v[n], rows[32:32 + B, 1, :]).then_inc(s_rowst, 16)
            eng.wait_ge(s_zero, 1)
            for n in range(SLOTS // P):
                eng.dma_start(xe_d[n * P:(n + 1) * P, :], zero[:]).then_inc(s_xe, 16)
            hold(eng, passed, s_rowst, 16 * (4 + CH // B))
            hold(eng, passed, s_xe, 16 * (SLOTS // P))

        @block.gpsimd
        def _(eng):
            eng.memset(ident[:], 0.0).then_inc(s_id, 1)
            eng.memset(zero[:], 0.0).then_inc(s_zero, 1)
            eng.wait_ge(s_id, 1)
            eng.affine_select(out=ident[:], in_=ident[:], compare_op=ALU.not_equal, fill=1.0, base=0,
                              pattern=[[-1, P]], channel_multiplier=1).then_inc(s_id, 1)
            eng.memset(mhalf[:], -0.5).then_inc(s_id, 1)
            eng.wait_ge(s_id, 3)

            def rsqrt(g):
                hold(eng, passed, s_stat, 9 * (g + 1))
                eng.tensor_tensor(rstd[:], veps[:], mhalf[:], ALU.pow).then_inc(s_rstd, 1)

            rsqrt(0)
            rsqrt(1)
            eng.wait_ge(s_wv, 16)
            eng.tensor_copy(wv_h[:], wv_raw[:]).then_inc(s_wvs, 1)
            eng.wait_ge(s_wvs, 1)
            eng.tensor_tensor(wv_l[:], wv_raw[:], wv_h[:].bitcast(F32), ALU.subtract).then_inc(s_wvs, 1)
            rsqrt(2)
            rsqrt(3)

        @block.tensor
        def _(eng):
            eng.wait_ge(s_silu, 3)
            for k in range(KT):
                eng.wait_ge(s_wm[k % 2], 16 * (k // 2 + 1))
                for s in range(6):
                    mm = eng.matmul(ps_mod[s // 4][32 * (s % 4):32 * (s % 4) + B, :], c_silu[:, k, :],
                                    wm[:, k % 2, s * D:(s + 1) * D], start=(k == 0), stop=(k == KT - 1))
                mm.then_inc(s_modk, 1)
            eng.wait_ge(s_rows, 1)
            eng.wait_ge(s_id, 2)
            for s in range(2):
                for k in range(KT):
                    mm = eng.transpose(ps_modt[s][:, k * B:(k + 1) * B],
                                       rows[32 * s:32 * s + B, 0, k * P:(k + 1) * P],
                                       ident[32 * s:32 * s + B, 32 * s:32 * s + B])
            mm.then_inc(s_modt, 1)

            def transposes(g):
                for n in range(4):
                    eng.wait_ge(s_xh, 4 * g + n + 1)
                    for k in range(KT):
                        if n == 0 and g >= 1:
                            eng.wait_ge(s_hm, KT * (g - 1) + k + 1)
                        mm = eng.transpose(ps_t[k][:, n * P:(n + 1) * P],
                                           xhat[:, n, k * P:(k + 1) * P], ident[:])
                    mm.then_inc(s_tr, 1)

            def values(g):
                for n in range(4):
                    t = 4 * g + n
                    if t == 0:
                        eng.wait_ge(s_wvs, 2)
                        eng.wait_ge(s_modc, 2)
                        eng.wait_ge(s_rows, 2)
                    if n == 0:
                        eng.wait_ge(s_hh, KT * (g + 1))
                        eng.wait_ge(s_hl, KT * (g + 1))
                    ge(eng, s_vev, t - 3)
                    for k in range(KT):
                        for m, (a, w) in enumerate(((hth, wv_h), (hth, wv_l), (htl, wv_h))):
                            mm = eng.matmul(ps_v[t % 4][:], a[:, k, t * P:(t + 1) * P], w[:, k, :],
                                            start=(k == 0 and m == 0), stop=(k == KT - 1 and m == 2))
                    mm.then_inc(s_vps, 1)

            transposes(0)
            for g in range(GROUPS):
                if g + 1 < GROUPS:
                    transposes(g + 1)
                values(g)

        @block.scalar
        def _(eng):
            eng.wait_ge(s_c, 16)
            eng.activation(c_e[:], c_sb[:], ACT.Exp, scale=-1.0).then_inc(s_e, 1)
            for g in range(GROUPS):
                for k in range(KT):
                    eng.wait_ge(s_hm, KT * g + k + 1)
                    eng.activation(hth[:, k, g * HALF:(g + 1) * HALF], hmod[:, k % 2], ACT.Copy)\
                        .then_inc(s_hh, 1)
                if g >= 1:
                    for n in range(4):
                        t = 4 * (g - 1) + n
                        eng.wait_ge(s_vps, t + 1)
                        eng.activation(v_all[:, t], ps_v[t % 4][:], ACT.Copy).then_inc(s_vev, 1)
            for t in range(TT - 4, TT):
                eng.wait_ge(s_vps, t + 1)
                eng.activation(v_all[:, t], ps_v[t % 4][:], ACT.Copy).then_inc(s_vev, 1)

        @block.vector
        def _(eng):
            eng.wait_ge(s_e, 1)
            eng.tensor_scalar(c_e[:], c_e[:], 1.0, None, ALU.add).then_inc(s_silu, 1)
            eng.wait_ge(s_silu, 1)
            eng.reciprocal(c_e[:], c_e[:]).then_inc(s_silu, 1)
            eng.wait_ge(s_silu, 2)
            eng.tensor_tensor(c_silu[:], c_sb[:], c_e[:], ALU.mult).then_inc(s_silu, 1)

            def layer_norm(g):
                ge(eng, s_xh, 4 * g)
                for n in range(4):
                    eng.wait_ge(s_x[n], 16 * (g + 1))
                    eng.bn_stats(stats[:, n], x_sb[:, n]).then_inc(s_stat, 1)
                    eng.wait_ge(s_stat, 9 * g + 2 * n + 1)
                    eng.bn_aggr(mv[:, n], stats[:, n]).then_inc(s_stat, 1)
                    eng.wait_ge(s_stat, 9 * g + 2 * n + 2)
                eng.tensor_scalar(veps[:], mv[:, :, 1], EPS, None, ALU.add).then_inc(s_stat, 1)
                eng.wait_ge(s_rstd, g + 1)
                for n in range(4):
                    if g >= 1:
                        eng.wait_ge(s_tr, 4 * (g - 1) + n + 1)
                    eng.tensor_scalar(xhat[:, n], x_sb[:, n], mv[:, n, 0:1], rstd[:, n:n + 1],
                                      ALU.subtract, ALU.mult).then_inc(s_xh, 1)

            layer_norm(0)
            eng.wait_ge(s_modk, KT)
            for s in range(6):
                q = 32 * (s % 4)
                cp = eng.tensor_copy(rows[q:q + B, s // 4, :], ps_mod[s // 4][q:q + B, :])
                if s in (1, 5):
                    cp.then_inc(s_rows, 1)
            eng.wait_ge(s_rows, 2)
            for n, s in enumerate((2, 5)):
                q, m = 32 * (s % 4), s // 4
                eng.tensor_scalar(gate_s[q:q + B, m], rows[q:q + B, m], 0.0, 2.0, ALU.is_ge, ALU.mult)
                eng.scalar_tensor_tensor(out=gate_a[q:q + B, m], in0=rows[q:q + B, m], scalar=-1.0,
                                         in1=rows[q:q + B, m], op0=ALU.mult, op1=ALU.max)\
                    .then_inc(s_rows, 1)
            eng.wait_ge(s_rows, 4)
            for n, s in enumerate((2, 5)):
                q, m = 32 * (s % 4), s // 4
                eng.tensor_scalar(gate_a[q:q + B, m], gate_a[q:q + B, m], 0.25, None, ALU.max)\
                    .then_inc(s_rows, 1)
            eng.wait_ge(s_rows, 6)
            for n, s in enumerate((2, 5)):
                q, m = 32 * (s % 4), s // 4
                st = eng.scalar_tensor_tensor(out=rows[q:q + B, m], in0=gate_s[q:q + B, m], scalar=-1.0,
                                              in1=gate_a[q:q + B, m], op0=ALU.add, op1=ALU.mult)
            st.then_inc(s_rows, 1)
            eng.wait_ge(s_modt, 1)
            eng.tensor_copy(mod_t[:, 0].rearrange("p k b -> p (k b)"), ps_modt[0][:, 0:KT * B])\
                .then_inc(s_modc, 1)
            eng.tensor_scalar(mod_t[:, 1].rearrange("p k b -> p (k b)"), ps_modt[1][:, 0:KT * B],
                              1.0, None, ALU.add).then_inc(s_modc, 1)
            eng.wait_ge(s_modc, 2)

            for g in range(GROUPS):
                if g + 1 < GROUPS:
                    layer_norm(g + 1)
                b = g // (GROUPS // B)
                for k in range(KT):
                    n = KT * g + k
                    if n % KT == 0:
                        eng.wait_ge(s_tr, 4 * (g + 1))
                    ge(eng, s_hh, n - 1)
                    ge(eng, s_hl, n - 1)
                    eng.tensor_scalar(hmod[:, k % 2], ps_t[k][:], mod_t[:, 1, k, b:b + 1],
                                      mod_t[:, 0, k, b:b + 1], ALU.mult, ALU.add).then_inc(s_hm, 1)
                    eng.wait_ge(s_hh, n + 1)
                    eng.tensor_tensor(htl[:, k, g * HALF:(g + 1) * HALF], hmod[:, k % 2],
                                      hth[:, k, g * HALF:(g + 1) * HALF].bitcast(F32), ALU.subtract)\
                        .then_inc(s_hl, 1)


def attention(nc, wqk, ctx_t, ident, hth, htl, v_all, wqk_h, wqk_l):
    SCALE = float(HN) ** -0.5
    QT = S // P
    CC = S // HALF
    STACK = 3 * HN
    UNITS = [(hd, qt) for qt in range(QT) for hd in range(2)]
    PER_STEP = [0, 0, 3, 3, 3, 3, 2, 2]
    with ExitStack() as ctx:
        def sb(name, shape, dt=F32):
            return ctx.enter_context(nc.sbuf_tensor(name, shape, dt))

        def sem(name):
            return ctx.enter_context(nc.semaphore(name))

        stack = sb("stack", [STACK + 2, 2, 4, S], F32R)
        part_h = sb("part_h", [P, S], F32R)
        part_l = sb("part_l", [P, S], F32R)
        w_raw = sb("w_raw", [P, 2, KT, P])
        probs = sb("probs", [P, 2, 2, S])
        v_one = sb("v_one", [P, 2, QT, 2, 2, HN])
        mx = sb("mx", [P, 2 * QT, CC])
        nmax = sb("nmax", [P, 2 * QT])
        mcat = sb("mcat", [P, 2, 2 * QT])
        mrow = sb("mrow", [4 * QT, P])
        rsum = sb("rsum", [P, S])
        cnorm = sb("cnorm", [P, S])
        ps_s = [ctx.enter_context(nc.psum_tensor(f"ps_s{n}", [P, HALF], F32)) for n in range(2)]
        ps_t = [ctx.enter_context(nc.psum_tensor(f"ps_t{n}", [P, S], F32)) for n in range(2)]
        ps_o = ctx.enter_context(nc.psum_tensor("ps_o", [P, S], F32))

        s_init = sem("constants_ready")
        s_wl = [sem("w_loaded0"), sem("w_loaded1")]
        s_ws = sem("w_split")
        s_wh = sem("w_high_part")
        s_proj = sem("proj_done")
        s_ph = sem("part_h_ready")
        s_pl = sem("part_l_ready")
        s_stk = sem("stack_loaded")
        s_sc = sem("scores_ready")
        s_mxd = sem("max_done")
        s_mch = sem("mcat_step")
        s_mt = sem("mrow_transposed")
        s_mc = sem("mrow_copied")
        s_mr = sem("mrow_loaded")
        s_st = sem("scores_t_ready")
        s_ex = sem("exp_done")
        s_pv = sem("pv_done")
        s_vo = sem("v_copied_pair")
        s_rs = sem("rsum_ready")
        s_cn = sem("ctx_normed")
        s_cst = sem("ctx_stored")

        passed = sem("waits_passed")
        block = ctx.enter_context(nc.Block())

        @block.sync
        def _(eng):
            def load_w(u, r):
                hold(eng, passed, s_ws, u - 1)
                eng.dma_start(w_raw[:, r], wqk[u]).then_inc(s_wl[r], 16)

            def move_stack(u, r):
                hold(eng, passed, s_ph, CC * (u + 1))
                hold(eng, passed, s_pl, CC * (u + 1))
                hold(eng, passed, s_st, 2 * QT * (u - 1))
                for j in range(4):
                    src_h, src_l = (a[HN * j:HN * (j + 1), :].bitcast(F32) for a in (part_h, part_l))
                    order = (src_h, src_l, src_h) if j < 2 else (src_h, src_h, src_l)
                    for n, src in enumerate(order):
                        eng.dma_start(stack[HN * n:HN * (n + 1), r, j, :].bitcast(F32), src).then_inc(s_stk, 16)

            def move_mrow(u, r):
                hold(eng, passed, s_mc, u + 1)
                for n in range(2):
                    eng.dma_start(stack[STACK + n:STACK + n + 1, r, 0:2, :]
                                  .rearrange("o j s -> o (j s)").bitcast(F32),
                                  mrow[2 * QT * n:2 * QT * (n + 1), :]).then_inc(s_mr, 16)

            def store_ctx(u):
                hold(eng, passed, s_cn, 2 * (u + 1))
                for b in range(2):
                    eng.dma_start(ctx_t[bass.ds(HN * u, HN), b, :] if not isinstance(u, int)
                                  else ctx_t[HN * u:HN * (u + 1), b, :],
                                  cnorm[64 * b:64 * b + HN, :]).then_inc(s_cst, 16)

            load_w(0, 0)
            load_w(1, 1)
            load_w(2, 0)
            move_stack(0, 0)
            load_w(3, 1)
            move_stack(1, 1)
            move_mrow(0, 0)

            def body(u, r, row, last=False):
                if row is not None:
                    hold(eng, passed, s_ws, u + 3)
                    src = wqk[row] if isinstance(row, int) else wqk[bass.ds(row, 1)]\
                        .rearrange("o p k n -> (o p) k n")
                    eng.dma_start(w_raw[:, r], src).then_inc(s_wl[r], 16)
                if not (last and r == 1):
                    move_mrow(u + 1, 1 - r)
                if not last:
                    move_stack(u + 2, r)
                store_ctx(u)

            for u in range(4):
                body(u, u % 2, (u + 4) % (NH // 2))
            with eng.Fori(2, 6) as i:
                for r in range(2):
                    body(2 * i + r, r, 2 * i + (r + 4 - NH // 2))
            for u in range(PAIRS - 4, PAIRS):
                body(u, u % 2, None, last=u >= PAIRS - 2)
            hold(eng, passed, s_cst, 32 * PAIRS)

        @block.gpsimd
        def _(eng):
            eng.memset(stack[STACK:STACK + 2].bitcast(F32), 1.0).then_inc(s_init, 1)
            eng.wait_ge(s_init, 1)
            eng.memset(v_one[:], 1.0).then_inc(s_init, 1)
            eng.wait_ge(s_init, 2)

            def split_w(u, r, waited):
                hold(eng, passed, s_wl[r], waited)
                hold(eng, passed, s_proj, CC * (u - 1))
                eng.tensor_copy(wqk_h[:, r], w_raw[:, r]).then_inc(s_wh, 1)
                hold(eng, passed, s_wh, u + 1)
                eng.tensor_tensor(wqk_l[:, r], w_raw[:, r], wqk_h[:, r].bitcast(F32), ALU.subtract)\
                    .then_inc(s_ws, 1)

            def copy_v(u, r, row, head):
                hold(eng, passed, s_pv, QT * (u - 1))
                cols = slice(head, head + 2 * HN) if isinstance(head, int) else bass.ds(head, 2 * HN)
                src = v_all[:, row:row + QT, cols]
                eng.tensor_copy(v_one[:, r, :, :, 0, :], src.rearrange("p t (a d) -> p t a d", a=2))\
                    .then_inc(s_vo, 1)

            for u in range(2):
                split_w(u, u, 16)
                copy_v(u, u, 0, u * 2 * HN)
            for u in range(2, 4):
                split_w(u, u - 2, 32)
            def body(u, r, row, head, w):
                copy_v(u + 2, r, row, head)
                if w is not None:
                    split_w(u + 4, r, w)

            for r in range(2):
                body(r, r, 0, (2 + r) * 2 * HN, 16 * 3)
            for lo, hi, batch in ((1, 3, 0), (3, 6, 1)):
                with eng.Fori(lo, hi) as i:
                    for r in range(2):
                        body(2 * i + r, r, QT * batch,
                             (2 * i + (r + 2 - 8 * batch)) * (2 * HN), i * 16 + 48)
            for u in (PAIRS - 4, PAIRS - 3):
                body(u, u % 2, QT, (u + 2 - 8) * 2 * HN, None)

        @block.tensor
        def _(eng):
            def proj(u, r, batch):
                ge(eng, s_ws, u + 1)
                for cc in range(CC):
                    if isinstance(u, int) and u < 2:
                        ge(eng, s_ph, CC * u)
                        ge(eng, s_pl, CC * u)
                    else:
                        eng.wait_ge(s_mxd, 4 * QT * u)
                        eng.wait_ge(s_mc, u)
                    at = batch * S + cc * HALF
                    for k in range(KT):
                        for m, (w, a) in enumerate(((wqk_h, hth), (wqk_l, hth), (wqk_h, htl))):
                            mm = eng.matmul(ps_s[cc][:], w[:, r, k, :], a[:, k, at:at + HALF],
                                            start=(k == 0 and m == 0), stop=(k == KT - 1 and m == 2))
                    mm.then_inc(s_proj, 1)

            def scores(u, r, n0, n1):
                for n in range(n0, n1):
                    hd, qt = UNITS[n]
                    for cc in range(CC):
                        if n == 0 and cc == 0:
                            ge(eng, s_stk, 16 * 12 * (u + 1))
                        if n == 0:
                            ge(eng, s_ph, CC * (u + 1))
                            ge(eng, s_pl, CC * (u + 1))
                            if isinstance(u, int) and u < 2:
                                eng.wait_ge(s_ph, 2 * CC)
                                eng.wait_ge(s_pl, 2 * CC)
                            ge(eng, s_mc, u)
                        else:
                            ge(eng, s_mxd, 4 * QT * u + 2 * n + cc - 1)
                        eng.matmul(ps_s[cc][:], stack[0:STACK, r, hd, qt * P:(qt + 1) * P],
                                   stack[0:STACK, r, 2 + hd, cc * HALF:(cc + 1) * HALF],
                                   start=True, stop=True).then_inc(s_sc, 1)

            def max_rows(u):
                ge(eng, s_mch, 3 * (u + 1))
                eng.transpose(ps_s[0][0:4 * QT, 0:P], mcat[:].rearrange("p a n -> p (a n)"), ident[:])\
                    .then_inc(s_mt, 1)

            def scores_t(u, r, kt, hd):
                if kt == 0 and hd == 0:
                    ge(eng, s_mr, 32 * (u + 1))
                ge(eng, s_ex, 2 * QT * u + 2 * kt + hd - 1)
                for cc in range(CC):
                    mm = eng.matmul(ps_t[hd][:, cc * HALF:(cc + 1) * HALF],
                                    stack[:, r, 2 + hd, kt * P:(kt + 1) * P],
                                    stack[:, r, hd, cc * HALF:(cc + 1) * HALF], start=True, stop=True)
                mm.then_inc(s_st, 1)

            def weighted(u, r, kt):
                ge(eng, s_ex, 2 * QT * u + 2 * kt + 2)
                if kt == 0:
                    ge(eng, s_vo, u + 1)
                    ge(eng, s_cn, 2 * u)
                for cc in range(CC):
                    for hd in range(2):
                        mm = eng.matmul(ps_o[64 * hd:64 * hd + 64, cc * HALF:(cc + 1) * HALF],
                                        v_one[:, r, kt, hd].rearrange("p a d -> p (a d)"),
                                        probs[:, kt % 2, hd, cc * HALF:(cc + 1) * HALF],
                                        start=(kt == 0), stop=(kt == QT - 1))
                mm.then_inc(s_pv, 1)

            eng.wait_ge(s_init, 2)
            proj(0, 0, 0)
            proj(1, 1, 0)
            scores(0, 0, 0, 2 * QT)
            max_rows(0)

            def body(u, r, batch, last=False):
                n = 0
                more = not (last and r == 1)
                for kt in range(QT):
                    for hd in range(2):
                        scores_t(u, r, kt, hd)
                    if more:
                        scores(u + 1, 1 - r, n, n + PER_STEP[kt])
                        n += PER_STEP[kt]
                    if kt >= 1:
                        weighted(u, r, kt - 1)
                if more:
                    max_rows(u + 1)
                weighted(u, r, QT - 1)
                if not last:
                    proj(u + 2, r, batch)

            for r in range(2):
                body(r, r, 0)
            for lo, hi, batch in ((1, 3, 0), (3, 7, 1)):
                with eng.Fori(lo, hi) as i:
                    for r in range(2):
                        body(2 * i + r, r, batch)
            for r in range(2):
                body(PAIRS - 2 + r, r, 0, last=True)

        @block.scalar
        def _(eng):
            def high_part(u):
                for cc in range(CC):
                    ge(eng, s_proj, CC * u + cc + 1)
                    if cc == 0:
                        ge(eng, s_stk, 16 * 12 * u)
                    eng.activation(part_h[:, cc * HALF:(cc + 1) * HALF], ps_s[cc][:], ACT.Copy)\
                        .then_inc(s_ph, 1)

            def body(u, last=False):
                for kt in range(QT):
                    for hd in range(2):
                        ge(eng, s_st, 2 * QT * u + 2 * kt + hd + 1)
                        ge(eng, s_pv, QT * u + kt - 1)
                        eng.activation(probs[:, kt % 2, hd, :], ps_t[hd][:], ACT.Exp, scale=SCALE)\
                            .then_inc(s_ex, 1)
                if not last:
                    high_part(u + 2)

            high_part(0)
            high_part(1)
            for u in range(2):
                body(u)
            with eng.Fori(1, PAIRS // 2 - 1) as i:
                for r in range(2):
                    body(2 * i + r)
            for r in range(2):
                body(PAIRS - 2 + r, last=True)

        @block.vector
        def _(eng):
            def low_part(u):
                for cc in range(CC):
                    ge(eng, s_ph, CC * u + cc + 1)
                    eng.tensor_tensor(part_l[:, cc * HALF:(cc + 1) * HALF], ps_s[cc][:],
                                      part_h[:, cc * HALF:(cc + 1) * HALF].bitcast(F32), ALU.subtract)\
                        .then_inc(s_pl, 1)

            def maxima(u):
                for n, (hd, qt) in enumerate(UNITS):
                    for cc in range(CC):
                        ge(eng, s_sc, 4 * QT * u + 2 * n + cc + 1)
                        if n == 0 and cc == 0:
                            ge(eng, s_mch, 3 * u)
                        at = hd * QT + qt
                        eng.tensor_reduce(mx[:, at, cc:cc + 1], ps_s[cc][:], AX.X, ALU.max)\
                            .then_inc(s_mxd, 1)
                ge(eng, s_mxd, 4 * QT * (u + 1))
                eng.tensor_reduce(nmax[:], mx[:], AX.X, ALU.max, negate=True).then_inc(s_mch, 1)
                ge(eng, s_mch, 3 * u + 1)
                ge(eng, s_mt, u)
                eng.tensor_copy(mcat[:, 0].bitcast(F32R), nmax[:]).then_inc(s_mch, 1)
                ge(eng, s_mch, 3 * u + 2)
                eng.tensor_tensor(mcat[:, 1].bitcast(F32R), nmax[:], mcat[:, 0], ALU.subtract)\
                    .then_inc(s_mch, 1)
                ge(eng, s_mt, u + 1)
                ge(eng, s_mr, 32 * u)
                eng.tensor_copy(mrow[:], ps_s[0][0:4 * QT, 0:P]).then_inc(s_mc, 1)

            def norm(u):
                ge(eng, s_pv, QT * (u + 1))
                ge(eng, s_cn, 2 * u)
                eng.reciprocal(rsum[:], ps_o[:]).then_inc(s_rs, 1)
                ge(eng, s_rs, u + 1)
                ge(eng, s_cst, 32 * u)
                for hd in range(2):
                    q = 64 * hd
                    eng.tensor_tensor(cnorm[q:q + HN], ps_o[q:q + HN], rsum[q + HN:q + 2 * HN], ALU.mult)\
                        .then_inc(s_cn, 1)

            low_part(0)
            low_part(1)
            maxima(0)

            def body(u, more=True, last=False):
                if more:
                    maxima(u + 1)
                norm(u)
                if not last:
                    low_part(u + 2)

            for u in range(2):
                body(u)
            with eng.Fori(1, PAIRS // 2 - 1) as i:
                for r in range(2):
                    body(2 * i + r)
            body(PAIRS - 2, last=True)
            body(PAIRS - 1, more=False, last=True)


def middle(nc, x, wproj, bproj, wr_se, mod_rows, ctx_t, x1_d, xe_d,
           ident, slots, wtop, gbt, sgate, h2h, h2l):
    PER_B = S // P
    with ExitStack() as ctx:
        def sb(name, shape, dt=F32):
            return ctx.enter_context(nc.sbuf_tensor(name, shape, dt))

        def sem(name):
            return ctx.enter_context(nc.semaphore(name))

        wp_raw = sb("wp_raw", [P, KT, D])
        wp_h = sb("wp_h", [P, KT, D], F32R)
        wp_l = sb("wp_l", [P, KT, D], F32R)
        wrse = sb("wrse", [P, KT, E + 1])
        ga_t = sb("ga_t", [P, B, D])
        cb_t = sb("cb_t", [P, B, D])
        sb_t = sb("sb_t", [P, B, D])
        gabp = sb("gabp", [P, B, D])
        bp_t = sb("bp_t", [P, D])
        iota_e = sb("iota_e", [P, TOPK, E])
        slot_a = sb("slot_a", [P, E])
        slot_b = sb("slot_b", [P, E])
        lower = sb("lower", [P, P], BF16)
        ones = sb("ones", [P, P], BF16)
        seen = sb("seen", [P, E], BF16)
        ct = sb("ct", [P, 2, KT, P])
        ct_h = sb("ct_h", [P, 2, KT, P], F32R)
        ct_l = sb("ct_l", [P, 2, KT, P], F32R)
        xt = sb("xt", [P, 2, D])
        x1 = sb("x1", [P, 2, D])
        xhat = sb("xhat2", [P, 2, D])
        h2 = sb("h2", [P, 2, D])
        h2t = sb("h2t", [P, 2, KT, P])
        stats = sb("stats2", [P, 2, 6])
        mv = sb("mv2", [P, 2, 2])
        veps = sb("veps2", [P, 2])
        rstd = sb("rstd2", [P, 2])
        mhalf = sb("mhalf2", [P, 1])
        nmax = sb("nmax2", [P, 2])
        esum = sb("esum", [P, 2])
        ex = sb("ex", [P, 2, E])
        ese = sb("ese", [P, 2])
        prb = sb("prb", [P, 2, E])
        top8 = sb("top8", [P, 2, 8])
        idx8 = sb("idx8", [P, 2, 8], U32)
        idxf = sb("idxf", [P, 2, TOPK])
        onehot = sb("onehot", [P, 2, TOPK, E])
        mask = sb("mask", [P, 2, E], BF16)
        wsum = sb("wsum", [P, 2])
        over = sb("over", [P, 2, E])
        slotv = sb("slotv", [P, 2, E])
        pick = sb("pick", [P, 2, TOPK, E])
        slotf = sb("slotf", [P, 2, TOPK])
        slot_i = sb("slot_i", [P, 2, TOPK], U32)
        ps_y = [ctx.enter_context(nc.psum_tensor(f"ps_y{n}", [P, D], F32)) for n in range(2)]
        ps_h = [ctx.enter_context(nc.psum_tensor(f"ps_h{n}", [P, D], F32)) for n in range(2)]
        ps_r = [ctx.enter_context(nc.psum_tensor(f"ps_r{n}", [P, D], F32)) for n in range(2)]
        ps_p = [ctx.enter_context(nc.psum_tensor(f"ps_p{n}", [P, D], F32)) for n in range(2)]

        s_wp = sem("wproj_loaded")
        s_tb = sem("tables_loaded")
        s_wps = sem("wproj_split")
        s_tab = sem("tables_ready")
        s_cst = sem("mid_constants")
        s_ct = [sem("ctx_loaded0"), sem("ctx_loaded1")]
        s_xt = [sem("x_in0"), sem("x_in1")]
        s_cth = sem("ctx_high")
        s_ctl = sem("ctx_low")
        s_xg = sem("x_bias_added")
        s_py = sem("projected")
        s_x1a = sem("gated")
        s_x1 = sem("x1_ready")
        s_x1s = [sem("x1_stored0"), sem("x1_stored1")]
        s_st = sem("stats2_step")
        s_rstd = sem("rstd2_ready")
        s_xh = sem("xhat2_ready")
        s_h2a = sem("h2_scaled")
        s_h2 = sem("h2_ready")
        s_tr = sem("h2_transposed")
        s_h2t = sem("h2t_ready")
        s_h2h = sem("h2h_ready")
        s_h2l = sem("h2l_ready")
        s_lg = sem("logits_ready")
        s_nm = sem("nmax_ready")
        s_ex = sem("router_exp")
        s_rt = sem("routing_step")
        s_mk = sem("mask_ready")
        s_pos = sem("positions_ready")
        s_sl = sem("slots_ready")
        s_kept = sem("seen_updated")
        s_sc = [sem("scattered0"), sem("scattered1")]

        x_t = x.rearrange("b s d -> (b s) d")
        ctx_v = ctx_t.rearrange("(k p) b s -> p k b s", p=P)

        def rows(t, r):
            return slice(t * P, (t + 1) * P) if isinstance(t, int) else bass.ds(t * P, P)

        def each_tile(eng, body, last_differs=False):
            half = PER_B // 2
            for b in range(B):
                lo, hi = (1 if b == 0 else 0), half - (1 if b == B - 1 else 0)
                if b == 0:
                    body(0, b)
                with eng.Fori(lo, hi) as i:
                    body(2 * i + PER_B * b, b)
                if b == B - 1:
                    body(TT - 2, b)

        passed = sem("waits_passed")
        block = ctx.enter_context(nc.Block())

        @block.sync
        def _(eng):
            eng.dma_start(wp_raw[:], wproj).then_inc(s_wp, 16)

            def load(t, b, r):
                hold(eng, passed, s_ctl, t - 1)
                hold(eng, passed, s_x1, t - 1)
                s0 = (t - PER_B * b) * P
                cols = slice(s0, s0 + P) if isinstance(t, int) else bass.ds(s0, P)
                eng.dma_start(ct[:, r], ctx_v[:, :, b, cols]).then_inc(s_ct[r], 16)
                eng.dma_start(xt[:, r], x_t[rows(t, r), :]).then_inc(s_xt[r], 16)

            for b in range(B):
                for src, dst in ((mod_rows[0], ga_t), (mod_rows[1], sb_t), (mod_rows[2], cb_t),
                                 (mod_rows[3], gbt)):
                    eng.dma_start(dst[:, b], src[b:b + 1, :].to_broadcast([P, D])).then_inc(s_tb, 16)
            eng.dma_start(bp_t[:], bproj.to_broadcast([P, D])).then_inc(s_tb, 16)
            eng.dma_start(wrse[:], wr_se).then_inc(s_tb, 16)
            load(0, 0, 0)
            load(1, 0, 1)

            def body(t, b):
                for r in range(2):
                    hold(eng, passed, s_x1, t + r + 1)
                    eng.dma_start(x1_d[rows(t + r, r), :], x1[:, r]).then_inc(s_x1s[r], 16)
                    nb = b
                    if isinstance(t, int) and t == TT - 2:
                        continue
                    load(t + r + 2, nb, r)

            half = PER_B // 2
            body(0, 0)
            with eng.Fori(1, half - 1) as i:
                body(2 * i, 0)
            body(PER_B - 2, 1)
            with eng.Fori(0, half - 1) as i:
                body(2 * i + PER_B, 1)
            body(TT - 2, 1)
            for r in range(2):
                eng.wait_ge(s_x1s[r], 16 * TT // 2)

        @block.gpsimd
        def _(eng):
            eng.memset(lower[:], 1.0).then_inc(s_cst, 1)
            eng.memset(ones[:], 1.0).then_inc(s_cst, 1)
            eng.memset(seen[:], 0.0).then_inc(s_cst, 1)
            eng.memset(mhalf[:], -0.5).then_inc(s_cst, 1)
            eng.wait_ge(s_cst, 4)
            eng.affine_select(out=lower[:], in_=lower[:], compare_op=ALU.is_gt, fill=0.0, base=0,
                              pattern=[[1, P]], channel_multiplier=-1).then_inc(s_cst, 1)
            eng.iota(iota_e[:], pattern=[[0, TOPK], [1, E]], base=0, channel_multiplier=0,
                     allow_small_or_imprecise_dtypes=True).then_inc(s_cst, 1)
            eng.iota(slot_a[:], pattern=[[CAP, E]], base=0, channel_multiplier=0,
                     allow_small_or_imprecise_dtypes=True).then_inc(s_cst, 1)
            eng.iota(slot_b[:], pattern=[[T - CAP, E]], base=2 * SLOTS, channel_multiplier=0,
                     allow_small_or_imprecise_dtypes=True).then_inc(s_cst, 1)
            eng.wait_ge(s_wp, 16)
            eng.tensor_copy(wp_h[:], wp_raw[:]).then_inc(s_wps, 1)
            eng.wait_ge(s_wps, 1)
            eng.tensor_tensor(wp_l[:], wp_raw[:], wp_h[:].bitcast(F32), ALU.subtract).then_inc(s_wps, 1)
            eng.wait_ge(s_tb, 16 * (4 * B + 2))
            for b in range(B):
                eng.tensor_tensor(gabp[:, b], ga_t[:, b], bp_t[:], ALU.mult).then_inc(s_tab, 1)
                eng.tensor_scalar(cb_t[:, b], cb_t[:, b], 1.0, None, ALU.add).then_inc(s_tab, 1)
            eng.wait_ge(s_tab, 2 * B)

            def low(t, r):
                hold(eng, passed, s_cth, t + 1)
                hold(eng, passed, s_py, t - 1)
                eng.tensor_tensor(ct_l[:, r], ct[:, r], ct_h[:, r].bitcast(F32), ALU.subtract)\
                    .then_inc(s_ctl, 1)

            def bias(t, b, r, landed):
                hold(eng, passed, s_xt[r], landed)
                eng.tensor_tensor(xt[:, r], xt[:, r], gabp[:, b], ALU.add).then_inc(s_xg, 1)

            def rsqrt(t, r):
                hold(eng, passed, s_st, 3 * (t + 1))
                eng.tensor_tensor(rstd[:, r:r + 1], veps[:, r:r + 1], mhalf[:], ALU.pow).then_inc(s_rstd, 1)

            def modulate(t, b, r):
                hold(eng, passed, s_xh, t + 1)
                if not (isinstance(t, int) and t < 2):
                    hold(eng, passed, s_tr, t - 1)
                eng.tensor_tensor(xhat[:, r], xhat[:, r], cb_t[:, b], ALU.mult).then_inc(s_h2a, 1)
                hold(eng, passed, s_h2a, t + 1)
                eng.tensor_tensor(h2[:, r], xhat[:, r], sb_t[:, b], ALU.add).then_inc(s_h2, 1)

            def send(t, r):
                hold(eng, passed, s_sl, t + 1)
                eng.tensor_copy(slots[:, bass.ds(t, 1), :] if not isinstance(t, int)
                                else slots[:, t:t + 1, :], slot_i[:, r:r + 1, :]).then_inc(s_kept, 1)
                for k in range(TOPK):
                    eng.indirect_dma_start(
                        out=xe_d, out_offset=bass.IndirectOffsetOnAxis(ap=slot_i[:, r, k:k + 1], axis=0),
                        in_=h2[:, r], in_offset=None, bounds_check=SLOTS - 1, oob_is_err=False)\
                        .then_inc(s_sc[r], 16)

            def body(t, b):
                half_t = t // 2 if isinstance(t, int) else None
                for r in range(2):
                    bias(t + r, b, r, 16 * (half_t + 1) if half_t is not None else t * 8 + 16)
                for r in range(2):
                    rsqrt(t + r, r)
                for r in range(2):
                    if not (isinstance(t, int) and t == 0):
                        hold(eng, passed, s_sc[r], t * (8 * TOPK))
                    modulate(t + r, b, r)
                if not (isinstance(t, int) and t == TT - 2):
                    for r in range(2):
                        low(t + r + 2, r)
                for r in range(2):
                    send(t + r, r)

            for r in range(2):
                low(r, r)

            each_tile(eng, body)
            for r in range(2):
                eng.wait_ge(s_sc[r], 16 * TOPK * TT // 2)

        @block.tensor
        def _(eng):
            def project(t, r):
                ge(eng, s_ctl, t + 1)
                ge(eng, s_x1a, t - 1)
                for k in range(KT):
                    for m, (a, w) in enumerate(((ct_h, wp_h), (ct_h, wp_l), (ct_l, wp_h))):
                        mm = eng.matmul(ps_y[r][:], a[:, r, k, :], w[:, k, :],
                                        start=(k == 0 and m == 0), stop=(k == KT - 1 and m == 2))
                mm.then_inc(s_py, 1)

            def route(t, r):
                ge(eng, s_h2, t + 1)
                ge(eng, s_h2h, t - 1)
                for k in range(KT):
                    tr = eng.transpose(ps_h[r][:, k * P:(k + 1) * P], h2[:, r, k * P:(k + 1) * P], ident[:])
                tr.then_inc(s_tr, 1)
                ge(eng, s_h2t, t + 1)
                ge(eng, s_ex, 2 * (t - 1))
                for k in range(KT):
                    mm = eng.matmul(ps_r[r][:, 0:E + 1], h2t[:, r, k, :], wrse[:, k, :],
                                    start=(k == 0), stop=(k == KT - 1))
                mm.then_inc(s_lg, 1)

            def positions(t, r):
                ge(eng, s_mk, 2 * t + 1)
                ge(eng, s_sl, t - 1)
                eng.matmul(ps_p[r][:, 0:E], lower[:], mask[:, r], start=True, stop=False)
                eng.matmul(ps_p[r][:, 0:E], ones[:], seen[:], start=False, stop=True).then_inc(s_pos, 1)

            eng.wait_ge(s_wps, 2)
            eng.wait_ge(s_cst, 8)
            project(0, 0)
            project(1, 1)

            def body(t, b):
                for r in range(2):
                    route(t + r, r)
                    if not (isinstance(t, int) and t == TT - 2):
                        project(t + r + 2, r)
                for r in range(2):
                    positions(t + r, r)

            each_tile(eng, body)

        @block.scalar
        def _(eng):
            def split(t, r, landed):
                eng.wait_ge(s_ct[r], landed)
                ge(eng, s_py, t - 1)
                eng.activation(ct_h[:, r], ct[:, r], ACT.Copy).then_inc(s_cth, 1)

            def transposed(t, r):
                ge(eng, s_tr, t + 1)
                ge(eng, s_lg, t - 1)
                ge(eng, s_h2l, t - 1)
                eng.activation(h2t[:, r].rearrange("p k n -> p (k n)"), ps_h[r][:], ACT.Copy)\
                    .then_inc(s_h2t, 1)
                dst = h2h[:, :, t * P:(t + 1) * P] if isinstance(t, int) else h2h[:, :, bass.ds(t * P, P)]
                eng.activation(dst, ps_h[r][:].rearrange("p (k n) -> p k n", k=KT), ACT.Copy)\
                    .then_inc(s_h2h, 1)

            def exps(t, r):
                ge(eng, s_nm, t + 1)
                eng.activation(ex[:, r], ps_r[r][:, 0:E], ACT.Exp, bias=nmax[:, r:r + 1],
                               accum_out=esum[:, r:r + 1]).then_inc(s_ex, 1)
                eng.activation(ese[:, r:r + 1], ps_r[r][:, E:E + 1], ACT.Exp, scale=-1.0)\
                    .then_inc(s_ex, 1)

            split(0, 0, 16)
            split(1, 1, 16)

            def body_ahead(t, b):
                transposed(t, 0)
                if not (isinstance(t, int) and t == TT - 2):
                    split(t + 2, 0, 16 * (t // 2 + 2) if isinstance(t, int) else t * 8 + 32)
                transposed(t + 1, 1)
                if not (isinstance(t, int) and t == TT - 2):
                    split(t + 3, 1, 16 * (t // 2 + 2) if isinstance(t, int) else t * 8 + 32)
                for r in range(2):
                    exps(t + r, r)

            each_tile(eng, body_ahead)

        @block.vector
        def _(eng):
            STEPS = 13

            def residual(t, b, r):
                ge(eng, s_py, t + 1)
                ge(eng, s_xg, t + 1)
                if not (isinstance(t, int) and t < 2):
                    eng.wait_ge(s_x1s[r], (t - r) * 8)
                eng.tensor_tensor(x1[:, r], ps_y[r][:], ga_t[:, b], ALU.mult).then_inc(s_x1a, 1)
                ge(eng, s_x1a, t + 1)
                eng.tensor_tensor(x1[:, r], x1[:, r], xt[:, r], ALU.add).then_inc(s_x1, 1)
                ge(eng, s_x1, t + 1)
                eng.bn_stats(stats[:, r], x1[:, r]).then_inc(s_st, 1)
                hold(eng, passed, s_st, 3 * t + 1)
                eng.bn_aggr(mv[:, r], stats[:, r]).then_inc(s_st, 1)
                ge(eng, s_st, 3 * t + 2)
                eng.tensor_scalar(veps[:, r:r + 1], mv[:, r, 1:2], EPS, None, ALU.add).then_inc(s_st, 1)

            def normalise(t, r):
                ge(eng, s_rstd, t + 1)
                ge(eng, s_h2, t - 1)
                eng.tensor_scalar(xhat[:, r], x1[:, r], mv[:, r, 0:1], rstd[:, r:r + 1],
                                  ALU.subtract, ALU.mult).then_inc(s_xh, 1)

            def low(t, r):
                ge(eng, s_h2h, t + 1)
                at = slice(t * P, (t + 1) * P) if isinstance(t, int) else bass.ds(t * P, P)
                eng.tensor_tensor(h2l[:, :, at], h2t[:, r], h2h[:, :, at].bitcast(F32), ALU.subtract)\
                    .then_inc(s_h2l, 1)

            def route(t, r):
                def step(n, ins):
                    ins.then_inc(s_rt, 1)
                    if n in (3, 4):
                        hold(eng, passed, s_rt, STEPS * t + n)
                    else:
                        ge(eng, s_rt, STEPS * t + n)

                ge(eng, s_lg, t + 1)
                ge(eng, s_ex, 2 * (t - 1))
                eng.tensor_reduce(nmax[:, r:r + 1], ps_r[r][:, 0:E], AX.X, ALU.max, negate=True)\
                    .then_inc(s_nm, 1)
                low(t, r)
                ge(eng, s_ex, 2 * (t + 1))
                at = slice(t, t + 1) if isinstance(t, int) else bass.ds(t, 1)
                step(1, eng.tensor_scalar(ese[:, r:r + 1], ese[:, r:r + 1], 1.0, None, ALU.add))
                eng.reciprocal(sgate[:, at], ese[:, r:r + 1])
                step(2, eng.reciprocal(esum[:, r:r + 1], esum[:, r:r + 1]))
                step(3, eng.tensor_scalar(prb[:, r], ex[:, r], esum[:, r:r + 1], None, ALU.mult))
                step(4, eng.max(top8[:, r], prb[:, r]))
                step(5, eng.max_index(idx8[:, r], top8[:, r], prb[:, r]))
                step(6, eng.tensor_copy(idxf[:, r], idx8[:, r, 0:TOPK]))
                step(7, eng.tensor_tensor(onehot[:, r], iota_e[:],
                                          idxf[:, r].unsqueeze(2).to_broadcast([P, TOPK, E]), ALU.is_equal))
                with nc.allow_low_precision(reason="sums of a one and three zeros are exact"):
                    eng.tensor_reduce(mask[:, r], onehot[:, r].rearrange("p k e -> p e k"), AX.X, ALU.add)\
                        .then_inc(s_mk, 1)
                step(8, eng.tensor_reduce(wsum[:, r:r + 1], top8[:, r, 0:TOPK], AX.X, ALU.add))
                eng.reciprocal(wsum[:, r:r + 1], wsum[:, r:r + 1])
                ge(eng, s_pos, t + 1)
                eng.tensor_tensor(seen[:], seen[:], mask[:, r], ALU.add).then_inc(s_mk, 1)
                step(9, eng.scalar_tensor_tensor(out=over[:, r], in0=ps_p[r][:, 0:E], scalar=float(CAP),
                                                 in1=slot_b[:], op0=ALU.is_ge, op1=ALU.mult))
                eng.tensor_tensor(slotv[:, r], ps_p[r][:, 0:E], slot_a[:], ALU.add)
                step(10, eng.tensor_scalar(top8[:, r, 0:TOPK], top8[:, r, 0:TOPK], wsum[:, r:r + 1], None,
                                           ALU.mult))
                step(11, eng.tensor_tensor(slotv[:, r], slotv[:, r], over[:, r], ALU.add))
                step(12, eng.tensor_tensor(pick[:, r], onehot[:, r],
                                           slotv[:, r].unsqueeze(1).to_broadcast([P, TOPK, E]), ALU.mult))
                step(13, eng.tensor_reduce(slotf[:, r], pick[:, r], AX.X, ALU.add))
                wt = wtop[:, at, :].rearrange("p o k -> p (o k)")
                eng.scalar_tensor_tensor(out=wt, in0=slotf[:, r], scalar=float(SLOTS),
                                         in1=top8[:, r, 0:TOPK], op0=ALU.is_lt, op1=ALU.mult)
                if not (isinstance(t, int) and t < 2):
                    eng.wait_ge(s_sc[r], (t - r) * (8 * TOPK))
                    ge(eng, s_kept, t - 1)
                eng.tensor_copy(slot_i[:, r], slotf[:, r]).then_inc(s_sl, 1)

            eng.wait_ge(s_tab, 2 * B)
            eng.wait_ge(s_cst, 8)

            def body(t, b):
                for r in range(2):
                    residual(t + r, b, r)
                for r in range(2):
                    normalise(t + r, r)
                for r in range(2):
                    route(t + r, r)

            each_tile(eng, body)


def ffn(nc, wsh, wgu, wd_a, wd_b, x1_d, res_d, xe_d, ye_d, gb_rows, ident, sgate, h2h, h2l):
    EPC = E // 2 // CH
    QC = HALF // P
    STAGES = 4 * EPC
    AT_POINT = {(s * 2 * FT) // STAGES: (s // 4, s % 4) for s in range(STAGES)}
    SLOT_USES = [len(range(s, FT, 3)) for s in range(3)]

    def before(n, j):
        return n - 3 if j >= 3 else n - (j + 1 + (FT - 1 - j) % 3)

    with ExitStack() as ctx:
        def sb(name, shape, dt=F32):
            return ctx.enter_context(nc.sbuf_tensor(name, shape, dt))

        def sem(name):
            return ctx.enter_context(nc.semaphore(name))

        def psum(name):
            return ctx.enter_context(nc.psum_tensor(name, [P, HALF], F32))

        w_raw = sb("ws_raw", [P, 3, 3 * D])
        w_h = sb("ws_h", [P, 3, 3 * D], F32R)
        w_l = sb("ws_l", [P, 3, 3 * D], F32R)
        sil = sb("sil", [P, HALF])
        gu = sb("gu", [P, HALF])
        gu_h = sb("gu_h", [P, 2, HALF], F32R)
        gu_l = sb("gu_l", [P, 2, HALF], F32R)
        res = sb("res", [P, QC, D])
        tmp = sb("tmp", [P, D])
        gbc = sb("gbc", [P, D])
        e_gu = sb("e_gu", [P, 2, 2, KT, F])
        e_da = sb("e_da", [P, 2, 2, D])
        e_db = sb("e_db", [F - 2 * P, 2, D])
        e_x = sb("e_x", [P, D])
        e_xt = sb("e_xt", [P, KT, P])
        e_sil = sb("e_sil", [P, F])
        e_h = sb("e_h", [P, F])
        e_ht = sb("e_ht", [P, 3, P])
        e_y = sb("e_y", [P, D])
        acc = [psum(f"ps_acc{n}") for n in range(QC)]
        ps_g, ps_u, ps_m0, ps_m1 = psum("ps_gate"), psum("ps_up"), psum("ps_m0"), psum("ps_m1")

        s_wl = [sem(f"ws_loaded{n}") for n in range(3)]
        s_wh = sem("ws_high")
        s_ws = sem("ws_split")
        s_g = sem("gate_done")
        s_u = sem("up_done")
        s_sil = sem("silu_done")
        s_gu = sem("gu_ready")
        s_guh = sem("gu_high")
        s_gul = sem("gu_low")
        s_dn = sem("down_done")
        s_x1 = sem("x1_chunk_loaded")
        s_gb = sem("gb_loaded")
        s_tmp = sem("shared_gated")
        s_res = sem("res_ready")
        s_rst = sem("res_stored")
        s_lgu = sem("expert_gate_up_loaded")
        s_ld = sem("expert_down_loaded")
        s_lx = sem("expert_tokens_loaded")
        s_e0 = sem("expert_tokens_transposed")
        s_ext = sem("expert_tokens_copied")
        s_e1 = sem("expert_gate_up_done")
        s_esl = sem("expert_silu_done")
        s_eh = sem("expert_hidden_ready")
        s_e2 = sem("expert_hidden_transposed")
        s_eht = sem("expert_hidden_copied")
        s_e3 = sem("expert_down_done")
        s_ey = sem("expert_rows_copied")
        s_yst = sem("expert_rows_stored")

        def each_chunk(eng, body):
            body(0, False)
            with eng.Fori(1, CH - 1) as c:
                body(c, False)
            body(CH - 1, True)

        def rows(at, n):
            return slice(at, at + n) if isinstance(at, int) else bass.ds(at, n)

        def at(a, i):
            return a[i] if isinstance(i, int) else a[bass.ds(i, 1)].rearrange("o p n -> (o p) n")

        passed = sem("waits_passed")
        block = ctx.enter_context(nc.Block())

        @block.sync
        def _(eng):
            def load_shared(n, j):
                hold(eng, passed, s_ws, before(n, j) + 1)
                eng.dma_start(w_raw[:, j % 3], wsh[j]).then_inc(s_wl[j % 3], 16)

            def load_gu(e):
                hold(eng, passed, s_e1, e)
                eng.dma_start(e_gu[:].rearrange("p a b k f -> p (a b k f)"), at(wgu, e)).then_inc(s_lgu, 16)

            def load_x(e):
                hold(eng, passed, s_e0, e)
                eng.dma_start(e_x[:], xe_d[rows(e * P, P), :]).then_inc(s_lx, 16)

            def load_down(e):
                hold(eng, passed, s_e3, e)
                eng.dma_start(e_da[:].rearrange("p a b n -> p (a b n)"), at(wd_a, e)).then_inc(s_ld, 16)
                eng.dma_start(e_db[:].rearrange("p a n -> p (a n)"), at(wd_b, e)).then_inc(s_ld, 16)

            def store_y(e):
                hold(eng, passed, s_ey, e + 1)
                eng.dma_start(ye_d[rows(e * P, P), :], e_y[:]).then_inc(s_yst, 16)

            load_shared(0, 0)
            load_shared(1, 1)
            load_x(0)
            load_gu(0)
            load_down(0)

            def body(c, last):
                hold(eng, passed, s_rst, 16 * QC * c)
                hold(eng, passed, s_tmp, QC * c)
                for q in range(QC):
                    eng.dma_start(res[:, q], x1_d[rows(c * HALF + q * P, P), :]).then_inc(s_x1, 16)
                src = gb_rows[rows(c, 1), :]
                eng.dma_start(gbc[:], src.to_broadcast([P, D])).then_inc(s_gb, 16)
                for j in range(FT):
                    n = FT * c + j
                    if not (last and j + 2 >= FT):
                        load_shared(n + 2, (j + 2) % FT)
                    for point in (2 * j, 2 * j + 1):
                        if point in AT_POINT:
                            q, stage = AT_POINT[point]
                            e = EPC * c + q
                            more = not (last and q == EPC - 1)
                            if stage == 0 and more:
                                load_x(e + 1)
                            if stage == 1 and more:
                                load_gu(e + 1)
                            if stage == 3:
                                if more:
                                    load_down(e + 1)
                                store_y(e)
                hold(eng, passed, s_res, QC * (c + 1))
                for q in range(QC):
                    eng.dma_start(res_d[rows(c * HALF + q * P, P), :], res[:, q]).then_inc(s_rst, 16)

            each_chunk(eng, body)
            hold(eng, passed, s_rst, 16 * QC * CH)
            hold(eng, passed, s_yst, 16 * E // 2)

        @block.gpsimd
        def _(eng):
            def body(c, last):
                for j in range(FT):
                    n = FT * c + j
                    use = SLOT_USES[j % 3] * c + (j // 3 + 1)
                    hold(eng, passed, s_wl[j % 3], use * 16)
                    hold(eng, passed, s_dn, before(n, j) + 1)
                    eng.tensor_copy(w_h[:, j % 3], w_raw[:, j % 3]).then_inc(s_wh, 1)
                    hold(eng, passed, s_wh, n + 1)
                    eng.tensor_tensor(w_l[:, j % 3], w_raw[:, j % 3], w_h[:, j % 3].bitcast(F32),
                                      ALU.subtract).then_inc(s_ws, 1)

            each_chunk(eng, body)

        @block.tensor
        def _(eng):
            def gate_up(c, n, j):
                ge(eng, s_ws, n + 1)
                for part, (bank, done, free) in enumerate(((ps_g, s_g, s_sil), (ps_u, s_u, s_gu))):
                    ge(eng, free, n)
                    for k in range(KT):
                        col = part * D + k * P
                        for m, (w, h) in enumerate(((w_h, h2h), (w_l, h2h), (w_h, h2l))):
                            mm = eng.matmul(bank[:], w[:, j % 3, col:col + P],
                                            h[:, k, rows(c * HALF, HALF)],
                                            start=(k == 0 and m == 0), stop=(k == KT - 1 and m == 2))
                    mm.then_inc(done, 1)

            def down(c, n, j):
                ge(eng, s_guh, n + 1)
                ge(eng, s_gul, n + 1)
                if j == 0:
                    ge(eng, s_tmp, QC * c)
                for q in range(QC):
                    for m, (g, w) in enumerate(((gu_h, w_h), (gu_h, w_l), (gu_l, w_h))):
                        mm = eng.matmul(acc[q][:], g[:, j % 2, q * P:(q + 1) * P],
                                        w[:, j % 3, 2 * D:3 * D],
                                        start=(j == 0 and m == 0), stop=(j == FT - 1 and m == 2))
                mm.then_inc(s_dn, 1)

            def stage0(e):
                ge(eng, s_lx, 16 * (e + 1))
                ge(eng, s_eht, 2 * e)
                for k in range(KT):
                    mm = eng.transpose(ps_m0[:, k * P:(k + 1) * P], e_x[:, k * P:(k + 1) * P], ident[:])
                mm.then_inc(s_e0, 1)

            def stage1(e):
                ge(eng, s_ext, e + 1)
                ge(eng, s_lgu, 16 * (e + 1))
                ge(eng, s_ey, e)
                for part, bank in enumerate((ps_m0, ps_m1)):
                    for k in range(KT):
                        for a in range(2):
                            mm = eng.matmul(bank[CAP * a:CAP * (a + 1), 0:F], e_xt[:, k, CAP * a:CAP * (a + 1)],
                                            e_gu[:, part, a, k, :], start=(k == 0), stop=(k == KT - 1))
                mm.then_inc(s_e1, 1)

            def stage2(e):
                ge(eng, s_eh, e + 1)
                for n, (f0, fs) in enumerate(F_TILES):
                    mm = eng.transpose(ps_m0[0:fs, n * P:(n + 1) * P], e_h[:, f0:f0 + fs], ident[:])
                mm.then_inc(s_e2, 1)

            def stage3(e):
                ge(eng, s_eht, 2 * (e + 1))
                ge(eng, s_ld, 32 * (e + 1))
                for n, (f0, fs) in enumerate(F_TILES):
                    for a in range(2):
                        w = e_da[:, a, n, :] if n < 2 else e_db[:, a, :]
                        mm = eng.matmul(ps_m1[CAP * a:CAP * (a + 1), :], e_ht[0:fs, n, CAP * a:CAP * (a + 1)],
                                        w, start=(n == 0), stop=(n == 2))
                mm.then_inc(s_e3, 1)

            stages = (stage0, stage1, stage2, stage3)

            def body(c, last):
                def point(p):
                    if p in AT_POINT:
                        q, stage = AT_POINT[p]
                        stages[stage](EPC * c + q)

                for j in range(FT):
                    n = FT * c + j
                    gate_up(c, n, j)
                    point(2 * j)
                    if j >= 1:
                        down(c, n - 1, j - 1)
                    point(2 * j + 1)
                down(c, FT * c + (FT - 1), FT - 1)

            each_chunk(eng, body)

        @block.scalar
        def _(eng):
            def body(c, last):
                def point(p):
                    if p not in AT_POINT:
                        return
                    q, stage = AT_POINT[p]
                    e = EPC * c + q
                    if stage == 0:
                        ge(eng, s_e0, e + 1)
                        ge(eng, s_e1, e)
                        eng.activation(e_xt[:].rearrange("p k n -> p (k n)"), ps_m0[:], ACT.Copy)\
                            .then_inc(s_ext, 1)
                    if stage == 1:
                        ge(eng, s_e1, e + 1)
                        ge(eng, s_eh, e)
                        eng.activation(e_sil[:], ps_m0[:, 0:F], ACT.Silu).then_inc(s_esl, 1)
                    if stage == 3:
                        ge(eng, s_e3, e + 1)
                        ge(eng, s_yst, 16 * e)
                        eng.activation(e_y[:], ps_m1[:], ACT.Copy).then_inc(s_ey, 1)

                for j in range(FT):
                    n = FT * c + j
                    ge(eng, s_g, n + 1)
                    ge(eng, s_gu, n)
                    eng.activation(sil[:], ps_g[:], ACT.Silu).then_inc(s_sil, 1)
                    point(2 * j)
                    ge(eng, s_gu, n + 1)
                    ge(eng, s_dn, n if j == 0 else n - 1)
                    eng.activation(gu_h[:, j % 2], gu[:], ACT.Copy).then_inc(s_guh, 1)
                    point(2 * j + 1)

            each_chunk(eng, body)

        @block.vector
        def _(eng):
            def body(c, last):
                def point(p):
                    if p not in AT_POINT:
                        return
                    q, stage = AT_POINT[p]
                    e = EPC * c + q
                    if stage == 1:
                        ge(eng, s_esl, e + 1)
                        ge(eng, s_e2, e)
                        eng.tensor_tensor(e_h[:], e_sil[:], ps_m1[:, 0:F], ALU.mult).then_inc(s_eh, 1)
                    if stage == 2:
                        ge(eng, s_e2, e + 1)
                        ge(eng, s_e3, e)
                        eng.tensor_copy(e_ht[:, 0:2, :].rearrange("p a n -> p (a n)"), ps_m0[:, 0:2 * P])\
                            .then_inc(s_eht, 1)
                        eng.tensor_copy(e_ht[0:F - 2 * P, 2, :], ps_m0[0:F - 2 * P, 2 * P:3 * P])\
                            .then_inc(s_eht, 1)

                for j in range(FT):
                    n = FT * c + j
                    ge(eng, s_sil, n + 1)
                    ge(eng, s_u, n + 1)
                    ge(eng, s_guh, n)
                    ge(eng, s_gul, n)
                    eng.tensor_tensor(gu[:], sil[:], ps_u[:], ALU.mult).then_inc(s_gu, 1)
                    point(2 * j)
                    ge(eng, s_guh, n + 1)
                    eng.tensor_tensor(gu_l[:, j % 2], gu[:], gu_h[:, j % 2].bitcast(F32), ALU.subtract)\
                        .then_inc(s_gul, 1)
                    point(2 * j + 1)
                ge(eng, s_dn, FT * (c + 1))
                ge(eng, s_x1, 16 * QC * (c + 1))
                ge(eng, s_gb, 16 * (c + 1))
                for q in range(QC):
                    t = QC * c + q
                    ge(eng, s_res, t)
                    eng.scalar_tensor_tensor(out=tmp[:], in0=acc[q][:], scalar=sgate[:, rows(t, 1)],
                                             in1=gbc[:], op0=ALU.mult, op1=ALU.mult).then_inc(s_tmp, 1)
                    ge(eng, s_tmp, t + 1)
                    eng.tensor_tensor(res[:, q], res[:, q], tmp[:], ALU.add).then_inc(s_res, 1)

            each_chunk(eng, body)


def combine(nc, res_d, ye_d, slots, wtop, gbt, out):
    with ExitStack() as ctx:
        def sb(name, shape, dt=F32):
            return ctx.enter_context(nc.sbuf_tensor(name, shape, dt))

        def sem(name):
            return ctx.enter_context(nc.semaphore(name))

        idx = sb("idx", [P, 2, TOPK], U32)
        wts = sb("wts", [P, 2, TOPK])
        got = sb("got", [P, 2, TOPK, D])
        rest = sb("rest", [P, 2, D])
        total = sb("total", [P, 2, D])
        s_zero = sem("got_zeroed")
        s_idx = sem("indices_ready")
        s_got = [sem("rows_got0"), sem("rows_got1")]
        s_res = [sem("res_loaded0"), sem("res_loaded1")]
        s_sum = sem("sum_step")
        s_tot = sem("total_ready")
        s_out = [sem("out_stored0"), sem("out_stored1")]
        out_t = out.rearrange("b s d -> (b s) d")
        STEPS = 6
        passed = sem("waits_passed")
        block = ctx.enter_context(nc.Block())

        def rows(at, n):
            return slice(at, at + n) if isinstance(at, int) else bass.ds(at, n)

        def each_tile(eng, body):
            body(0)
            with eng.Fori(1, TT // 2) as i:
                body(2 * i)

        @block.gpsimd
        def _(eng):
            eng.memset(got[:], 0.0).then_inc(s_zero, 1)
            eng.wait_ge(s_zero, 1)

            def body(t):
                for r in range(2):
                    hold(eng, passed, s_tot, t + r - 1)
                    eng.tensor_copy(wts[:, r:r + 1, :], wtop[:, rows(t + r, 1), :]).then_inc(s_idx, 1)
                    eng.tensor_copy(idx[:, r:r + 1, :], slots[:, rows(t + r, 1), :]).then_inc(s_idx, 1)
                    hold(eng, passed, s_idx, 2 * (t + r + 1))
                    for k in range(TOPK):
                        eng.indirect_dma_start(
                            out=got[:, r, k], out_offset=None, in_=ye_d,
                            in_offset=bass.IndirectOffsetOnAxis(ap=idx[:, r, k:k + 1], axis=0),
                            bounds_check=SLOTS - 1, oob_is_err=False).then_inc(s_got[r], 16)

            each_tile(eng, body)

        @block.sync
        def _(eng):
            def body(t):
                for r in range(2):
                    hold(eng, passed, s_tot, t + r - 1)
                    eng.dma_start(rest[:, r], res_d[rows((t + r) * P, P), :]).then_inc(s_res[r], 16)
                for r in range(2):
                    hold(eng, passed, s_tot, t + r + 1)
                    eng.dma_start(out_t[rows((t + r) * P, P), :], total[:, r]).then_inc(s_out[r], 16)

            each_tile(eng, body)
            for r in range(2):
                eng.wait_ge(s_out[r], 16 * TT // 2)

        @block.vector
        def _(eng):
            def body(t0):
                for r in range(2):
                    t = t0 + r

                    def step(n, ins):
                        ins.then_inc(s_sum, 1)
                        ge(eng, s_sum, (STEPS - 1) * t + n)

                    b = 0
                    eng.wait_ge(s_got[r], t0 * (8 * TOPK) + 16 * TOPK)
                    eng.wait_ge(s_res[r], t0 * 8 + 16)
                    if not (isinstance(t0, int) and t0 == 0):
                        eng.wait_ge(s_out[r], t0 * 8)
                    step(1, eng.tensor_scalar(total[:, r], got[:, r, 0], wts[:, r, 0:1], None, ALU.mult))
                    for k in range(1, TOPK):
                        step(k + 1, eng.scalar_tensor_tensor(out=total[:, r], in0=got[:, r, k],
                                                             scalar=wts[:, r, k:k + 1], in1=total[:, r],
                                                             op0=ALU.mult, op1=ALU.add))
                    step(5, eng.tensor_tensor(total[:, r], total[:, r], gb_of(t0), ALU.mult))
                    eng.tensor_tensor(total[:, r], total[:, r], rest[:, r], ALU.add).then_inc(s_tot, 1)

            half = TT // 4
            gb_at = [0]

            def gb_of(t0):
                return gbt[:, gb_at[0]]

            body(0)
            with eng.Fori(1, half) as i:
                body(2 * i)
            gb_at[0] = 1
            with eng.Fori(half, 2 * half) as i:
                body(2 * i)


def kernel(L0_attn_query, L0_attn_key, L0_attn_value, L0_attn_Wqkv, L0_attn_Wproj, L0_attn_bproj,
           L0_ffn_Wr, L0_ffn_Wg, L0_ffn_Wu, L0_ffn_Wd, L0_ffn_Wsg, L0_ffn_Wsu, L0_ffn_Wsd, L0_ffn_Wse,
           L0_c, L0_wmod):
    import numpy as np
    import concourse.bacc as bacc
    from concourse.bass_utils import run_bass_kernel_spmd

    def tiles(w):
        w = np.asarray(w)
        return w.reshape(-1, P, w.shape[1]).transpose(1, 0, 2)

    wqkv = np.asarray(L0_attn_Wqkv).reshape(NH, 3, HN, D)
    qk = np.stack([np.concatenate([wqkv[2 * u, 0], wqkv[2 * u + 1, 0], wqkv[2 * u, 1], wqkv[2 * u + 1, 1]]).T
                   for u in range(NH // 2)])
    arrays = {
        "x": L0_attn_query,
        "wqk": qk.reshape(NH // 2, KT, P, P).transpose(0, 2, 1, 3),
        "wv": tiles(wqkv[:, 2].reshape(D, D).T),
        "wproj": tiles(np.asarray(L0_attn_Wproj).T),
        "bproj": np.asarray(L0_attn_bproj).reshape(1, D),
        "wr_se": tiles(np.concatenate([L0_ffn_Wr, L0_ffn_Wse], axis=1)),
        "c": np.asarray(L0_c).T.reshape(KT, P, B).transpose(1, 0, 2),
        "wmod": L0_wmod,
    }
    wsg = np.asarray(L0_ffn_Wsg).reshape(KT, P, FT, P).transpose(2, 1, 0, 3).reshape(FT, P, D)
    wsu = np.asarray(L0_ffn_Wsu).reshape(KT, P, FT, P).transpose(2, 1, 0, 3).reshape(FT, P, D)
    arrays["wsh"] = np.concatenate([wsg, wsu, np.asarray(L0_ffn_Wsd).reshape(FT, P, D)], axis=2)
    ep = E // 2
    g4 = [np.asarray(w).reshape(ep, 2, KT, P, F).transpose(0, 3, 1, 2, 4) for w in (L0_ffn_Wg, L0_ffn_Wu)]
    arrays["wgu"] = np.stack(g4, axis=2).reshape(ep, P, 2 * 2 * KT * F)
    wd = np.asarray(L0_ffn_Wd).reshape(ep, 2, F, D)
    arrays["wd_a"] = wd[:, :, :2 * P].reshape(ep, 2, 2, P, D).transpose(0, 3, 1, 2, 4).reshape(ep, P, 4 * D)
    arrays["wd_b"] = wd[:, :, 2 * P:].transpose(0, 2, 1, 3).reshape(ep, F - 2 * P, 2 * D)

    nc = bacc.Bacc("TRN2", target_bir_lowering=False, num_devices=1)
    given, aps = {}, {}
    for name, a in arrays.items():
        a = np.ascontiguousarray(a)
        given[f"in_{name}"] = a
        aps[name] = nc.dram_tensor(f"in_{name}", a.shape, mybir.dt.from_np(a.dtype), kind="ExternalInput").ap()
    aps["out"] = nc.dram_tensor("out_0", (B, S, D), F32, kind="ExternalOutput").ap()
    adaln_kernel(nc, **aps)
    r = run_bass_kernel_spmd(nc, [given], core_ids=[0])
    return r.results[0]["out_0"]
```

```python
from contextlib import ExitStack

import concourse.bass as bass
from concourse import mybir

ALU = mybir.AluOpType
ACT = mybir.ActivationFunctionType
AX = mybir.AxisListType
F32 = mybir.dt.float32
F32R = mybir.dt.float32r
BF16 = mybir.dt.bfloat16
U32 = mybir.dt.uint32
I32 = mybir.dt.int32

P = 128
B, S, D = 2, 1024, 512
T = B * S
KT = D // P
NH, HN = 16, 32
PAIRS = B * NH // 2
HALF = 512
TT = T // P
E, TOPK, F, CAP = 32, 4, 352, 64
FS = 1408
FT = FS // P
CH = T // HALF
SLOTS = E * CAP
EPS = 1e-5
F_TILES = [(0, 128), (128, 128), (256, 96)]
PAIR_BYTES = 4


def ge(eng, sem, value):
    if isinstance(value, int) and value <= 0:
        return
    eng.wait_ge(sem, value)


def hold(eng, passed, sem, value):
    ge(eng, sem, value)
    if not isinstance(value, int):
        eng.sem_inc(passed, 1)


def adaln_kernel(nc, x, wqk, wv, wproj, bproj, wr_se, c, wmod, wsh, wgu, wd_a, wd_b, out):
    mod_rows = nc.dram_tensor("mod_rows", (4, B, D), F32).ap()
    gb_rows = nc.dram_tensor("gb_rows", (CH, D), F32).ap()
    ctx_t = nc.dram_tensor("ctx_t", (D, B, S), F32).ap()
    x1_d = nc.dram_tensor("x1_d", (T, D), F32).ap()
    res_d = nc.dram_tensor("res_d", (T, D), F32).ap()
    xe_d = nc.dram_tensor("xe_d", (SLOTS, D), F32).ap()
    ye_d = nc.dram_tensor("ye_d", (SLOTS, D), F32).ap()

    with ExitStack() as top:
        ident = top.enter_context(nc.sbuf_tensor("ident", [P, P], F32))
        prologue_and_attention(nc, x, wqk, wv, c, wmod, mod_rows, gb_rows, ctx_t, xe_d, ident)
        slots = top.enter_context(nc.sbuf_tensor("slots", [P, TT, TOPK], U32))
        wtop = top.enter_context(nc.sbuf_tensor("wtop", [P, TT, TOPK], F32))
        gbt = top.enter_context(nc.sbuf_tensor("gbt", [P, B, D], F32))
        with ExitStack() as mid:
            sgate = mid.enter_context(nc.sbuf_tensor("sgate", [P, TT], F32))
            h2h = mid.enter_context(nc.sbuf_tensor("h2h", [P, KT, T], F32R))
            h2l = mid.enter_context(nc.sbuf_tensor("h2l", [P, KT, T], F32R))
            middle(nc, x, wproj, bproj, wr_se, mod_rows, ctx_t, x1_d, xe_d,
                   ident, slots, wtop, gbt, sgate, h2h, h2l)
            ffn(nc, wsh, wgu, wd_a, wd_b, x1_d, res_d, xe_d, ye_d, gb_rows, ident, sgate, h2h, h2l)
        combine(nc, res_d, ye_d, slots, wtop, gbt, out)


def prologue_and_attention(nc, x, wqk, wv, c, wmod, mod_rows, gb_rows, ctx_t, xe_d, ident):
    with ExitStack() as ctx:
        def sb(name, shape, dt=F32):
            return ctx.enter_context(nc.sbuf_tensor(name, shape, dt))

        hth = sb("hth", [P, KT, T], F32R)
        htl = sb("htl", [P, KT, T], F32R)
        v_all = sb("v_all", [P, TT, D])
        wqk_h = sb("wqk_h", [P, 2, KT, P], F32R)
        wqk_l = sb("wqk_l", [P, 2, KT, P], F32R)
        prologue(nc, x, wv, c, wmod, mod_rows, gb_rows, xe_d, ident, hth, htl, v_all)
        attention(nc, wqk, ctx_t, ident, hth, htl, v_all, wqk_h, wqk_l)


def prologue(nc, x, wv, c, wmod, mod_rows, gb_rows, xe_d, ident, hth, htl, v_all):
    GROUPS = T // HALF
    with ExitStack() as ctx:
        def sb(name, shape, dt=F32):
            return ctx.enter_context(nc.sbuf_tensor(name, shape, dt))

        def sem(name):
            return ctx.enter_context(nc.semaphore(name))

        c_sb = sb("c_sb", [P, KT, B])
        c_e = sb("c_e", [P, KT, B])
        c_silu = sb("c_silu", [P, KT, B])
        wm = sb("wm", [P, 2, 6 * D])
        rows = sb("rows", [P, 2, D])
        gate_s = sb("gate_s", [P, 2, D])
        gate_a = sb("gate_a", [P, 2, D])
        mod_t = sb("mod_t", [P, 2, KT, B])
        zero = sb("zero", [P, D])
        x_sb = sb("x_sb", [P, 4, D])
        xhat = sb("xhat", [P, 4, D])
        stats = sb("stats", [P, 4, 6])
        mv = sb("mv", [P, 4, 2])
        veps = sb("veps", [P, 4])
        rstd = sb("rstd", [P, 4])
        mhalf = sb("mhalf", [P, 4])
        hmod = sb("hmod", [P, 2, HALF])
        wv_raw = sb("wv_raw", [P, KT, D])
        wv_h = sb("wv_h", [P, KT, D], F32R)
        wv_l = sb("wv_l", [P, KT, D], F32R)
        banks = [ctx.enter_context(nc.psum_tensor(f"pro_bank{n}", [P, HALF], F32)) for n in range(8)]
        ps_mod, ps_modt, ps_v, ps_t = banks[0:2], banks[2:4], banks[0:4], banks[4:8]

        s_c = sem("c_loaded")
        s_wm = [sem("wmod_loaded0"), sem("wmod_loaded1")]
        s_wv = sem("wv_loaded")
        s_x = [sem(f"x_loaded{n}") for n in range(4)]
        s_e = sem("c_exp_done")
        s_silu = sem("c_silu_step")
        s_modk = sem("mod_k_done")
        s_rows = sem("rows_step")
        s_modt = sem("mod_t_done")
        s_modc = sem("mod_cols_ready")
        s_rowst = sem("rows_stored")
        s_id = sem("ident_step")
        s_zero = sem("zero_ready")
        s_xe = sem("xe_zeroed")
        s_stat = sem("stats_step")
        s_rstd = sem("rstd_ready")
        s_xh = sem("xhat_ready")
        s_tr = sem("transposed")
        s_hm = sem("hmod_ready")
        s_hh = sem("hth_ready")
        s_hl = sem("htl_ready")
        s_wvs = sem("wv_split")
        s_vps = sem("v_product_done")
        s_vev = sem("v_copied")

        x_t = x.rearrange("b s d -> (b s) d").rearrange("(n p) d -> n p d", p=P)
        wm_t = wmod.rearrange("(k p) n -> k p n", p=P)
        passed = sem("waits_passed")
        block = ctx.enter_context(nc.Block())

        @block.sync
        def _(eng):
            eng.dma_start(c_sb[:], c).then_inc(s_c, 16)
            for k in range(KT):
                if k >= 2:
                    hold(eng, passed, s_modk, k - 1)
                eng.dma_start(wm[:, k % 2], wm_t[k]).then_inc(s_wm[k % 2], 16)
                if k < 2:
                    for n in range(2 * k, 2 * k + 2):
                        eng.dma_start(x_sb[:, n], x_t[n]).then_inc(s_x[n], 16)
            eng.dma_start(wv_raw[:], wv).then_inc(s_wv, 16)
            for t in range(4, TT):
                hold(eng, passed, s_xh, t - 3)
                eng.dma_start(x_sb[:, t % 4], x_t[t]).then_inc(s_x[t % 4], 16)
            eng.wait_ge(s_rows, 7)
            for n, s in enumerate((2, 3, 4, 5)):
                src = rows[32 * (s % 4):32 * (s % 4) + B, s // 4, :]
                eng.dma_start(mod_rows[n], src).then_inc(s_rowst, 16)
            gb_v = gb_rows.rearrange("(b r) d -> r b d", b=B)
            for n in range(CH // B):
                eng.dma_start(gb_v[n], rows[32:32 + B, 1, :]).then_inc(s_rowst, 16)
            eng.wait_ge(s_zero, 1)
            for n in range(SLOTS // P):
                eng.dma_start(xe_d[n * P:(n + 1) * P, :], zero[:]).then_inc(s_xe, 16)
            hold(eng, passed, s_rowst, 16 * (4 + CH // B))
            hold(eng, passed, s_xe, 16 * (SLOTS // P))

        @block.gpsimd
        def _(eng):
            eng.memset(ident[:], 0.0).then_inc(s_id, 1)
            eng.memset(zero[:], 0.0).then_inc(s_zero, 1)
            eng.wait_ge(s_id, 1)
            eng.affine_select(out=ident[:], in_=ident[:], compare_op=ALU.not_equal, fill=1.0, base=0,
                              pattern=[[-1, P]], channel_multiplier=1).then_inc(s_id, 1)
            eng.memset(mhalf[:], -0.5).then_inc(s_id, 1)
            eng.wait_ge(s_id, 3)

            def rsqrt(g):
                hold(eng, passed, s_stat, 9 * (g + 1))
                eng.tensor_tensor(rstd[:], veps[:], mhalf[:], ALU.pow).then_inc(s_rstd, 1)

            rsqrt(0)
            rsqrt(1)
            eng.wait_ge(s_wv, 16)
            eng.tensor_copy(wv_h[:], wv_raw[:]).then_inc(s_wvs, 1)
            eng.wait_ge(s_wvs, 1)
            eng.tensor_tensor(wv_l[:], wv_raw[:], wv_h[:].bitcast(F32), ALU.subtract).then_inc(s_wvs, 1)
            rsqrt(2)
            rsqrt(3)

        @block.tensor
        def _(eng):
            eng.wait_ge(s_silu, 3)
            for k in range(KT):
                eng.wait_ge(s_wm[k % 2], 16 * (k // 2 + 1))
                for s in range(6):
                    mm = eng.matmul(ps_mod[s // 4][32 * (s % 4):32 * (s % 4) + B, :], c_silu[:, k, :],
                                    wm[:, k % 2, s * D:(s + 1) * D], start=(k == 0), stop=(k == KT - 1))
                mm.then_inc(s_modk, 1)
            eng.wait_ge(s_rows, 1)
            eng.wait_ge(s_id, 2)
            for s in range(2):
                for k in range(KT):
                    mm = eng.transpose(ps_modt[s][:, k * B:(k + 1) * B],
                                       rows[32 * s:32 * s + B, 0, k * P:(k + 1) * P],
                                       ident[32 * s:32 * s + B, 32 * s:32 * s + B])
            mm.then_inc(s_modt, 1)

            def transposes(g):
                for n in range(4):
                    eng.wait_ge(s_xh, 4 * g + n + 1)
                    for k in range(KT):
                        if n == 0 and g >= 1:
                            eng.wait_ge(s_hm, KT * (g - 1) + k + 1)
                        mm = eng.transpose(ps_t[k][:, n * P:(n + 1) * P],
                                           xhat[:, n, k * P:(k + 1) * P], ident[:])
                    mm.then_inc(s_tr, 1)

            def values(g):
                for n in range(4):
                    t = 4 * g + n
                    if t == 0:
                        eng.wait_ge(s_wvs, 2)
                        eng.wait_ge(s_modc, 2)
                        eng.wait_ge(s_rows, 2)
                    if n == 0:
                        eng.wait_ge(s_hh, KT * (g + 1))
                        eng.wait_ge(s_hl, KT * (g + 1))
                    ge(eng, s_vev, t - 3)
                    for k in range(KT):
                        for m, (a, w) in enumerate(((hth, wv_h), (hth, wv_l), (htl, wv_h))):
                            mm = eng.matmul(ps_v[t % 4][:], a[:, k, t * P:(t + 1) * P], w[:, k, :],
                                            start=(k == 0 and m == 0), stop=(k == KT - 1 and m == 2))
                    mm.then_inc(s_vps, 1)

            transposes(0)
            for g in range(GROUPS):
                if g + 1 < GROUPS:
                    transposes(g + 1)
                values(g)

        @block.scalar
        def _(eng):
            eng.wait_ge(s_c, 16)
            eng.activation(c_e[:], c_sb[:], ACT.Exp, scale=-1.0).then_inc(s_e, 1)
            for g in range(GROUPS):
                for k in range(KT):
                    eng.wait_ge(s_hm, KT * g + k + 1)
                    eng.activation(hth[:, k, g * HALF:(g + 1) * HALF], hmod[:, k % 2], ACT.Copy)\
                        .then_inc(s_hh, 1)
                if g >= 1:
                    for n in range(4):
                        t = 4 * (g - 1) + n
                        eng.wait_ge(s_vps, t + 1)
                        eng.activation(v_all[:, t], ps_v[t % 4][:], ACT.Copy).then_inc(s_vev, 1)
            for t in range(TT - 4, TT):
                eng.wait_ge(s_vps, t + 1)
                eng.activation(v_all[:, t], ps_v[t % 4][:], ACT.Copy).then_inc(s_vev, 1)

        @block.vector
        def _(eng):
            eng.wait_ge(s_e, 1)
            eng.tensor_scalar(c_e[:], c_e[:], 1.0, None, ALU.add).then_inc(s_silu, 1)
            eng.wait_ge(s_silu, 1)
            eng.reciprocal(c_e[:], c_e[:]).then_inc(s_silu, 1)
            eng.wait_ge(s_silu, 2)
            eng.tensor_tensor(c_silu[:], c_sb[:], c_e[:], ALU.mult).then_inc(s_silu, 1)

            def layer_norm(g):
                ge(eng, s_xh, 4 * g)
                for n in range(4):
                    eng.wait_ge(s_x[n], 16 * (g + 1))
                    eng.bn_stats(stats[:, n], x_sb[:, n]).then_inc(s_stat, 1)
                    eng.wait_ge(s_stat, 9 * g + 2 * n + 1)
                    eng.bn_aggr(mv[:, n], stats[:, n]).then_inc(s_stat, 1)
                    eng.wait_ge(s_stat, 9 * g + 2 * n + 2)
                eng.tensor_scalar(veps[:], mv[:, :, 1], EPS, None, ALU.add).then_inc(s_stat, 1)
                eng.wait_ge(s_rstd, g + 1)
                for n in range(4):
                    if g >= 1:
                        eng.wait_ge(s_tr, 4 * (g - 1) + n + 1)
                    eng.tensor_scalar(xhat[:, n], x_sb[:, n], mv[:, n, 0:1], rstd[:, n:n + 1],
                                      ALU.subtract, ALU.mult).then_inc(s_xh, 1)

            layer_norm(0)
            eng.wait_ge(s_modk, KT)
            for s in range(6):
                q = 32 * (s % 4)
                cp = eng.tensor_copy(rows[q:q + B, s // 4, :], ps_mod[s // 4][q:q + B, :])
                if s in (1, 5):
                    cp.then_inc(s_rows, 1)
            eng.wait_ge(s_rows, 2)
            for n, s in enumerate((2, 5)):
                q, m = 32 * (s % 4), s // 4
                eng.tensor_scalar(gate_s[q:q + B, m], rows[q:q + B, m], 0.0, 2.0, ALU.is_ge, ALU.mult)
                eng.scalar_tensor_tensor(out=gate_a[q:q + B, m], in0=rows[q:q + B, m], scalar=-1.0,
                                         in1=rows[q:q + B, m], op0=ALU.mult, op1=ALU.max)\
                    .then_inc(s_rows, 1)
            eng.wait_ge(s_rows, 4)
            for n, s in enumerate((2, 5)):
                q, m = 32 * (s % 4), s // 4
                eng.tensor_scalar(gate_a[q:q + B, m], gate_a[q:q + B, m], 0.25, None, ALU.max)\
                    .then_inc(s_rows, 1)
            eng.wait_ge(s_rows, 6)
            for n, s in enumerate((2, 5)):
                q, m = 32 * (s % 4), s // 4
                st = eng.scalar_tensor_tensor(out=rows[q:q + B, m], in0=gate_s[q:q + B, m], scalar=-1.0,
                                              in1=gate_a[q:q + B, m], op0=ALU.add, op1=ALU.mult)
            st.then_inc(s_rows, 1)
            eng.wait_ge(s_modt, 1)
            eng.tensor_copy(mod_t[:, 0].rearrange("p k b -> p (k b)"), ps_modt[0][:, 0:KT * B])\
                .then_inc(s_modc, 1)
            eng.tensor_scalar(mod_t[:, 1].rearrange("p k b -> p (k b)"), ps_modt[1][:, 0:KT * B],
                              1.0, None, ALU.add).then_inc(s_modc, 1)
            eng.wait_ge(s_modc, 2)

            for g in range(GROUPS):
                if g + 1 < GROUPS:
                    layer_norm(g + 1)
                b = g // (GROUPS // B)
                for k in range(KT):
                    n = KT * g + k
                    if n % KT == 0:
                        eng.wait_ge(s_tr, 4 * (g + 1))
                    ge(eng, s_hh, n - 1)
                    ge(eng, s_hl, n - 1)
                    eng.tensor_scalar(hmod[:, k % 2], ps_t[k][:], mod_t[:, 1, k, b:b + 1],
                                      mod_t[:, 0, k, b:b + 1], ALU.mult, ALU.add).then_inc(s_hm, 1)
                    eng.wait_ge(s_hh, n + 1)
                    eng.tensor_tensor(htl[:, k, g * HALF:(g + 1) * HALF], hmod[:, k % 2],
                                      hth[:, k, g * HALF:(g + 1) * HALF].bitcast(F32), ALU.subtract)\
                        .then_inc(s_hl, 1)


def attention(nc, wqk, ctx_t, ident, hth, htl, v_all, wqk_h, wqk_l):
    SCALE = float(HN) ** -0.5
    QT = S // P
    CC = S // HALF
    STACK = 3 * HN
    UNITS = [(hd, qt) for qt in range(QT) for hd in range(2)]
    PER_STEP = [0, 0, 2, 3, 3, 3, 3, 2]
    MOVES, MOVES_H = 8, 4
    with ExitStack() as ctx:
        def sb(name, shape, dt=F32):
            return ctx.enter_context(nc.sbuf_tensor(name, shape, dt))

        def sem(name):
            return ctx.enter_context(nc.semaphore(name))

        stack = sb("stack", [STACK + 2, 2, 4, S], F32R)
        part_h = sb("part_h", [P, S], F32R)
        part_l = sb("part_l", [P, S], F32R)
        w_raw = sb("w_raw", [P, 2, KT, P])
        probs = sb("probs", [P, 2, 2, S])
        v_one = sb("v_one", [P, 2, QT, 2, 2, HN])
        mx = sb("mx", [P, 2 * QT, CC])
        nmax = sb("nmax", [P, 2 * QT])
        mcat = sb("mcat", [P, 2, 2 * QT])
        mrow = sb("mrow", [4 * QT, P])
        o_sb = sb("o_sb", [P, S])
        rsum = sb("rsum", [P, S])
        cnorm = sb("cnorm", [P, S])
        ps_s = [ctx.enter_context(nc.psum_tensor(f"ps_s{n}", [P, HALF], F32)) for n in range(2)]
        ps_t = [ctx.enter_context(nc.psum_tensor(f"ps_t{n}", [P, S], F32)) for n in range(2)]
        ps_o = ctx.enter_context(nc.psum_tensor("ps_o", [P, S], F32))

        s_init = sem("constants_ready")
        s_wl = [sem("w_loaded0"), sem("w_loaded1")]
        s_ws = sem("w_split")
        s_wh = sem("w_high_part")
        s_proj = sem("proj_done")
        s_ph = sem("part_h_ready")
        s_pl = sem("part_l_ready")
        s_stk = sem("stack_loaded")
        s_stkh = sem("stack_first_third_loaded")
        s_sc = sem("scores_ready")
        s_mxd = sem("max_done")
        s_mch = sem("mcat_step")
        s_mt = sem("mrow_transposed")
        s_mc = sem("mrow_copied")
        s_mr = sem("mrow_loaded")
        s_st = sem("scores_t_ready")
        s_ex = sem("exp_done")
        s_pv = sem("pv_done")
        s_vo = sem("v_copied_pair")
        s_oc = sem("context_copied")
        s_rs = sem("rsum_ready")
        s_cn = sem("ctx_normed")
        s_cst = sem("ctx_stored")

        passed = sem("waits_passed")
        block = ctx.enter_context(nc.Block())

        def move_part(eng, part, r, j, n, done):
            eng.dma_start(stack[HN * n:HN * (n + 1), r, j, :].bitcast(F32),
                          part[HN * j:HN * (j + 1), :].bitcast(F32)).then_inc(done, 16)

        @block.sync
        def _(eng):
            def load_w(u, r):
                hold(eng, passed, s_ws, u - 1)
                eng.dma_start(w_raw[:, r], wqk[u]).then_inc(s_wl[r], 16)

            def move_stack(u, r):
                hold(eng, passed, s_ph, CC * (u + 1))
                hold(eng, passed, s_pl, CC * (u + 1))
                hold(eng, passed, s_st, 2 * QT * (u - 1))
                for j in range(4):
                    for n, part in enumerate((part_l, part_h) if j < 2 else (part_h, part_l)):
                        move_part(eng, part, r, j, n + 1, s_stk)

            def move_mrow(u, r):
                hold(eng, passed, s_mc, u + 1)
                for n in range(2):
                    eng.dma_start(stack[STACK + n:STACK + n + 1, r, 0:2, :]
                                  .rearrange("o j s -> o (j s)").bitcast(F32),
                                  mrow[2 * QT * n:2 * QT * (n + 1), :]).then_inc(s_mr, 16)

            def store_ctx(u):
                hold(eng, passed, s_cn, 2 * (u + 1))
                for b in range(2):
                    eng.dma_start(ctx_t[bass.ds(HN * u, HN), b, :] if not isinstance(u, int)
                                  else ctx_t[HN * u:HN * (u + 1), b, :],
                                  cnorm[64 * b:64 * b + HN, :]).then_inc(s_cst, 16)

            load_w(0, 0)
            load_w(1, 1)
            load_w(2, 0)
            move_stack(0, 0)
            load_w(3, 1)
            move_stack(1, 1)
            move_mrow(0, 0)

            def body(u, r, row, last=False):
                if row is not None:
                    hold(eng, passed, s_ws, u + 3)
                    src = wqk[row] if isinstance(row, int) else wqk[bass.ds(row, 1)]\
                        .rearrange("o p k n -> (o p) k n")
                    eng.dma_start(w_raw[:, r], src).then_inc(s_wl[r], 16)
                if not (last and r == 1):
                    move_mrow(u + 1, 1 - r)
                if not last:
                    move_stack(u + 2, r)
                store_ctx(u)

            for u in range(4):
                body(u, u % 2, (u + 4) % (NH // 2))
            with eng.Fori(2, 6) as i:
                for r in range(2):
                    body(2 * i + r, r, 2 * i + (r + 4 - NH // 2))
            for u in range(PAIRS - 4, PAIRS):
                body(u, u % 2, None, last=u >= PAIRS - 2)
            hold(eng, passed, s_cst, 32 * PAIRS)

        @block.gpsimd
        def _(eng):
            eng.memset(stack[STACK:STACK + 2].bitcast(F32), 1.0).then_inc(s_init, 1)
            eng.wait_ge(s_init, 1)
            eng.memset(v_one[:], 1.0).then_inc(s_init, 1)
            eng.wait_ge(s_init, 2)

            def split_w(u, r, waited):
                hold(eng, passed, s_wl[r], waited)
                hold(eng, passed, s_proj, CC * (u - 1))
                eng.tensor_copy(wqk_h[:, r], w_raw[:, r]).then_inc(s_wh, 1)
                hold(eng, passed, s_wh, u + 1)
                eng.tensor_tensor(wqk_l[:, r], w_raw[:, r], wqk_h[:, r].bitcast(F32), ALU.subtract)\
                    .then_inc(s_ws, 1)

            def copy_v(u, r, row, head):
                hold(eng, passed, s_pv, QT * (u - 1))
                cols = slice(head, head + 2 * HN) if isinstance(head, int) else bass.ds(head, 2 * HN)
                src = v_all[:, row:row + QT, cols]
                eng.tensor_copy(v_one[:, r, :, :, 0, :], src.rearrange("p t (a d) -> p t a d", a=2))\
                    .then_inc(s_vo, 1)

            def move_high(u, r):
                hold(eng, passed, s_ph, CC * (u + 1))
                hold(eng, passed, s_st, 2 * QT * (u - 1))
                for j in range(4):
                    move_part(eng, part_h, r, j, 0, s_stkh)

            for u in range(2):
                split_w(u, u, 16)
                copy_v(u, u, 0, u * 2 * HN)
            for u in range(2):
                move_high(u, u)
            for u in range(2, 4):
                split_w(u, u - 2, 32)
            def body(u, r, row, head, w):
                copy_v(u + 2, r, row, head)
                move_high(u + 2, r)
                if w is not None:
                    split_w(u + 4, r, w)

            for r in range(2):
                body(r, r, 0, (2 + r) * 2 * HN, 16 * 3)
            for lo, hi, batch in ((1, 3, 0), (3, 6, 1)):
                with eng.Fori(lo, hi) as i:
                    for r in range(2):
                        body(2 * i + r, r, QT * batch,
                             (2 * i + (r + 2 - 8 * batch)) * (2 * HN), i * 16 + 48)
            for u in (PAIRS - 4, PAIRS - 3):
                body(u, u % 2, QT, (u + 2 - 8) * 2 * HN, None)

        @block.tensor
        def _(eng):
            def proj(u, r, batch):
                ge(eng, s_ws, u + 1)
                for cc in range(CC):
                    if isinstance(u, int) and u < 2:
                        ge(eng, s_ph, CC * u)
                        ge(eng, s_pl, CC * u)
                    else:
                        eng.wait_ge(s_mxd, 4 * QT * u)
                        eng.wait_ge(s_mc, u)
                    at = batch * S + cc * HALF
                    for k in range(KT):
                        for m, (w, a) in enumerate(((wqk_h, hth), (wqk_l, hth), (wqk_h, htl))):
                            mm = eng.matmul(ps_s[cc][:], w[:, r, k, :], a[:, k, at:at + HALF],
                                            start=(k == 0 and m == 0), stop=(k == KT - 1 and m == 2))
                    mm.then_inc(s_proj, 1)

            def score(u, r, m):
                n, cc = m // CC, m % CC
                hd, qt = UNITS[n]
                if m == 0:
                    ge(eng, s_stk, 16 * MOVES * (u + 1))
                    ge(eng, s_stkh, 16 * MOVES_H * (u + 1))
                    if isinstance(u, int) and u < 2:
                        eng.wait_ge(s_ph, 2 * CC)
                        eng.wait_ge(s_pl, 2 * CC)
                    ge(eng, s_mc, u)
                if n == 0:
                    ge(eng, s_ph, CC * (u + 1))
                    ge(eng, s_pl, CC * (u + 1))
                else:
                    ge(eng, s_mxd, 4 * QT * u + m - 1)
                eng.matmul(ps_s[cc][:], stack[0:STACK, r, hd, qt * P:(qt + 1) * P],
                           stack[0:STACK, r, 2 + hd, cc * HALF:(cc + 1) * HALF],
                           start=True, stop=True).then_inc(s_sc, 1)

            def max_rows(u):
                ge(eng, s_mch, 3 * (u + 1))
                eng.transpose(ps_s[0][0:4 * QT, 0:P], mcat[:].rearrange("p a n -> p (a n)"), ident[:])\
                    .then_inc(s_mt, 1)

            def scores_t(u, r, kt, hd):
                if kt == 0 and hd == 0:
                    ge(eng, s_mr, 32 * (u + 1))
                ge(eng, s_ex, 2 * QT * u + 2 * kt + hd - 1)
                for cc in range(CC):
                    mm = eng.matmul(ps_t[hd][:, cc * HALF:(cc + 1) * HALF],
                                    stack[:, r, 2 + hd, kt * P:(kt + 1) * P],
                                    stack[:, r, hd, cc * HALF:(cc + 1) * HALF], start=True, stop=True)
                mm.then_inc(s_st, 1)

            def weighted(u, r, kt, cc):
                if cc == 0:
                    ge(eng, s_ex, 2 * QT * u + 2 * kt + 2)
                    if kt == 0:
                        ge(eng, s_vo, u + 1)
                        ge(eng, s_oc, u)
                for hd in range(2):
                    mm = eng.matmul(ps_o[64 * hd:64 * hd + 64, cc * HALF:(cc + 1) * HALF],
                                    v_one[:, r, kt, hd].rearrange("p a d -> p (a d)"),
                                    probs[:, kt % 2, hd, cc * HALF:(cc + 1) * HALF],
                                    start=(kt == 0), stop=(kt == QT - 1))
                if cc == CC - 1:
                    mm.then_inc(s_pv, 1)

            eng.wait_ge(s_init, 2)
            proj(0, 0, 0)
            proj(1, 1, 0)
            for m in range(4 * QT):
                score(0, 0, m)
            max_rows(0)

            def body(u, r, batch, last=False):
                more = not (last and r == 1)
                m = 0
                for kt in range(QT):
                    count = CC * PER_STEP[kt] if more else 0
                    gaps = [count // 6, (count * 3) // 6, (count * 4) // 6, count]
                    for seg in range(4):
                        if seg % 2 == 0:
                            scores_t(u, r, kt, seg // 2)
                        elif kt >= 1:
                            weighted(u, r, kt - 1, seg // 2)
                        for k in range(gaps[seg - 1] if seg else 0, gaps[seg]):
                            score(u + 1, 1 - r, m + k)
                    m += count
                weighted(u, r, QT - 1, 0)
                if more:
                    max_rows(u + 1)
                weighted(u, r, QT - 1, 1)
                if not last:
                    proj(u + 2, r, batch)

            for r in range(2):
                body(r, r, 0)
            for lo, hi, batch in ((1, 3, 0), (3, 7, 1)):
                with eng.Fori(lo, hi) as i:
                    for r in range(2):
                        body(2 * i + r, r, batch)
            for r in range(2):
                body(PAIRS - 2 + r, r, 0, last=True)

        @block.scalar
        def _(eng):
            def high_part(u):
                for cc in range(CC):
                    ge(eng, s_proj, CC * u + cc + 1)
                    if cc == 0:
                        ge(eng, s_stk, 16 * MOVES * u)
                        ge(eng, s_stkh, 16 * MOVES_H * u)
                    eng.activation(part_h[:, cc * HALF:(cc + 1) * HALF], ps_s[cc][:], ACT.Copy)\
                        .then_inc(s_ph, 1)

            def body(u, last=False):
                for kt in range(QT):
                    for hd in range(2):
                        ge(eng, s_st, 2 * QT * u + 2 * kt + hd + 1)
                        ge(eng, s_pv, QT * u + kt - 1)
                        eng.activation(probs[:, kt % 2, hd, :], ps_t[hd][:], ACT.Exp, scale=SCALE)\
                            .then_inc(s_ex, 1)
                ge(eng, s_pv, QT * (u + 1))
                ge(eng, s_cn, 2 * u)
                eng.activation(o_sb[:], ps_o[:], ACT.Copy).then_inc(s_oc, 1)
                if not last:
                    high_part(u + 2)

            high_part(0)
            high_part(1)
            for u in range(2):
                body(u)
            with eng.Fori(1, PAIRS // 2 - 1) as i:
                for r in range(2):
                    body(2 * i + r)
            for r in range(2):
                body(PAIRS - 2 + r, last=True)

        @block.vector
        def _(eng):
            def low_part(u):
                for cc in range(CC):
                    ge(eng, s_ph, CC * u + cc + 1)
                    if cc == 0:
                        ge(eng, s_stk, 16 * MOVES * u)
                    eng.tensor_tensor(part_l[:, cc * HALF:(cc + 1) * HALF], ps_s[cc][:],
                                      part_h[:, cc * HALF:(cc + 1) * HALF].bitcast(F32), ALU.subtract)\
                        .then_inc(s_pl, 1)

            def maxima(u):
                for n, (hd, qt) in enumerate(UNITS):
                    for cc in range(CC):
                        ge(eng, s_sc, 4 * QT * u + 2 * n + cc + 1)
                        if n == 0 and cc == 0:
                            ge(eng, s_mch, 3 * u)
                        at = hd * QT + qt
                        eng.tensor_reduce(mx[:, at, cc:cc + 1], ps_s[cc][:], AX.X, ALU.max)\
                            .then_inc(s_mxd, 1)
                ge(eng, s_mxd, 4 * QT * (u + 1))
                eng.tensor_reduce(nmax[:], mx[:], AX.X, ALU.max, negate=True).then_inc(s_mch, 1)
                ge(eng, s_mch, 3 * u + 1)
                ge(eng, s_mt, u)
                eng.tensor_copy(mcat[:, 0].bitcast(F32R), nmax[:]).then_inc(s_mch, 1)
                ge(eng, s_mch, 3 * u + 2)
                eng.tensor_tensor(mcat[:, 1].bitcast(F32R), nmax[:], mcat[:, 0], ALU.subtract)\
                    .then_inc(s_mch, 1)
                ge(eng, s_mt, u + 1)
                ge(eng, s_mr, 32 * u)
                eng.tensor_copy(mrow[:], ps_s[0][0:4 * QT, 0:P]).then_inc(s_mc, 1)

            def inverse(u, cc):
                if cc == 0:
                    ge(eng, s_oc, u + 1)
                    ge(eng, s_cn, 2 * u)
                at = slice(cc * HALF, (cc + 1) * HALF)
                eng.reciprocal(rsum[:, at], o_sb[:, at]).then_inc(s_rs, 1)

            def norm(u):
                ge(eng, s_rs, CC * (u + 1))
                ge(eng, s_cst, 32 * u)
                for hd in range(2):
                    q = 64 * hd
                    eng.tensor_tensor(cnorm[q:q + HN], o_sb[q:q + HN], rsum[q + HN:q + 2 * HN], ALU.mult)\
                        .then_inc(s_cn, 1)

            low_part(0)
            low_part(1)
            maxima(0)

            def body(u, more=True, last=False):
                if more:
                    maxima(u + 1)
                inverse(u, 0)
                if not last:
                    low_part(u + 2)
                inverse(u, 1)
                norm(u)

            for u in range(2):
                body(u)
            with eng.Fori(1, PAIRS // 2 - 1) as i:
                for r in range(2):
                    body(2 * i + r)
            body(PAIRS - 2, last=True)
            body(PAIRS - 1, more=False, last=True)


def middle(nc, x, wproj, bproj, wr_se, mod_rows, ctx_t, x1_d, xe_d,
           ident, slots, wtop, gbt, sgate, h2h, h2l):
    PR = TT // 2
    with ExitStack() as ctx:
        def sb(name, shape, dt=F32):
            return ctx.enter_context(nc.sbuf_tensor(name, shape, dt))

        def sem(name):
            return ctx.enter_context(nc.semaphore(name))

        wp_raw = sb("wp_raw", [P, KT, D])
        wp_h = sb("wp_h", [P, KT, D], F32R)
        wp_l = sb("wp_l", [P, KT, D], F32R)
        bp_raw = sb("bp_raw", [1, D])
        bp_h = sb("bp_h", [1, D], F32R)
        bp_l = sb("bp_l", [1, D], F32R)
        one_row = sb("one_row", [1, P], F32R)
        wrse = sb("wrse", [P, KT, E + 1])
        ga_t = sb("ga_t", [P, B, D])
        cb_t = sb("cb_t", [P, B, D])
        sb_t = sb("sb_t", [P, B, D])
        iota_e = sb("iota_e", [P, 2, TOPK, E])
        slot_a = sb("slot_a", [P, 2, E])
        slot_b = sb("slot_b", [P, 2, E])
        lower = sb("lower", [P, P], BF16)
        ones = sb("ones", [P, P], BF16)
        seen = sb("seen", [P, E], BF16)
        ct = sb("ct", [P, 2, KT, P])
        ct_h = sb("ct_h", [P, 2, KT, P], F32R)
        ct_l = sb("ct_l", [P, 2, KT, P], F32R)
        xt = sb("xt", [P, 2, D])
        x1 = sb("x1", [P, 2, D])
        xhat = sb("xhat2", [P, 2, D])
        h2 = sb("h2", [P, 2, 2, D])
        h2t = sb("h2t", [P, 2, KT, P])
        stats = sb("stats2", [P, 2, 6])
        mv = sb("mv2", [P, 2, 2])
        veps = sb("veps2", [P, 2])
        rstd = sb("rstd2", [P, 2])
        mhalf = sb("mhalf2", [P, 2])
        nmax = sb("nmax2", [P, 2])
        esum = sb("esum", [P, 2])
        ex = sb("ex", [P, 2, E])
        ese = sb("ese", [P, 2])
        prb = sb("prb", [P, 2, E])
        top8 = sb("top8", [P, 2, 8])
        idx8 = sb("idx8", [P, 2, 8], U32)
        idxf = sb("idxf", [P, 2, TOPK])
        onehot = sb("onehot", [P, 2, TOPK, E])
        mask = sb("mask", [P, 2, E], BF16)
        wsum = sb("wsum", [P, 2])
        wnorm = sb("wnorm", [P, 2, TOPK])
        over = sb("over", [P, 2, E])
        slotv = sb("slotv", [P, 2, E])
        pick = sb("pick", [P, 2, TOPK, E])
        slotf = sb("slotf", [P, 2, TOPK])
        slot_i = sb("slot_i", [P, 2, TOPK], U32)
        ps_y = [ctx.enter_context(nc.psum_tensor(f"ps_y{n}", [P, D], F32)) for n in range(2)]
        ps_h = [ctx.enter_context(nc.psum_tensor(f"ps_h{n}", [P, D], F32)) for n in range(2)]
        ps_r = ctx.enter_context(nc.psum_tensor("ps_r", [P, 2, D // 2], F32))
        ps_p = ctx.enter_context(nc.psum_tensor("ps_p", [P, 2, D // 2], F32))

        s_wp = sem("wproj_loaded")
        s_tb = sem("tables_loaded")
        s_wps = sem("wproj_split")
        s_bps = sem("bproj_split")
        s_tab = sem("tables_ready")
        s_cst = sem("mid_constants")
        s_ct = [sem("ctx_loaded0"), sem("ctx_loaded1")]
        s_xt = [sem("x_in0"), sem("x_in1")]
        s_cth = sem("ctx_high")
        s_ctl = sem("ctx_low")
        s_py = sem("projected")
        s_x1a = sem("gated")
        s_x1 = sem("x1_ready")
        s_x1s = [sem("x1_stored0"), sem("x1_stored1")]
        s_st = sem("stats2_step")
        s_rstd = sem("rstd2_ready")
        s_xh = sem("xhat2_ready")
        s_h2 = sem("h2_ready")
        s_tr = sem("h2_transposed")
        s_h2t = sem("h2t_ready")
        s_h2h = sem("h2h_ready")
        s_h2l = sem("h2l_ready")
        s_lg = sem("logits_ready")
        s_nm = sem("nmax_ready")
        s_ex = sem("router_exp")
        s_rt = sem("routing_step")
        s_mk = sem("mask_ready")
        s_pos = sem("positions_ready")
        s_sl = sem("slots_ready")
        s_sc = [sem("scattered0"), sem("scattered1")]

        x_t = x.rearrange("b s d -> (b s) d")
        ctx_v = ctx_t.rearrange("(k p) b s -> p k (b s)", p=P)

        def at(n, size):
            return slice(n, n + size) if isinstance(n, int) else bass.ds(n, size)

        def table(a, b):
            return a[:, b] if isinstance(b, int) else a[:, bass.ds(b, 1), :].rearrange("p o d -> p (o d)")

        def each_pair(eng, body):
            for i in range(2):
                body(i, i, 0)
            with eng.Fori(1, PR // 2 - 1) as j:
                body(2 * j, 0, j - 1)
                body(2 * j + 1, 1, 1)
            for i in range(PR - 2, PR):
                body(i, i % 2, 1)

        def exists(i):
            return not isinstance(i, int) or i < PR

        passed = sem("waits_passed")
        block = ctx.enter_context(nc.Block())

        @block.sync
        def _(eng):
            def load_ct(i):
                for r in range(2):
                    hold(eng, passed, s_ctl, 2 * i + (r - 1))
                    eng.dma_start(ct[:, r], ctx_v[:, :, at((2 * i + r) * P, P)]).then_inc(s_ct[r], 16)

            def load_xt(i, r):
                hold(eng, passed, s_x1, 2 * i + (r - 1))
                eng.dma_start(xt[:, r], x_t[at((2 * i + r) * P, P), :]).then_inc(s_xt[r], 16)

            def store_x1(i, r):
                hold(eng, passed, s_x1, 2 * i + (r + 1))
                eng.dma_start(x1_d[at((2 * i + r) * P, P), :], x1[:, r]).then_inc(s_x1s[r], 16)

            load_ct(0)
            eng.dma_start(wp_raw[:], wproj).then_inc(s_wp, 16)
            eng.dma_start(bp_raw[:], bproj).then_inc(s_tb, 16)
            for r in range(2):
                load_xt(0, r)
            eng.dma_start(wrse[:], wr_se).then_inc(s_tb, 16)
            for b in range(B):
                for src, dst in ((mod_rows[0], ga_t), (mod_rows[1], sb_t), (mod_rows[2], cb_t),
                                 (mod_rows[3], gbt)):
                    eng.dma_start(dst[:, b], src[b:b + 1, :].to_broadcast([P, D])).then_inc(s_tb, 16)
            load_ct(1)
            for r in range(2):
                store_x1(0, r)
                load_xt(1, r)

            def body(i, q, b):
                if exists(i + 2):
                    load_ct(i + 2)
                if exists(i + 1):
                    for r in range(2):
                        store_x1(i + 1, r)
                        if exists(i + 2):
                            load_xt(i + 2, r)

            each_pair(eng, body)
            for r in range(2):
                eng.wait_ge(s_x1s[r], 16 * PR)

        @block.gpsimd
        def _(eng):
            eng.wait_ge(s_wp, 16)
            eng.tensor_copy(wp_h[:], wp_raw[:]).then_inc(s_wps, 1)
            eng.wait_ge(s_wps, 1)
            eng.tensor_tensor(wp_l[:], wp_raw[:], wp_h[:].bitcast(F32), ALU.subtract).then_inc(s_wps, 1)
            eng.memset(mhalf[:], -0.5).then_inc(s_cst, 1)
            eng.memset(lower[:], 1.0).then_inc(s_cst, 1)
            eng.wait_ge(s_tb, 16 * (4 * B + 2))
            eng.tensor_scalar(cb_t[:], cb_t[:], 1.0, None, ALU.add).then_inc(s_tab, 1)
            eng.wait_ge(s_cst, 2)
            eng.affine_select(out=lower[:], in_=lower[:], compare_op=ALU.is_gt, fill=0.0, base=0,
                              pattern=[[1, P]], channel_multiplier=-1).then_inc(s_cst, 1)
            eng.iota(iota_e[:], pattern=[[0, 2], [0, TOPK], [1, E]], base=0, channel_multiplier=0,
                     allow_small_or_imprecise_dtypes=True).then_inc(s_cst, 1)
            eng.iota(slot_a[:], pattern=[[0, 2], [CAP, E]], base=0, channel_multiplier=0,
                     allow_small_or_imprecise_dtypes=True).then_inc(s_cst, 1)
            eng.iota(slot_b[:], pattern=[[0, 2], [T - CAP, E]], base=2 * SLOTS, channel_multiplier=0,
                     allow_small_or_imprecise_dtypes=True).then_inc(s_cst, 1)
            eng.memset(ones[:], 1.0).then_inc(s_cst, 1)
            eng.memset(seen[:], 0.0).then_inc(s_cst, 1)
            eng.wait_ge(s_cst, 8)

            def rsqrt(i):
                hold(eng, passed, s_st, 5 * (i + 1))
                eng.tensor_tensor(rstd[:], veps[:], mhalf[:], ALU.pow).then_inc(s_rstd, 1)

            def send(i, q, r):
                hold(eng, passed, s_sl, i + 1)
                for k in range(TOPK):
                    eng.indirect_dma_start(
                        out=xe_d, out_offset=bass.IndirectOffsetOnAxis(ap=slot_i[:, r, k:k + 1], axis=0),
                        in_=h2[:, q, r], in_offset=None, bounds_check=SLOTS - 1, oob_is_err=False)\
                        .then_inc(s_sc[r], 16)

            rsqrt(0)

            def body(i, q, b):
                if exists(i + 1):
                    rsqrt(i + 1)
                if not (isinstance(i, int) and i == 0):
                    send(i - 1, 1 - q, 1)
                send(i, q, 0)

            each_pair(eng, body)
            send(PR - 1, (PR - 1) % 2, 1)
            for r in range(2):
                eng.wait_ge(s_sc[r], 16 * TOPK * PR)

        @block.tensor
        def _(eng):
            def project(i):
                for r in range(2):
                    ge(eng, s_ctl, 2 * i + (r + 1))
                    ge(eng, s_x1a, 2 * i + (r - 1))
                    for k in range(KT):
                        for m, (a, w) in enumerate(((ct_h, wp_h), (ct_h, wp_l), (ct_l, wp_h))):
                            eng.matmul(ps_y[r][:], a[:, r, k, :], w[:, k, :],
                                       start=(k == 0 and m == 0), stop=False)
                    eng.matmul(ps_y[r][:], one_row[:], bp_h[:], start=False, stop=False)
                    eng.matmul(ps_y[r][:], one_row[:], bp_l[:], start=False, stop=True).then_inc(s_py, 1)

            def transposes(i, q):
                for r in range(2):
                    ge(eng, s_h2, 2 * i + (r + 1))
                    ge(eng, s_h2h, 2 * i + (r - 1))
                    for k in range(KT):
                        tr = eng.transpose(ps_h[r][:, k * P:(k + 1) * P], h2[:, q, r, k * P:(k + 1) * P],
                                           ident[:])
                    tr.then_inc(s_tr, 1)

            def logits(i):
                ge(eng, s_ex, 3 * i)
                for r in range(2):
                    ge(eng, s_h2t, 2 * i + (r + 1))
                    for k in range(KT):
                        mm = eng.matmul(ps_r[:, r, 0:E + 1], h2t[:, r, k, :], wrse[:, k, :],
                                        start=(k == 0), stop=(k == KT - 1))
                mm.then_inc(s_lg, 1)

            def positions(i):
                ge(eng, s_mk, 3 * i + 1)
                ge(eng, s_sl, i)
                eng.matmul(ps_p[:, 0, 0:E], lower[:], mask[:, 0], start=True, stop=False)
                eng.matmul(ps_p[:, 0, 0:E], ones[:], seen[:], start=False, stop=True)
                eng.matmul(ps_p[:, 1, 0:E], lower[:], mask[:, 1], start=True, stop=False)
                eng.matmul(ps_p[:, 1, 0:E], ones[:], mask[:, 0], start=False, stop=False)
                eng.matmul(ps_p[:, 1, 0:E], ones[:], seen[:], start=False, stop=True).then_inc(s_pos, 1)

            eng.wait_ge(s_wps, 2)
            eng.wait_ge(s_bps, 3)
            project(0)
            project(1)
            eng.wait_ge(s_cst, 8)
            transposes(0, 0)
            eng.wait_ge(s_tb, 16 * (4 * B + 2))
            logits(0)

            def body(i, q, b):
                if exists(i + 2):
                    project(i + 2)
                positions(i)
                if exists(i + 1):
                    transposes(i + 1, 1 - q)
                    logits(i + 1)

            each_pair(eng, body)

        @block.scalar
        def _(eng):
            def split(i):
                for r in range(2):
                    ge(eng, s_ct[r], 16 * (i + 1))
                    ge(eng, s_py, 2 * i + (r - 1))
                    eng.activation(ct_h[:, r], ct[:, r], ACT.Copy).then_inc(s_cth, 1)

            def copies(i):
                for r in range(2):
                    ge(eng, s_tr, 2 * i + (r + 1))
                    ge(eng, s_lg, i)
                    ge(eng, s_h2l, 2 * i)
                    eng.activation(h2t[:, r].rearrange("p k n -> p (k n)"), ps_h[r][:], ACT.Copy)\
                        .then_inc(s_h2t, 1)
                    eng.activation(h2h[:, :, at((2 * i + r) * P, P)],
                                   ps_h[r][:].rearrange("p (k n) -> p k n", k=KT), ACT.Copy)\
                        .then_inc(s_h2h, 1)

            def exps(i):
                ge(eng, s_nm, i + 1)
                for r in range(2):
                    eng.activation(ex[:, r], ps_r[:, r, 0:E], ACT.Exp, bias=nmax[:, r:r + 1],
                                   accum_out=esum[:, r:r + 1]).then_inc(s_ex, 1)
                eng.activation(ese[:], ps_r[:, :, E], ACT.Exp, scale=-1.0).then_inc(s_ex, 1)

            split(0)
            split(1)
            copies(0)

            def body(i, q, b):
                if exists(i + 2):
                    split(i + 2)
                exps(i)
                if exists(i + 1):
                    copies(i + 1)

            each_pair(eng, body)

        @block.vector
        def _(eng):
            STEPS = 14

            def low_ct(i):
                for r in range(2):
                    ge(eng, s_cth, 2 * i + (r + 1))
                    ge(eng, s_py, 2 * i + (r - 1))
                    eng.tensor_tensor(ct_l[:, r], ct[:, r], ct_h[:, r].bitcast(F32), ALU.subtract)\
                        .then_inc(s_ctl, 1)

            def residual(i, b):
                for r in range(2):
                    ge(eng, s_py, 2 * i + (r + 1))
                    ge(eng, s_x1s[r], 16 * i)
                    ge(eng, s_xh, 2 * i)
                    eng.tensor_tensor(x1[:, r], ps_y[r][:], table(ga_t, b), ALU.mult).then_inc(s_x1a, 1)
                for r in range(2):
                    ge(eng, s_xt[r], 16 * (i + 1))
                    ge(eng, s_x1a, 2 * i + (r + 1))
                    eng.tensor_tensor(x1[:, r], x1[:, r], xt[:, r], ALU.add).then_inc(s_x1, 1)
                for r in range(2):
                    ge(eng, s_x1, 2 * i + (r + 1))
                    eng.bn_stats(stats[:, r], x1[:, r]).then_inc(s_st, 1)
                for r in range(2):
                    hold(eng, passed, s_st, 5 * i + (r + 1))
                    eng.bn_aggr(mv[:, r], stats[:, r]).then_inc(s_st, 1)
                ge(eng, s_st, 5 * i + 4)
                ge(eng, s_rstd, i)
                eng.tensor_scalar(veps[:], mv[:, :, 1], EPS, None, ALU.add).then_inc(s_st, 1)

            def modulate(i, q, b):
                for r in range(2):
                    ge(eng, s_h2, 2 * i)
                    eng.scalar_tensor_tensor(out=xhat[:, r], in0=x1[:, r], scalar=mv[:, r, 0:1],
                                             in1=table(cb_t, b), op0=ALU.subtract, op1=ALU.mult)\
                        .then_inc(s_xh, 1)
                ge(eng, s_rstd, i + 1)
                for r in range(2):
                    ge(eng, s_xh, 2 * i + (r + 1))
                    if not (isinstance(i, int) and i < 2):
                        ge(eng, s_tr, 2 * i - 2)
                        ge(eng, s_sc[r], (16 * TOPK) * i - 16 * TOPK)
                    eng.scalar_tensor_tensor(out=h2[:, q, r], in0=xhat[:, r], scalar=rstd[:, r:r + 1],
                                             in1=table(sb_t, b), op0=ALU.mult, op1=ALU.add)\
                        .then_inc(s_h2, 1)

            def router_max(i):
                ge(eng, s_lg, i + 1)
                ge(eng, s_ex, 3 * i)
                eng.tensor_reduce(nmax[:], ps_r[:, :, 0:E], AX.X, ALU.max, negate=True).then_inc(s_nm, 1)

            def low(i):
                for r in range(2):
                    ge(eng, s_h2h, 2 * i + (r + 1))
                    cols = at((2 * i + r) * P, P)
                    eng.tensor_tensor(h2l[:, :, cols], h2t[:, r], h2h[:, :, cols].bitcast(F32),
                                      ALU.subtract).then_inc(s_h2l, 1)

            def route(i):
                def step(n, ins):
                    ins.then_inc(s_rt, 1)

                def after(n, alone=False):
                    if alone:
                        hold(eng, passed, s_rt, STEPS * i + n)
                    else:
                        ge(eng, s_rt, STEPS * i + n)

                ge(eng, s_ex, 3 * i + 3)
                step(1, eng.reciprocal(esum[:], esum[:]))
                step(2, eng.tensor_scalar(ese[:], ese[:], 1.0, None, ALU.add))
                after(1)
                step(3, eng.tensor_tensor(prb[:], ex[:], esum[:].unsqueeze(2).to_broadcast([P, 2, E]),
                                          ALU.mult))
                after(3, alone=True)
                for r in range(2):
                    mxi = eng.max(top8[:, r], prb[:, r])
                step(4, mxi)
                after(4, alone=True)
                for r in range(2):
                    mxi = eng.max_index(idx8[:, r], top8[:, r], prb[:, r])
                step(5, mxi)
                eng.reciprocal(sgate[:, at(2 * i, 2)], ese[:])
                after(5)
                step(6, eng.tensor_copy(idxf[:], idx8[:, :, 0:TOPK]))
                eng.tensor_reduce(wsum[:], top8[:, :, 0:TOPK], AX.X, ALU.add)
                after(6)
                step(7, eng.tensor_tensor(onehot[:], iota_e[:],
                                          idxf[:].unsqueeze(3).to_broadcast([P, 2, TOPK, E]), ALU.is_equal))
                after(7)
                with nc.allow_low_precision(reason="sums of a one and three zeros are exact"):
                    eng.tensor_reduce(mask[:], onehot[:].rearrange("p r k e -> p r e k"), AX.X, ALU.add)\
                        .then_inc(s_mk, 1)
                step(8, eng.reciprocal(wsum[:], wsum[:]))
                after(8)
                step(9, eng.tensor_tensor(wnorm[:], top8[:, :, 0:TOPK],
                                          wsum[:].unsqueeze(2).to_broadcast([P, 2, TOPK]), ALU.mult))
                ge(eng, s_pos, i + 1)
                eng.tensor_tensor(seen[:], seen[:], mask[:, 0], ALU.add).then_inc(s_mk, 1)
                eng.scalar_tensor_tensor(out=over[:], in0=ps_p[:, :, 0:E], scalar=float(CAP),
                                         in1=slot_b[:], op0=ALU.is_ge, op1=ALU.mult)
                step(10, eng.tensor_tensor(slotv[:], ps_p[:, :, 0:E], slot_a[:], ALU.add))
                ge(eng, s_mk, 3 * i + 2)
                eng.tensor_tensor(seen[:], seen[:], mask[:, 1], ALU.add).then_inc(s_mk, 1)
                after(10)
                step(11, eng.tensor_tensor(slotv[:], slotv[:], over[:], ALU.add))
                after(11)
                step(12, eng.tensor_tensor(pick[:], onehot[:],
                                           slotv[:].unsqueeze(2).to_broadcast([P, 2, TOPK, E]), ALU.mult))
                after(12)
                step(13, eng.tensor_reduce(slotf[:], pick[:], AX.X, ALU.add))
                after(13)
                step(14, eng.scalar_tensor_tensor(out=wtop[:, at(2 * i, 2), :], in0=slotf[:],
                                                  scalar=float(SLOTS), in1=wnorm[:],
                                                  op0=ALU.is_lt, op1=ALU.mult))
                for r in range(2):
                    ge(eng, s_sc[r], 16 * TOPK * i)
                eng.tensor_copy(slots[:, at(2 * i, 2), :], slotf[:])
                eng.tensor_copy(slot_i[:], slotf[:]).then_inc(s_sl, 1)

            eng.memset(one_row[:].bitcast(F32), 1.0).then_inc(s_bps, 1)
            eng.wait_ge(s_tb, 16 * (4 * B + 2))
            eng.tensor_copy(bp_h[:], bp_raw[:]).then_inc(s_bps, 1)
            eng.wait_ge(s_bps, 2)
            eng.tensor_tensor(bp_l[:], bp_raw[:], bp_h[:].bitcast(F32), ALU.subtract).then_inc(s_bps, 1)
            low_ct(0)
            low_ct(1)
            residual(0, 0)
            eng.wait_ge(s_tab, 1)
            modulate(0, 0, 0)
            eng.wait_ge(s_cst, 8)

            def body(i, q, b):
                if exists(i + 2):
                    low_ct(i + 2)
                if exists(i + 1):
                    residual(i + 1, b)
                router_max(i)
                low(i)
                route(i)
                if exists(i + 1):
                    modulate(i + 1, 1 - q, b)

            each_pair(eng, body)


def ffn(nc, wsh, wgu, wd_a, wd_b, x1_d, res_d, xe_d, ye_d, gb_rows, ident, sgate, h2h, h2l):
    EPC = E // 2 // CH
    QC = HALF // P
    STAGES = 4 * EPC
    AT_POINT = {(s * 2 * FT) // STAGES: (s // 4, s % 4) for s in range(STAGES)}
    SLOT_USES = [len(range(s, FT, 3)) for s in range(3)]

    def before(n, j):
        return n - 3 if j >= 3 else n - (j + 1 + (FT - 1 - j) % 3)

    with ExitStack() as ctx:
        def sb(name, shape, dt=F32):
            return ctx.enter_context(nc.sbuf_tensor(name, shape, dt))

        def sem(name):
            return ctx.enter_context(nc.semaphore(name))

        def psum(name):
            return ctx.enter_context(nc.psum_tensor(name, [P, HALF], F32))

        w_raw = sb("ws_raw", [P, 3, 3 * D])
        w_h = sb("ws_h", [P, 3, 3 * D], F32R)
        w_l = sb("ws_l", [P, 3, 3 * D], F32R)
        sil = sb("sil", [P, HALF])
        gu = sb("gu", [P, HALF])
        gu_h = sb("gu_h", [P, 2, HALF], F32R)
        gu_l = sb("gu_l", [P, 2, HALF], F32R)
        res = sb("res", [P, QC, D])
        tmp = sb("tmp", [P, D])
        gbc = sb("gbc", [P, D])
        e_gu = sb("e_gu", [P, 2, 2, KT, F])
        e_da = sb("e_da", [P, 2, 2, D])
        e_db = sb("e_db", [F - 2 * P, 2, D])
        e_x = sb("e_x", [P, D])
        e_xt = sb("e_xt", [P, KT, P])
        e_sil = sb("e_sil", [P, F])
        e_h = sb("e_h", [P, F])
        e_ht = sb("e_ht", [P, 3, P])
        e_y = sb("e_y", [P, D])
        acc = [psum(f"ps_acc{n}") for n in range(QC)]
        ps_g, ps_u, ps_m0, ps_m1 = psum("ps_gate"), psum("ps_up"), psum("ps_m0"), psum("ps_m1")

        s_wl = [sem(f"ws_loaded{n}") for n in range(3)]
        s_wh = sem("ws_high")
        s_ws = sem("ws_split")
        s_g = sem("gate_done")
        s_u = sem("up_done")
        s_sil = sem("silu_done")
        s_gu = sem("gu_ready")
        s_guh = sem("gu_high")
        s_gul = sem("gu_low")
        s_dn = sem("down_done")
        s_x1 = sem("x1_chunk_loaded")
        s_gb = sem("gb_loaded")
        s_tmp = sem("shared_gated")
        s_res = sem("res_ready")
        s_rst = sem("res_stored")
        s_lgu = sem("expert_gate_up_loaded")
        s_ld = sem("expert_down_loaded")
        s_lx = sem("expert_tokens_loaded")
        s_e0 = sem("expert_tokens_transposed")
        s_ext = sem("expert_tokens_copied")
        s_e1 = sem("expert_gate_up_done")
        s_esl = sem("expert_silu_done")
        s_eh = sem("expert_hidden_ready")
        s_e2 = sem("expert_hidden_transposed")
        s_eht = sem("expert_hidden_copied")
        s_e3 = sem("expert_down_done")
        s_ey = sem("expert_rows_copied")
        s_yst = sem("expert_rows_stored")

        def each_chunk(eng, body):
            body(0, False)
            with eng.Fori(1, CH - 1) as c:
                body(c, False)
            body(CH - 1, True)

        def rows(at, n):
            return slice(at, at + n) if isinstance(at, int) else bass.ds(at, n)

        def at(a, i):
            return a[i] if isinstance(i, int) else a[bass.ds(i, 1)].rearrange("o p n -> (o p) n")

        passed = sem("waits_passed")
        block = ctx.enter_context(nc.Block())

        @block.sync
        def _(eng):
            def load_shared(n, j):
                hold(eng, passed, s_ws, before(n, j) + 1)
                eng.dma_start(w_raw[:, j % 3], wsh[j]).then_inc(s_wl[j % 3], 16)

            def load_gu(e):
                hold(eng, passed, s_e1, e)
                eng.dma_start(e_gu[:].rearrange("p a b k f -> p (a b k f)"), at(wgu, e)).then_inc(s_lgu, 16)

            def load_x(e):
                hold(eng, passed, s_e0, e)
                eng.dma_start(e_x[:], xe_d[rows(e * P, P), :]).then_inc(s_lx, 16)

            def load_down(e):
                hold(eng, passed, s_e3, e)
                eng.dma_start(e_da[:].rearrange("p a b n -> p (a b n)"), at(wd_a, e)).then_inc(s_ld, 16)
                eng.dma_start(e_db[:].rearrange("p a n -> p (a n)"), at(wd_b, e)).then_inc(s_ld, 16)

            def store_y(e):
                hold(eng, passed, s_ey, e + 1)
                eng.dma_start(ye_d[rows(e * P, P), :], e_y[:]).then_inc(s_yst, 16)

            load_shared(0, 0)
            load_shared(1, 1)
            load_x(0)
            load_gu(0)
            load_down(0)

            def body(c, last):
                hold(eng, passed, s_rst, 16 * QC * c)
                hold(eng, passed, s_tmp, QC * c)
                for q in range(QC):
                    eng.dma_start(res[:, q], x1_d[rows(c * HALF + q * P, P), :]).then_inc(s_x1, 16)
                src = gb_rows[rows(c, 1), :]
                eng.dma_start(gbc[:], src.to_broadcast([P, D])).then_inc(s_gb, 16)
                for j in range(FT):
                    n = FT * c + j
                    if not (last and j + 2 >= FT):
                        load_shared(n + 2, (j + 2) % FT)
                    for point in (2 * j, 2 * j + 1):
                        if point in AT_POINT:
                            q, stage = AT_POINT[point]
                            e = EPC * c + q
                            more = not (last and q == EPC - 1)
                            if stage == 0 and more:
                                load_x(e + 1)
                            if stage == 1 and more:
                                load_gu(e + 1)
                            if stage == 3:
                                if more:
                                    load_down(e + 1)
                                store_y(e)
                hold(eng, passed, s_res, QC * (c + 1))
                for q in range(QC):
                    eng.dma_start(res_d[rows(c * HALF + q * P, P), :], res[:, q]).then_inc(s_rst, 16)

            each_chunk(eng, body)
            hold(eng, passed, s_rst, 16 * QC * CH)
            hold(eng, passed, s_yst, 16 * E // 2)

        @block.gpsimd
        def _(eng):
            def body(c, last):
                for j in range(FT):
                    n = FT * c + j
                    use = SLOT_USES[j % 3] * c + (j // 3 + 1)
                    hold(eng, passed, s_wl[j % 3], use * 16)
                    hold(eng, passed, s_dn, before(n, j) + 1)
                    eng.tensor_copy(w_h[:, j % 3], w_raw[:, j % 3]).then_inc(s_wh, 1)
                    hold(eng, passed, s_wh, n + 1)
                    eng.tensor_tensor(w_l[:, j % 3], w_raw[:, j % 3], w_h[:, j % 3].bitcast(F32),
                                      ALU.subtract).then_inc(s_ws, 1)

            each_chunk(eng, body)

        @block.tensor
        def _(eng):
            def gate_up(c, n, j):
                ge(eng, s_ws, n + 1)
                for part, (bank, done, free) in enumerate(((ps_g, s_g, s_sil), (ps_u, s_u, s_gu))):
                    ge(eng, free, n)
                    for k in range(KT):
                        col = part * D + k * P
                        for m, (w, h) in enumerate(((w_h, h2h), (w_l, h2h), (w_h, h2l))):
                            mm = eng.matmul(bank[:], w[:, j % 3, col:col + P],
                                            h[:, k, rows(c * HALF, HALF)],
                                            start=(k == 0 and m == 0), stop=(k == KT - 1 and m == 2))
                    mm.then_inc(done, 1)

            def down(c, n, j):
                ge(eng, s_guh, n + 1)
                ge(eng, s_gul, n + 1)
                if j == 0:
                    ge(eng, s_tmp, QC * c)
                for q in range(QC):
                    for m, (g, w) in enumerate(((gu_h, w_h), (gu_h, w_l), (gu_l, w_h))):
                        mm = eng.matmul(acc[q][:], g[:, j % 2, q * P:(q + 1) * P],
                                        w[:, j % 3, 2 * D:3 * D],
                                        start=(j == 0 and m == 0), stop=(j == FT - 1 and m == 2))
                mm.then_inc(s_dn, 1)

            def stage0(e):
                ge(eng, s_lx, 16 * (e + 1))
                ge(eng, s_eht, 2 * e)
                for k in range(KT):
                    mm = eng.transpose(ps_m0[:, k * P:(k + 1) * P], e_x[:, k * P:(k + 1) * P], ident[:])
                mm.then_inc(s_e0, 1)

            def stage1(e):
                ge(eng, s_ext, e + 1)
                ge(eng, s_lgu, 16 * (e + 1))
                ge(eng, s_ey, e)
                for part, bank in enumerate((ps_m0, ps_m1)):
                    for k in range(KT):
                        for a in range(2):
                            mm = eng.matmul(bank[CAP * a:CAP * (a + 1), 0:F], e_xt[:, k, CAP * a:CAP * (a + 1)],
                                            e_gu[:, part, a, k, :], start=(k == 0), stop=(k == KT - 1))
                mm.then_inc(s_e1, 1)

            def stage2(e):
                ge(eng, s_eh, e + 1)
                for n, (f0, fs) in enumerate(F_TILES):
                    mm = eng.transpose(ps_m0[0:fs, n * P:(n + 1) * P], e_h[:, f0:f0 + fs], ident[:])
                mm.then_inc(s_e2, 1)

            def stage3(e):
                ge(eng, s_eht, 2 * (e + 1))
                ge(eng, s_ld, 32 * (e + 1))
                for n, (f0, fs) in enumerate(F_TILES):
                    for a in range(2):
                        w = e_da[:, a, n, :] if n < 2 else e_db[:, a, :]
                        mm = eng.matmul(ps_m1[CAP * a:CAP * (a + 1), :], e_ht[0:fs, n, CAP * a:CAP * (a + 1)],
                                        w, start=(n == 0), stop=(n == 2))
                mm.then_inc(s_e3, 1)

            stages = (stage0, stage1, stage2, stage3)

            def body(c, last):
                def point(p):
                    if p in AT_POINT:
                        q, stage = AT_POINT[p]
                        stages[stage](EPC * c + q)

                for j in range(FT):
                    n = FT * c + j
                    gate_up(c, n, j)
                    point(2 * j)
                    if j >= 1:
                        down(c, n - 1, j - 1)
                    point(2 * j + 1)
                down(c, FT * c + (FT - 1), FT - 1)

            each_chunk(eng, body)

        @block.scalar
        def _(eng):
            def body(c, last):
                def point(p):
                    if p not in AT_POINT:
                        return
                    q, stage = AT_POINT[p]
                    e = EPC * c + q
                    if stage == 0:
                        ge(eng, s_e0, e + 1)
                        ge(eng, s_e1, e)
                        eng.activation(e_xt[:].rearrange("p k n -> p (k n)"), ps_m0[:], ACT.Copy)\
                            .then_inc(s_ext, 1)
                    if stage == 1:
                        ge(eng, s_e1, e + 1)
                        ge(eng, s_eh, e)
                        eng.activation(e_sil[:], ps_m0[:, 0:F], ACT.Silu).then_inc(s_esl, 1)
                    if stage == 3:
                        ge(eng, s_e3, e + 1)
                        ge(eng, s_yst, 16 * e)
                        eng.activation(e_y[:], ps_m1[:], ACT.Copy).then_inc(s_ey, 1)

                for j in range(FT):
                    n = FT * c + j
                    ge(eng, s_g, n + 1)
                    ge(eng, s_gu, n)
                    eng.activation(sil[:], ps_g[:], ACT.Silu).then_inc(s_sil, 1)
                    point(2 * j)
                    ge(eng, s_gu, n + 1)
                    ge(eng, s_dn, n if j == 0 else n - 1)
                    eng.activation(gu_h[:, j % 2], gu[:], ACT.Copy).then_inc(s_guh, 1)
                    point(2 * j + 1)

            each_chunk(eng, body)

        @block.vector
        def _(eng):
            def body(c, last):
                def point(p):
                    if p not in AT_POINT:
                        return
                    q, stage = AT_POINT[p]
                    e = EPC * c + q
                    if stage == 1:
                        ge(eng, s_esl, e + 1)
                        ge(eng, s_e2, e)
                        eng.tensor_tensor(e_h[:], e_sil[:], ps_m1[:, 0:F], ALU.mult).then_inc(s_eh, 1)
                    if stage == 2:
                        ge(eng, s_e2, e + 1)
                        ge(eng, s_e3, e)
                        eng.tensor_copy(e_ht[:, 0:2, :].rearrange("p a n -> p (a n)"), ps_m0[:, 0:2 * P])\
                            .then_inc(s_eht, 1)
                        eng.tensor_copy(e_ht[0:F - 2 * P, 2, :], ps_m0[0:F - 2 * P, 2 * P:3 * P])\
                            .then_inc(s_eht, 1)

                for j in range(FT):
                    n = FT * c + j
                    ge(eng, s_sil, n + 1)
                    ge(eng, s_u, n + 1)
                    ge(eng, s_guh, n)
                    ge(eng, s_gul, n)
                    eng.tensor_tensor(gu[:], sil[:], ps_u[:], ALU.mult).then_inc(s_gu, 1)
                    point(2 * j)
                    ge(eng, s_guh, n + 1)
                    eng.tensor_tensor(gu_l[:, j % 2], gu[:], gu_h[:, j % 2].bitcast(F32), ALU.subtract)\
                        .then_inc(s_gul, 1)
                    point(2 * j + 1)
                ge(eng, s_dn, FT * (c + 1))
                ge(eng, s_x1, 16 * QC * (c + 1))
                ge(eng, s_gb, 16 * (c + 1))
                for q in range(QC):
                    t = QC * c + q
                    ge(eng, s_res, t)
                    eng.scalar_tensor_tensor(out=tmp[:], in0=acc[q][:], scalar=sgate[:, rows(t, 1)],
                                             in1=gbc[:], op0=ALU.mult, op1=ALU.mult).then_inc(s_tmp, 1)
                    ge(eng, s_tmp, t + 1)
                    eng.tensor_tensor(res[:, q], res[:, q], tmp[:], ALU.add).then_inc(s_res, 1)

            each_chunk(eng, body)


def combine(nc, res_d, ye_d, slots, wtop, gbt, out):
    with ExitStack() as ctx:
        def sb(name, shape, dt=F32):
            return ctx.enter_context(nc.sbuf_tensor(name, shape, dt))

        def sem(name):
            return ctx.enter_context(nc.semaphore(name))

        idx = sb("idx", [P, 2, TOPK], U32)
        wts = sb("wts", [P, 2, TOPK])
        got = sb("got", [P, 2, TOPK, D])
        rest = sb("rest", [P, 2, D])
        total = sb("total", [P, 2, D])
        s_zero = sem("got_zeroed")
        s_idx = sem("indices_ready")
        s_got = [sem("rows_got0"), sem("rows_got1")]
        s_res = [sem("res_loaded0"), sem("res_loaded1")]
        s_sum = sem("sum_step")
        s_tot = sem("total_ready")
        s_out = [sem("out_stored0"), sem("out_stored1")]
        out_t = out.rearrange("b s d -> (b s) d")
        STEPS = 6
        passed = sem("waits_passed")
        block = ctx.enter_context(nc.Block())

        def rows(at, n):
            return slice(at, at + n) if isinstance(at, int) else bass.ds(at, n)

        def each_tile(eng, body):
            body(0)
            with eng.Fori(1, TT // 2) as i:
                body(2 * i)

        @block.gpsimd
        def _(eng):
            eng.memset(got[:], 0.0).then_inc(s_zero, 1)
            eng.wait_ge(s_zero, 1)

            def body(t):
                for r in range(2):
                    hold(eng, passed, s_tot, t + r - 1)
                    eng.tensor_copy(wts[:, r:r + 1, :], wtop[:, rows(t + r, 1), :]).then_inc(s_idx, 1)
                    eng.tensor_copy(idx[:, r:r + 1, :], slots[:, rows(t + r, 1), :]).then_inc(s_idx, 1)
                    hold(eng, passed, s_idx, 2 * (t + r + 1))
                    for k in range(TOPK):
                        eng.indirect_dma_start(
                            out=got[:, r, k], out_offset=None, in_=ye_d,
                            in_offset=bass.IndirectOffsetOnAxis(ap=idx[:, r, k:k + 1], axis=0),
                            bounds_check=SLOTS - 1, oob_is_err=False).then_inc(s_got[r], 16)

            each_tile(eng, body)

        @block.sync
        def _(eng):
            def body(t):
                for r in range(2):
                    hold(eng, passed, s_tot, t + r - 1)
                    eng.dma_start(rest[:, r], res_d[rows((t + r) * P, P), :]).then_inc(s_res[r], 16)
                for r in range(2):
                    hold(eng, passed, s_tot, t + r + 1)
                    eng.dma_start(out_t[rows((t + r) * P, P), :], total[:, r]).then_inc(s_out[r], 16)

            each_tile(eng, body)
            for r in range(2):
                eng.wait_ge(s_out[r], 16 * TT // 2)

        @block.vector
        def _(eng):
            def body(t0):
                for r in range(2):
                    t = t0 + r

                    def step(n, ins):
                        ins.then_inc(s_sum, 1)
                        ge(eng, s_sum, (STEPS - 1) * t + n)

                    b = 0
                    eng.wait_ge(s_got[r], t0 * (8 * TOPK) + 16 * TOPK)
                    eng.wait_ge(s_res[r], t0 * 8 + 16)
                    if not (isinstance(t0, int) and t0 == 0):
                        eng.wait_ge(s_out[r], t0 * 8)
                    step(1, eng.tensor_scalar(total[:, r], got[:, r, 0], wts[:, r, 0:1], None, ALU.mult))
                    for k in range(1, TOPK):
                        step(k + 1, eng.scalar_tensor_tensor(out=total[:, r], in0=got[:, r, k],
                                                             scalar=wts[:, r, k:k + 1], in1=total[:, r],
                                                             op0=ALU.mult, op1=ALU.add))
                    step(5, eng.tensor_tensor(total[:, r], total[:, r], gb_of(t0), ALU.mult))
                    eng.tensor_tensor(total[:, r], total[:, r], rest[:, r], ALU.add).then_inc(s_tot, 1)

            half = TT // 4
            gb_at = [0]

            def gb_of(t0):
                return gbt[:, gb_at[0]]

            body(0)
            with eng.Fori(1, half) as i:
                body(2 * i)
            gb_at[0] = 1
            with eng.Fori(half, 2 * half) as i:
                body(2 * i)


def kernel(L0_attn_query, L0_attn_key, L0_attn_value, L0_attn_Wqkv, L0_attn_Wproj, L0_attn_bproj,
           L0_ffn_Wr, L0_ffn_Wg, L0_ffn_Wu, L0_ffn_Wd, L0_ffn_Wsg, L0_ffn_Wsu, L0_ffn_Wsd, L0_ffn_Wse,
           L0_c, L0_wmod):
    import numpy as np
    import concourse.bacc as bacc
    from concourse.bass_utils import run_bass_kernel_spmd

    def tiles(w):
        w = np.asarray(w)
        return w.reshape(-1, P, w.shape[1]).transpose(1, 0, 2)

    wqkv = np.asarray(L0_attn_Wqkv).reshape(NH, 3, HN, D)
    qk = np.stack([np.concatenate([wqkv[2 * u, 0], wqkv[2 * u + 1, 0], wqkv[2 * u, 1], wqkv[2 * u + 1, 1]]).T
                   for u in range(NH // 2)])
    arrays = {
        "x": L0_attn_query,
        "wqk": qk.reshape(NH // 2, KT, P, P).transpose(0, 2, 1, 3),
        "wv": tiles(wqkv[:, 2].reshape(D, D).T),
        "wproj": tiles(np.asarray(L0_attn_Wproj).T),
        "bproj": np.asarray(L0_attn_bproj).reshape(1, D),
        "wr_se": tiles(np.concatenate([L0_ffn_Wr, L0_ffn_Wse], axis=1)),
        "c": np.asarray(L0_c).T.reshape(KT, P, B).transpose(1, 0, 2),
        "wmod": L0_wmod,
    }
    wsg = np.asarray(L0_ffn_Wsg).reshape(KT, P, FT, P).transpose(2, 1, 0, 3).reshape(FT, P, D)
    wsu = np.asarray(L0_ffn_Wsu).reshape(KT, P, FT, P).transpose(2, 1, 0, 3).reshape(FT, P, D)
    arrays["wsh"] = np.concatenate([wsg, wsu, np.asarray(L0_ffn_Wsd).reshape(FT, P, D)], axis=2)
    ep = E // 2
    g4 = [np.asarray(w).reshape(ep, 2, KT, P, F).transpose(0, 3, 1, 2, 4) for w in (L0_ffn_Wg, L0_ffn_Wu)]
    arrays["wgu"] = np.stack(g4, axis=2).reshape(ep, P, 2 * 2 * KT * F)
    wd = np.asarray(L0_ffn_Wd).reshape(ep, 2, F, D)
    arrays["wd_a"] = wd[:, :, :2 * P].reshape(ep, 2, 2, P, D).transpose(0, 3, 1, 2, 4).reshape(ep, P, 4 * D)
    arrays["wd_b"] = wd[:, :, 2 * P:].transpose(0, 2, 1, 3).reshape(ep, F - 2 * P, 2 * D)

    nc = bacc.Bacc("TRN2", target_bir_lowering=False, num_devices=1)
    given, aps = {}, {}
    for name, a in arrays.items():
        a = np.ascontiguousarray(a)
        given[f"in_{name}"] = a
        aps[name] = nc.dram_tensor(f"in_{name}", a.shape, mybir.dt.from_np(a.dtype), kind="ExternalInput").ap()
    aps["out"] = nc.dram_tensor("out_0", (B, S, D), F32, kind="ExternalOutput").ap()
    adaln_kernel(nc, **aps)
    r = run_bass_kernel_spmd(nc, [given], core_ids=[0])
    return r.results[0]["out_0"]
```

```python
from contextlib import ExitStack

import concourse.bass as bass
from concourse import mybir

ALU = mybir.AluOpType
ACT = mybir.ActivationFunctionType
AX = mybir.AxisListType
F32 = mybir.dt.float32
F32R = mybir.dt.float32r
BF16 = mybir.dt.bfloat16
U32 = mybir.dt.uint32
I32 = mybir.dt.int32

P = 128
B, S, D = 2, 1024, 512
T = B * S
KT = D // P
NH, HN = 16, 32
PAIRS = B * NH // 2
HALF = 512
TT = T // P
E, TOPK, F, CAP = 32, 4, 352, 64
FS = 1408
FT = FS // P
CH = T // HALF
SLOTS = E * CAP
EPS = 1e-5
F_TILES = [(0, 128), (128, 128), (256, 96)]


def ge(eng, sem, value):
    if isinstance(value, int) and value <= 0:
        return
    eng.wait_ge(sem, value)


def hold(eng, passed, sem, value):
    ge(eng, sem, value)
    if not isinstance(value, int):
        eng.sem_inc(passed, 1)


def adaln_kernel(nc, x, wqk, wv, wproj, bproj, wr_se, c, wmod, wsh, wgu, wd_a, wd_b, out):
    mod_rows = nc.dram_tensor("mod_rows", (4, B, D), F32).ap()
    gb_rows = nc.dram_tensor("gb_rows", (CH, D), F32).ap()
    inv_d = nc.dram_tensor("inv_d", (2, 2, S), F32).ap()
    ctx_t = nc.dram_tensor("ctx_t", (D, B, S), F32).ap()
    x1_d = nc.dram_tensor("x1_d", (T, D), F32).ap()
    res_d = nc.dram_tensor("res_d", (T, D), F32).ap()
    xe_d = nc.dram_tensor("xe_d", (SLOTS, D), F32).ap()
    ye_d = nc.dram_tensor("ye_d", (SLOTS, D), F32).ap()

    with ExitStack() as top:
        ident = top.enter_context(nc.sbuf_tensor("ident", [P, P], F32))
        wp_h = top.enter_context(nc.sbuf_tensor("wp_h", [P, KT, D], F32R))
        wp_l = top.enter_context(nc.sbuf_tensor("wp_l", [P, KT, D], F32R))
        prologue_and_attention(nc, x, wqk, wv, wproj, c, wmod, mod_rows, gb_rows, inv_d, ctx_t, xe_d,
                               ident, wp_h, wp_l)
        slots = top.enter_context(nc.sbuf_tensor("slots", [P, TT, TOPK], U32))
        wtop = top.enter_context(nc.sbuf_tensor("wtop", [P, TT, TOPK], F32))
        gbt = top.enter_context(nc.sbuf_tensor("gbt", [P, B, D], F32))
        with ExitStack() as mid:
            sgate = mid.enter_context(nc.sbuf_tensor("sgate", [P, TT], F32))
            h2h = mid.enter_context(nc.sbuf_tensor("h2h", [P, KT, T], F32R))
            h2l = mid.enter_context(nc.sbuf_tensor("h2l", [P, KT, T], F32R))
            first = {
                "w_raw": mid.enter_context(nc.sbuf_tensor("ws_raw", [P, 3, 3 * D], F32)),
                "h2": mid.enter_context(nc.sbuf_tensor("h2", [P, 2, 2, D], F32)),
                "slot_i": mid.enter_context(nc.sbuf_tensor("slot_i", [P, 2, 2, TOPK], U32)),
                "s_sc": [[mid.enter_context(nc.semaphore(f"scattered{q}{r}")) for r in range(2)]
                         for q in range(2)],
                "s_wl": [mid.enter_context(nc.semaphore(f"ws_loaded{n}")) for n in range(3)],
            }
            middle(nc, x, wp_h, wp_l, bproj, wr_se, mod_rows, ctx_t, x1_d, xe_d,
                   ident, slots, wtop, gbt, sgate, h2h, h2l, wsh, first)
            ffn(nc, first, wp_h, wsh, wgu, wd_a, wd_b, x1_d, res_d, xe_d, ye_d, gb_rows, ident, sgate, h2h, h2l,
                slots, wtop, gbt, out)


def prologue_and_attention(nc, x, wqk, wv, wproj, c, wmod, mod_rows, gb_rows, inv_d, ctx_t, xe_d,
                           ident, wp_h, wp_l):
    with ExitStack() as ctx:
        def sb(name, shape, dt=F32):
            return ctx.enter_context(nc.sbuf_tensor(name, shape, dt))

        hth = sb("hth", [P, KT, T], F32R)
        htl = sb("htl", [P, KT, T], F32R)
        v_all = sb("v_all", [P, TT, D])
        wqk_h = sb("wqk_h", [P, KT, P], F32R)
        wqk_l = sb("wqk_l", [P, KT, P], F32R)
        prologue(nc, x, wqk, wv, wproj, c, wmod, mod_rows, gb_rows, xe_d, ident, hth, htl, v_all,
                 wqk_h, wqk_l, wp_h, wp_l)
        attention(nc, wqk, inv_d, ctx_t, ident, hth, htl, v_all, wqk_h, wqk_l)


def prologue(nc, x, wqk, wv, wproj, c, wmod, mod_rows, gb_rows, xe_d, ident, hth, htl, v_all,
             wqk_h, wqk_l, wp_h, wp_l):
    GROUPS = T // HALF
    with ExitStack() as ctx:
        def sb(name, shape, dt=F32):
            return ctx.enter_context(nc.sbuf_tensor(name, shape, dt))

        def sem(name):
            return ctx.enter_context(nc.semaphore(name))

        c_sb = sb("c_sb", [P, KT, B])
        c_e = sb("c_e", [P, KT, B])
        c_silu = sb("c_silu", [P, KT, B])
        wm = sb("wm", [P, 2, 4 * D])
        rows = sb("rows", [P, 2, D])
        gate_s = sb("gate_s", [P, D])
        gate_a = sb("gate_a", [P, D])
        mod_t = sb("mod_t", [P, 2, KT, B])
        zero = sb("zero", [P, D])
        x_sb = sb("x_sb", [P, 4, D])
        xhat = sb("xhat", [P, 4, D])
        stats = sb("stats", [P, 4, 6])
        mv = sb("mv", [P, 4, 2])
        veps = sb("veps", [P, 4])
        rstd = sb("rstd", [P, 4])
        mhalf = sb("mhalf", [P, 4])
        hmod = sb("hmod", [P, KT, HALF])
        wv_raw = sb("wv_raw", [P, KT, D])
        wqk_raw = sb("wqk_raw", [P, KT, P])
        wv_h = sb("wv_h", [P, KT, D], F32R)
        wv_l = sb("wv_l", [P, KT, D], F32R)
        banks = [ctx.enter_context(nc.psum_tensor(f"pro_bank{n}", [P, HALF], F32)) for n in range(8)]
        ps_rest, ps_first, ps_modt, ps_v, ps_t = banks[0], banks[1], banks[2:4], banks[1:4], banks[4:8]
        NV = len(ps_v)

        s_c = sem("c_loaded")
        s_wm = [sem("wmod_loaded0"), sem("wmod_loaded1")]
        s_wv = sem("wv_loaded")
        s_wqk = sem("wqk_loaded")
        s_wp = sem("wproj_loaded0")
        s_wqs = sem("wqk_split")
        s_wps = sem("wproj_split0")
        s_x = [sem(f"x_loaded{n}") for n in range(4)]
        s_e = sem("c_exp_done")
        s_silu = sem("c_silu_step")
        s_modk = sem("mod_k_done")
        s_rows = sem("rows_step")
        s_modt = sem("mod_t_done")
        s_modc = sem("mod_cols_ready")
        s_rowst = sem("rows_stored")
        s_id = sem("ident_step")
        s_zero = sem("zero_ready")
        s_xe = sem("xe_zeroed")
        s_stat = sem("stats_step")
        s_rstd = sem("rstd_ready")
        s_xh = sem("xhat_ready")
        s_tr = sem("transposed")
        s_hm = sem("hmod_ready")
        s_hh = sem("hth_ready")
        s_hl = sem("htl_ready")
        s_wvs = sem("wv_split")
        s_vps = sem("v_product_done")
        s_vev = sem("v_copied")

        x_t = x.rearrange("b s d -> (b s) d").rearrange("(n p) d -> n p d", p=P)
        wm_t = wmod.rearrange("(k p) n -> k p n", p=P)
        passed = sem("waits_passed")
        block = ctx.enter_context(nc.Block())

        @block.sync
        def _(eng):
            eng.dma_start(c_sb[:], c).then_inc(s_c, 16)
            for k in range(KT):
                eng.dma_start(wm[:, k // 2, (k % 2) * 2 * D:(k % 2 + 1) * 2 * D], wm_t[k][:, 0:2 * D])\
                    .then_inc(s_wm[k // 2], 16)
                eng.dma_start(x_sb[:, k], x_t[k]).then_inc(s_x[k], 16)
            eng.dma_start(wv_raw[:], wv).then_inc(s_wv, 16)
            for t in range(4, TT):
                if t in (8, 12):
                    for k in (t // 4 - 2) * 2, (t // 4 - 2) * 2 + 1:
                        hold(eng, passed, s_modk, 2 * k + 2 if k < 2 else k + 3)
                        eng.dma_start(wm[:, k % 2], wm_t[k][:, 2 * D:6 * D]).then_inc(s_wm[k % 2], 16)
                hold(eng, passed, s_xh, t - 3)
                eng.dma_start(x_sb[:, t % 4], x_t[t]).then_inc(s_x[t % 4], 16)
                if t == 11:
                    eng.dma_start(wqk_raw[:], wqk[0]).then_inc(s_wqk, 16)
                if t == TT - 1:
                    eng.wait_ge(s_wvs, 2)
                    eng.dma_start(wv_raw[:], wproj).then_inc(s_wp, 16)
            eng.wait_ge(s_zero, 1)
            for n in range(SLOTS // P):
                eng.dma_start(xe_d[n * P:(n + 1) * P, :], zero[:]).then_inc(s_xe, 16)
            eng.wait_ge(s_rows, 7)
            for n in range(4):
                eng.dma_start(mod_rows[n], rows[32 * n:32 * n + B, 1, :]).then_inc(s_rowst, 16)
            gb_v = gb_rows.rearrange("(b r) d -> r b d", b=B)
            for n in range(CH // B):
                eng.dma_start(gb_v[n], rows[96:96 + B, 1, :]).then_inc(s_rowst, 16)
            hold(eng, passed, s_rowst, 16 * (4 + CH // B))
            hold(eng, passed, s_xe, 16 * (SLOTS // P))

        @block.gpsimd
        def _(eng):
            eng.memset(ident[:], 0.0).then_inc(s_id, 1)
            eng.memset(zero[:], 0.0).then_inc(s_zero, 1)
            eng.wait_ge(s_id, 1)
            eng.affine_select(out=ident[:], in_=ident[:], compare_op=ALU.not_equal, fill=1.0, base=0,
                              pattern=[[-1, P]], channel_multiplier=1).then_inc(s_id, 1)
            eng.memset(mhalf[:], -0.5).then_inc(s_id, 1)
            eng.wait_ge(s_id, 3)

            def rsqrt(g):
                hold(eng, passed, s_stat, 9 * (g + 1))
                eng.tensor_tensor(rstd[:], veps[:], mhalf[:], ALU.pow).then_inc(s_rstd, 1)

            def split(high, low, raw, landed, done):
                eng.wait_ge(landed, 16)
                eng.tensor_copy(high[:], raw[:]).then_inc(done, 1)
                eng.wait_ge(done, 1)
                eng.tensor_tensor(low[:], raw[:], high[:].bitcast(F32), ALU.subtract).then_inc(done, 1)

            rsqrt(0)
            eng.wait_ge(s_wv, 16)
            eng.tensor_copy(wv_h[:], wv_raw[:]).then_inc(s_wvs, 1)
            rsqrt(1)
            rsqrt(2)
            split(wqk_h, wqk_l, wqk_raw, s_wqk, s_wqs)
            rsqrt(3)
            split(wp_h, wp_l, wv_raw, s_wp, s_wps)

        @block.tensor
        def _(eng):
            def modulation(bank, count, buffer, counts, tiles):
                for k in tiles:
                    eng.wait_ge(s_wm[buffer(k)[0]], counts[k])
                    for n in range(count):
                        at = buffer(k)[1] + n * D
                        mm = eng.matmul(bank[32 * n:32 * n + B, :], c_silu[:, k, :],
                                        wm[:, buffer(k)[0], at:at + D], start=(k == 0), stop=(k == KT - 1))
                    mm.then_inc(s_modk, 1)

            eng.wait_ge(s_silu, 3)
            modulation(ps_first, 2, lambda k: (k // 2, (k % 2) * 2 * D), (32, 32, 32, 32), range(KT))
            eng.wait_ge(s_rows, 1)
            eng.wait_ge(s_id, 2)
            for s in range(2):
                for k in range(KT):
                    mm = eng.transpose(ps_modt[s][:, k * B:(k + 1) * B],
                                       rows[32 * s:32 * s + B, 0, k * P:(k + 1) * P],
                                       ident[32 * s:32 * s + B, 32 * s:32 * s + B])
            mm.then_inc(s_modt, 1)

            def transposes(g):
                for n in range(4):
                    eng.wait_ge(s_xh, 4 * g + n + 1)
                    for k in range(KT):
                        if n == 0 and g >= 1:
                            eng.wait_ge(s_hh, KT * (g - 1) + k + 1)
                        mm = eng.transpose(ps_t[k][:, n * P:(n + 1) * P],
                                           xhat[:, n, k * P:(k + 1) * P], ident[:])
                    mm.then_inc(s_tr, 1)

            def values(g):
                for n in range(4):
                    t = 4 * g + n
                    if t == 0:
                        eng.wait_ge(s_wvs, 2)
                        eng.wait_ge(s_modc, 2)
                    ge(eng, s_vev, t - NV + 1)
                    for k in range(KT):
                        if n == 0:
                            eng.wait_ge(s_hh, KT * g + k + 1)
                            eng.wait_ge(s_hl, KT * g + k + 1)
                        for m, (a, w) in enumerate(((hth, wv_h), (hth, wv_l), (htl, wv_h))):
                            mm = eng.matmul(ps_v[t % NV][:], a[:, k, t * P:(t + 1) * P], w[:, k, :],
                                            start=(k == 0 and m == 0), stop=(k == KT - 1 and m == 2))
                    mm.then_inc(s_vps, 1)

            transposes(0)
            for g in range(GROUPS):
                if g + 1 < GROUPS:
                    transposes(g + 1)
                values(g)
                if g < 2:
                    modulation(ps_rest, 4, lambda k: (k % 2, 0), (48, 48, 64, 64), (2 * g, 2 * g + 1))

        @block.scalar
        def _(eng):
            eng.wait_ge(s_c, 16)
            eng.activation(c_e[:], c_sb[:], ACT.Exp, scale=-1.0).then_inc(s_e, 1)
            eng.wait_ge(s_modc, 2)

            def copy_values(t):
                eng.wait_ge(s_vps, t + 1)
                eng.activation(v_all[:, t], ps_v[t % NV][:], ACT.Copy).then_inc(s_vev, 1)

            for g in range(GROUPS):
                b = g // (GROUPS // B)
                for k in range(KT):
                    n = KT * g + k
                    scale, bias = (mod_t[:, m, k, b:b + 1] for m in (1, 0))
                    eng.wait_ge(s_tr, 4 * (g + 1))
                    ge(eng, s_hl, n - KT + 1)
                    eng.activation(hmod[:, k], ps_t[k][:], ACT.Identity, bias=bias, scale=scale)\
                        .then_inc(s_hm, 1)
                    eng.activation(hth[:, k, g * HALF:(g + 1) * HALF], ps_t[k][:], ACT.Identity,
                                   bias=bias, scale=scale).then_inc(s_hh, 1)
                    if g >= 1:
                        copy_values(4 * (g - 1) + k)
            for t in range(TT - 4, TT):
                copy_values(t)

        @block.vector
        def _(eng):
            eng.wait_ge(s_e, 1)
            eng.tensor_scalar(c_e[:], c_e[:], 1.0, None, ALU.add).then_inc(s_silu, 1)
            eng.wait_ge(s_silu, 1)
            eng.reciprocal(c_e[:], c_e[:]).then_inc(s_silu, 1)
            eng.wait_ge(s_silu, 2)
            eng.tensor_tensor(c_silu[:], c_sb[:], c_e[:], ALU.mult).then_inc(s_silu, 1)

            def layer_norm(g, between=None):
                ge(eng, s_xh, 4 * g)
                for n in range(4):
                    eng.wait_ge(s_x[n], 16 * (g + 1))
                    eng.bn_stats(stats[:, n], x_sb[:, n]).then_inc(s_stat, 1)
                    eng.wait_ge(s_stat, 9 * g + 2 * n + 1)
                    eng.bn_aggr(mv[:, n], stats[:, n]).then_inc(s_stat, 1)
                    eng.wait_ge(s_stat, 9 * g + 2 * n + 2)
                eng.tensor_scalar(veps[:], mv[:, :, 1], EPS, None, ALU.add).then_inc(s_stat, 1)
                if between:
                    between()
                eng.wait_ge(s_rstd, g + 1)
                for n in range(4):
                    if g >= 1:
                        eng.wait_ge(s_tr, 4 * (g - 1) + n + 1)
                    eng.tensor_scalar(xhat[:, n], x_sb[:, n], mv[:, n, 0:1], rstd[:, n:n + 1],
                                      ALU.subtract, ALU.mult).then_inc(s_xh, 1)

            def rows_out():
                eng.wait_ge(s_modk, 2 * KT)
                for n in range(4):
                    cp = eng.tensor_copy(rows[32 * n:32 * n + B, 1, :], ps_rest[32 * n:32 * n + B, :])
                cp.then_inc(s_rows, 1)
                eng.wait_ge(s_rows, 2)
                for q in (0, 96):
                    gate = rows[q:q + B, 1]
                    eng.tensor_scalar(gate_s[q:q + B], gate, 0.0, 2.0, ALU.is_ge, ALU.mult)
                    eng.scalar_tensor_tensor(out=gate_a[q:q + B], in0=gate, scalar=-1.0,
                                             in1=gate, op0=ALU.mult, op1=ALU.max).then_inc(s_rows, 1)
                eng.wait_ge(s_rows, 4)
                for q in (0, 96):
                    eng.tensor_scalar(gate_a[q:q + B], gate_a[q:q + B], 0.25, None, ALU.max)\
                        .then_inc(s_rows, 1)
                eng.wait_ge(s_rows, 6)
                for q in (0, 96):
                    st = eng.scalar_tensor_tensor(out=rows[q:q + B, 1], in0=gate_s[q:q + B], scalar=-1.0,
                                                  in1=gate_a[q:q + B], op0=ALU.add, op1=ALU.mult)
                st.then_inc(s_rows, 1)

            def low_wv():
                eng.wait_ge(s_wvs, 1)
                eng.tensor_tensor(wv_l[:], wv_raw[:], wv_h[:].bitcast(F32), ALU.subtract).then_inc(s_wvs, 1)

            layer_norm(0)
            eng.wait_ge(s_modk, KT)
            for s in range(2):
                cp = eng.tensor_copy(rows[32 * s:32 * s + B, 0, :], ps_first[32 * s:32 * s + B, :])
            cp.then_inc(s_rows, 1)
            eng.wait_ge(s_modt, 1)
            eng.tensor_copy(mod_t[:, 0].rearrange("p k b -> p (k b)"), ps_modt[0][:, 0:KT * B])\
                .then_inc(s_modc, 1)
            eng.tensor_scalar(mod_t[:, 1].rearrange("p k b -> p (k b)"), ps_modt[1][:, 0:KT * B],
                              1.0, None, ALU.add).then_inc(s_modc, 1)

            for g in range(GROUPS):
                if g + 1 < GROUPS:
                    layer_norm(g + 1, low_wv if g == 0 else None)
                for k in range(KT):
                    n = KT * g + k
                    eng.wait_ge(s_hh, n + 1)
                    eng.tensor_tensor(htl[:, k, g * HALF:(g + 1) * HALF], hmod[:, k],
                                      hth[:, k, g * HALF:(g + 1) * HALF].bitcast(F32), ALU.subtract)\
                        .then_inc(s_hl, 1)
                if g == 2:
                    rows_out()


def attention(nc, wqk, inv_d, ctx_t, ident, hth, htl, v_all, wqk_h, wqk_l):
    NI = PAIRS // 2
    SCALE = float(HN) ** -0.5
    QT = S // P
    CC = S // HALF
    STACK = 3 * HN
    UNITS = [(hd, qt) for qt in range(QT) for hd in range(2)]
    PER_STEP = [0, 0, 2, 3, 3, 3, 3, 2]
    MOVES, MOVES_H = 7, 5
    with ExitStack() as ctx:
        def sb(name, shape, dt=F32):
            return ctx.enter_context(nc.sbuf_tensor(name, shape, dt))

        def sem(name):
            return ctx.enter_context(nc.semaphore(name))

        stack = sb("stack", [STACK + 2, 2, 4, S], F32R)
        part_h = sb("part_h", [P, S], F32R)
        part_l = sb("part_l", [P, S], F32R)
        w_raw = sb("w_raw", [P, KT, P])
        probs = sb("probs", [P, 2, 2, S])
        v_one = sb("v_one", [P, 2, QT, 2, 2, HN])
        mx = sb("mx", [P, 2 * QT, CC])
        nmax = sb("nmax", [P, 2 * QT])
        mcat = sb("mcat", [P, 2, 2 * QT])
        mrow = sb("mrow", [4 * QT, P])
        o_sb = sb("o_sb", [P, S])
        srec = sb("srec", [P, 2, S // P])
        rsum = sb("rsum", [P, S])
        cnorm = sb("cnorm", [P, S])
        ps_s = [ctx.enter_context(nc.psum_tensor(f"ps_s{n}", [P, HALF], F32)) for n in range(2)]
        ps_t = [ctx.enter_context(nc.psum_tensor(f"ps_t{n}", [P, S], F32)) for n in range(2)]
        ps_o = ctx.enter_context(nc.psum_tensor("ps_o", [P, S], F32))

        s_init = sem("constants_ready")
        s_wl = sem("w_loaded")
        s_ws = sem("w_split")
        s_wh = sem("w_high_part")
        s_proj = sem("proj_done")
        s_ph = sem("part_h_ready")
        s_pl = sem("part_l_ready")
        s_stk = sem("stack_loaded")
        s_stkh = sem("stack_first_third_loaded")
        s_sc = sem("scores_ready")
        s_mxd = sem("max_done")
        s_mch = sem("mcat_step")
        s_mt = sem("mrow_transposed")
        s_mc = sem("mrow_copied")
        s_mr = sem("mrow_loaded")
        s_st = sem("scores_t_ready")
        s_ex = sem("exp_done")
        s_pv = sem("pv_done")
        s_vo = sem("v_copied_pair")
        s_oc = sem("context_copied")
        s_sr = sem("sums_spread")
        s_rs = sem("sums_inverted")
        s_iv = sem("inverses_stored")
        s_rb = sem("inverses_loaded")
        s_cn = sem("ctx_normed")
        s_cst = sem("ctx_stored")

        passed = sem("waits_passed")
        block = ctx.enter_context(nc.Block())

        def each_pair(eng, body):
            for r in range(2):
                body(0, r)
            with eng.Fori(1, NI - 2) as i:
                for r in range(2):
                    body(i, r)
            for i in range(NI - 2, NI):
                for r in range(2):
                    body(i, r)

        def exists(i):
            return not isinstance(i, int) or i < NI

        def move_part(eng, part, r, j, n, done):
            eng.dma_start(stack[HN * n:HN * (n + 1), r, j, :].bitcast(F32),
                          part[HN * j:HN * (j + 1), :].bitcast(F32)).then_inc(done, 16)

        @block.sync
        def _(eng):
            def load_w(i):
                hold(eng, passed, s_ws, i - 1)
                src = wqk[i] if isinstance(i, int) else wqk[bass.ds(i, 1)].rearrange("o p k n -> (o p) k n")
                eng.dma_start(w_raw[:], src).then_inc(s_wl, 16)

            def move_stack(u, r):
                hold(eng, passed, s_ph, CC * (u + 1))
                hold(eng, passed, s_pl, CC * (u + 1))
                hold(eng, passed, s_st, 2 * QT * (u - 1))
                for j in range(4):
                    for n, part in enumerate((part_l, part_h) if j < 2 else (part_h, part_l)):
                        if (j, n) != (3, 0):
                            move_part(eng, part, r, j, n + 1, s_stk)

            def move_mrow(u, r):
                hold(eng, passed, s_mc, u + 1)
                for n in range(2):
                    eng.dma_start(stack[STACK + n:STACK + n + 1, r, 0:2, :]
                                  .rearrange("o j s -> o (j s)").bitcast(F32),
                                  mrow[2 * QT * n:2 * QT * (n + 1), :]).then_inc(s_mr, 16)

            def store_ctx(i, r):
                hold(eng, passed, s_cn, 4 * i + (2 * r + 2))
                row = HN * (NI * r + i) if isinstance(i, int) else HN * i + HN * NI * r
                rows = slice(row, row + HN) if isinstance(i, int) else bass.ds(row, HN)
                for b in range(2):
                    eng.dma_start(ctx_t[rows, b, :], cnorm[64 * b:64 * b + HN, :]).then_inc(s_cst, 16)

            load_w(1)
            move_stack(0, 0)
            move_stack(1, 1)
            move_mrow(0, 0)

            def body(i, r):
                u = 2 * i + r
                if r == 0 and exists(i + 2):
                    load_w(i + 2)
                if exists(i + r):
                    move_mrow(u + 1, 1 - r)
                if exists(i + 1):
                    move_stack(u + 2, r)
                store_ctx(i, r)

            each_pair(eng, body)
            hold(eng, passed, s_cst, 32 * PAIRS)

        @block.gpsimd
        def _(eng):
            eng.memset(stack[STACK:STACK + 2, :, 2:4].bitcast(F32), 1.0).then_inc(s_init, 1)
            eng.wait_ge(s_init, 2)

            def split_w(i):
                hold(eng, passed, s_wl, 16 * i)
                hold(eng, passed, s_proj, 2 * CC * i)
                eng.tensor_copy(wqk_h[:], w_raw[:]).then_inc(s_wh, 1)
                hold(eng, passed, s_wh, i)
                eng.tensor_tensor(wqk_l[:], w_raw[:], wqk_h[:].bitcast(F32), ALU.subtract)\
                    .then_inc(s_ws, 1)

            def copy_v(i, r):
                hold(eng, passed, s_pv, QT * (2 * i + (r - 1)))
                head = i * (2 * HN)
                cols = slice(head, head + 2 * HN) if isinstance(head, int) else bass.ds(head, 2 * HN)
                src = v_all[:, QT * r:QT * (r + 1), cols]
                eng.tensor_copy(v_one[:, r, :, :, 0, :], src.rearrange("p t (a d) -> p t a d", a=2))\
                    .then_inc(s_vo, 1)

            def move_high(u, r):
                hold(eng, passed, s_ph, CC * (u + 1))
                hold(eng, passed, s_st, 2 * QT * (u - 1))
                for j in range(4):
                    move_part(eng, part_h, r, j, 0, s_stkh)
                move_part(eng, part_h, r, 3, 1, s_stkh)

            for r in range(2):
                copy_v(0, r)
            move_high(0, 0)
            move_high(1, 1)
            split_w(1)

            def spread_sums(u):
                hold(eng, passed, s_oc, u + 1)
                for hd in range(2):
                    eng.dma_start(srec[:, hd, :], o_sb[64 * hd + HN:64 * hd + HN + 1, :]).then_inc(s_sr, 16)

            def norm(u, r):
                hold(eng, passed, s_rs, u + 1)
                eng.dma_start(inv_d[r].rearrange("h (p j) -> p h j", p=P), srec[:]).then_inc(s_iv, 16)
                hold(eng, passed, s_iv, 16 * (u + 1))
                for hd in range(2):
                    eng.dma_start(rsum[64 * hd:64 * hd + HN, :], inv_d[r, hd:hd + 1, :].to_broadcast([HN, S]))\
                        .then_inc(s_rb, 16)
                hold(eng, passed, s_rb, 32 * (u + 1))
                hold(eng, passed, s_cst, 32 * u)
                for hd in range(2):
                    q = 64 * hd
                    hold(eng, passed, s_cn, 2 * u + hd)
                    eng.tensor_tensor(cnorm[q:q + HN], o_sb[q:q + HN], rsum[q:q + HN], ALU.mult)\
                        .then_inc(s_cn, 1)
                hold(eng, passed, s_cn, 2 * (u + 1))

            def body(i, r):
                u = 2 * i + r
                if not (isinstance(i, int) and i + r == 0):
                    norm(u - 1, 1 - r)
                if r == 1 and exists(i + 2):
                    split_w(i + 2)
                if exists(i + 1):
                    move_high(u + 2, r)
                if exists(i + r):
                    spread_sums(u)
                if exists(i + 1):
                    copy_v(i + 1, r)

            each_pair(eng, body)

        @block.tensor
        def _(eng):
            def proj(i, r):
                u = 2 * i + r
                ge(eng, s_ws, i)
                for cc in (1, 0):
                    if isinstance(u, int) and u < 2:
                        ge(eng, s_ph, CC * u)
                        ge(eng, s_pl, CC * u)
                    else:
                        ge(eng, s_mxd, 4 * QT * (u - 1))
                        if cc == 0:
                            ge(eng, s_mc, u - 1)
                    at = r * S + cc * HALF
                    for k in range(KT):
                        for m, (w, a) in enumerate(((wqk_h, hth), (wqk_l, hth), (wqk_h, htl))):
                            mm = eng.matmul(ps_s[cc][:], w[:, k, :], a[:, k, at:at + HALF],
                                            start=(k == 0 and m == 0), stop=(k == KT - 1 and m == 2))
                    mm.then_inc(s_proj, 1)

            def score(u, r, m):
                n, cc = m // CC, m % CC
                hd, qt = UNITS[n]
                if m == 0:
                    ge(eng, s_stk, 16 * MOVES * (u + 1))
                    ge(eng, s_stkh, 16 * MOVES_H * (u + 1))
                    ge(eng, s_mc, u)
                if n == 0:
                    ready = CC * (u + 2) if not isinstance(u, int) else CC * min(u + 2, PAIRS)
                    ge(eng, s_ph, ready)
                    ge(eng, s_pl, ready)
                else:
                    ge(eng, s_mxd, 4 * QT * u + m - 1)
                eng.matmul(ps_s[cc][:], stack[0:STACK, r, hd, qt * P:(qt + 1) * P],
                           stack[0:STACK, r, 2 + hd, cc * HALF:(cc + 1) * HALF],
                           start=True, stop=True).then_inc(s_sc, 1)

            def max_rows(u):
                ge(eng, s_mch, 3 * (u + 1))
                eng.transpose(ps_s[0][0:4 * QT, 0:P], mcat[:].rearrange("p a n -> p (a n)"), ident[:])\
                    .then_inc(s_mt, 1)

            def scores_t(u, r, kt, hd):
                if kt == 0 and hd == 0:
                    ge(eng, s_mr, 32 * (u + 1))
                ge(eng, s_ex, 2 * QT * u + 2 * kt + hd - 1)
                for cc in range(CC):
                    mm = eng.matmul(ps_t[hd][:, cc * HALF:(cc + 1) * HALF],
                                    stack[:, r, 2 + hd, kt * P:(kt + 1) * P],
                                    stack[:, r, hd, cc * HALF:(cc + 1) * HALF], start=True, stop=True)
                mm.then_inc(s_st, 1)

            def weighted(u, r, kt, quarter):
                if quarter == 0:
                    ge(eng, s_ex, 2 * QT * u + 2 * kt + 2)
                    if kt == 0:
                        ge(eng, s_vo, u + 1)
                        ge(eng, s_oc, u)
                if kt == 0:
                    if quarter % 2:
                        return
                    cols = slice(quarter * (S // 4), (quarter + 2) * (S // 4))
                else:
                    cols = slice(quarter * (S // 4), (quarter + 1) * (S // 4))
                for hd in range(2):
                    mm = eng.matmul(ps_o[64 * hd:64 * hd + 64, cols],
                                    v_one[:, r, kt, hd].rearrange("p a d -> p (a d)"),
                                    probs[:, kt % 2, hd, cols], start=(kt == 0),
                                    stop=(kt == QT - 1 and quarter % 2 == 1))
                if quarter == (3 if kt else 2):
                    mm.then_inc(s_pv, 1)

            proj(0, 0)
            proj(0, 1)
            for m in range(4 * QT):
                score(0, 0, m)
            max_rows(0)
            proj(1, 0)
            eng.wait_ge(s_init, 2)

            def body(i, r):
                u = 2 * i + r
                more = exists(i + r)
                m = 0
                for kt in range(QT):
                    for half in range(2):
                        count = PER_STEP[kt] if more else 0
                        if kt < 2:
                            scores_t(u, r, kt, half)
                        if kt == 0 and (not isinstance(u, int) or 0 < u <= PAIRS - 3):
                            for quarter in (2 * half, 2 * half + 1):
                                weighted(u - 1, 1 - r, QT - 1, quarter)
                        if half == 0:
                            values = [(kt - 2, 2), (kt - 2, 3)] if kt >= 2 else []
                        else:
                            values = [(kt - 1, 0), (kt - 1, 1)] if kt >= 1 else []
                        for k in range(max(count, 2)):
                            if k < count:
                                score(u + 1, 1 - r, m + k)
                            if k < len(values):
                                weighted(u, r, *values[k])
                        if kt >= 2:
                            scores_t(u, r, kt, half)
                        m += count
                weighted(u, r, QT - 2, 2)
                weighted(u, r, QT - 2, 3)
                if more:
                    max_rows(u + 1)
                if exists(i + 1 + r):
                    proj(i + 1 + r, 1 - r)
                else:
                    for quarter in range(4):
                        weighted(u, r, QT - 1, quarter)

            each_pair(eng, body)

        @block.scalar
        def _(eng):
            def high_part(u):
                for n, cc in enumerate((1, 0)):
                    ge(eng, s_proj, CC * u + n + 1)
                    if n == 0:
                        ge(eng, s_stk, 16 * MOVES * u)
                        ge(eng, s_stkh, 16 * MOVES_H * u)
                    eng.activation(part_h[:, cc * HALF:(cc + 1) * HALF], ps_s[cc][:], ACT.Copy)\
                        .then_inc(s_ph, 1)

            def body(i, r):
                u = 2 * i + r
                for kt in range(QT):
                    for hd in range(2):
                        ge(eng, s_st, 2 * QT * u + 2 * kt + hd + 1)
                        ge(eng, s_pv, QT * u + kt - 1)
                        eng.activation(probs[:, kt % 2, hd, :], ps_t[hd][:], ACT.Exp, scale=SCALE)\
                            .then_inc(s_ex, 1)
                    if kt == 0 and exists(i + 1):
                        high_part(u + 2)

            high_part(0)
            high_part(1)
            each_pair(eng, body)

        @block.vector
        def _(eng):
            def low_part(u):
                for n, cc in enumerate((1, 0)):
                    ge(eng, s_ph, CC * u + n + 1)
                    if n == 0:
                        ge(eng, s_stk, 16 * MOVES * u)
                    eng.tensor_tensor(part_l[:, cc * HALF:(cc + 1) * HALF], ps_s[cc][:],
                                      part_h[:, cc * HALF:(cc + 1) * HALF].bitcast(F32), ALU.subtract)\
                        .then_inc(s_pl, 1)

            def maxima(u):
                for n, (hd, qt) in enumerate(UNITS):
                    if n == 4 and not (isinstance(u, int) and u < 2):
                        inverse(u - 2)
                    for cc in range(CC):
                        ge(eng, s_sc, 4 * QT * u + 2 * n + cc + 1)
                        if n == 0 and cc == 0:
                            ge(eng, s_mch, 3 * u)
                        at = hd * QT + qt
                        eng.tensor_reduce(mx[:, at, cc:cc + 1], ps_s[cc][:], AX.X, ALU.max)\
                            .then_inc(s_mxd, 1)
                ge(eng, s_mxd, 4 * QT * (u + 1))
                eng.tensor_reduce(nmax[:], mx[:], AX.X, ALU.max, negate=True).then_inc(s_mch, 1)
                ge(eng, s_mch, 3 * u + 1)
                ge(eng, s_mt, u)
                eng.tensor_copy(mcat[:, 0].bitcast(F32R), nmax[:]).then_inc(s_mch, 1)
                ge(eng, s_mch, 3 * u + 2)
                eng.tensor_tensor(mcat[:, 1].bitcast(F32R), nmax[:], mcat[:, 0], ALU.subtract)\
                    .then_inc(s_mch, 1)
                ge(eng, s_mt, u + 1)
                ge(eng, s_mr, 32 * u)
                eng.tensor_copy(mrow[:], ps_s[0][0:4 * QT, 0:P]).then_inc(s_mc, 1)

            def inverse(u):
                ge(eng, s_sr, 32 * (u + 1))
                eng.reciprocal(srec[:], srec[:]).then_inc(s_rs, 1)

            eng.memset(v_one[:, :, :, :, 1, :], 1.0).then_inc(s_init, 1)
            low_part(0)
            low_part(1)
            maxima(0)

            def body(i, r):
                u = 2 * i + r
                if exists(i + 1):
                    low_part(u + 2)
                if exists(i + r):
                    maxima(u + 1)
                else:
                    inverse(u - 1)
                ge(eng, s_pv, QT * (u + 1))
                ge(eng, s_cn, 2 * u)
                if exists(i + r):
                    eng.tensor_copy(o_sb[:], ps_o[:]).then_inc(s_oc, 1)

            each_pair(eng, body)
            ge(eng, s_cst, 32 * (PAIRS - 1))
            for cc in range(CC):
                cols = slice(cc * HALF, (cc + 1) * HALF)
                eng.reciprocal(rsum[:, cols], ps_o[:, cols]).then_inc(s_rs, 1)
                ge(eng, s_rs, PAIRS + cc)
                for hd in range(2):
                    q = 64 * hd
                    mul = eng.tensor_tensor(cnorm[q:q + HN, cols], ps_o[q:q + HN, cols],
                                            rsum[q + HN:q + 2 * HN, cols], ALU.mult)
                    if cc == CC - 1:
                        mul.then_inc(s_cn, 1)


def send_rows(eng, xe_d, first, q, r):
    for k in range(TOPK):
        index = bass.IndirectOffsetOnAxis(ap=first["slot_i"][:, q, r, k:k + 1], axis=0)
        eng.indirect_dma_start(out=xe_d, out_offset=index, in_=first["h2"][:, q, r], in_offset=None,
                               bounds_check=SLOTS - 1, oob_is_err=False).then_inc(first["s_sc"][q][r], 16)


def middle(nc, x, wp_h, wp_l, bproj, wr_se, mod_rows, ctx_t, x1_d, xe_d,
           ident, slots, wtop, gbt, sgate, h2h, h2l, wsh, first):
    PR = TT // 2
    with ExitStack() as ctx:
        def sb(name, shape, dt=F32):
            return ctx.enter_context(nc.sbuf_tensor(name, shape, dt))

        def sem(name):
            return ctx.enter_context(nc.semaphore(name))

        bp_raw = sb("bp_raw", [1, D])
        bp_h = sb("bp_h", [1, D], F32R)
        bp_l = sb("bp_l", [1, D], F32R)
        one_row = sb("one_row", [1, P], F32R)
        wrse = sb("wrse", [P, KT, E + 1])
        ga_t = sb("ga_t", [P, B, D])
        cb_t = sb("cb_t", [P, B, D])
        sb_t = sb("sb_t", [P, B, D])
        iota_e = sb("iota_e", [P, 2, TOPK, E])
        slot_a = sb("slot_a", [P, 2, E])
        slot_b = sb("slot_b", [P, 2, E])
        lower = sb("lower", [P, P], BF16)
        ones = sb("ones", [P, P], BF16)
        seen = sb("seen", [P, E], BF16)
        ct = sb("ct", [P, 2, KT, P])
        ct_h = sb("ct_h", [P, 2, KT, P], F32R)
        ct_l = sb("ct_l", [P, 2, KT, P], F32R)
        xt = sb("xt", [P, 2, D])
        x1 = sb("x1", [P, 2, D])
        xhat = sb("xhat2", [P, 2, D])
        h2, slot_i = first["h2"], first["slot_i"]
        h2t = sb("h2t", [P, 2, KT, P])
        stats = sb("stats2", [P, 2, 6])
        mv = sb("mv2", [P, 2, 2])
        veps = sb("veps2", [P, 2])
        rstd = sb("rstd2", [P, 2])
        mhalf = sb("mhalf2", [P, 2])
        nmax = sb("nmax2", [P, 2])
        esum = sb("esum", [P, 2])
        ex = sb("ex", [P, 2, E])
        ese = sb("ese", [P, 2])
        prb = sb("prb", [P, 2, E])
        top8 = sb("top8", [P, 2, 8])
        idx8 = sb("idx8", [P, 2, 8], U32)
        idxf = sb("idxf", [P, 2, TOPK])
        onehot = sb("onehot", [P, 2, TOPK, E])
        mask = sb("mask", [P, 2, E], BF16)
        wsum = sb("wsum", [P, 2])
        wnorm = sb("wnorm", [P, 2, TOPK])
        over = sb("over", [P, 2, E])
        slotv = sb("slotv", [P, 2, E])
        pick = sb("pick", [P, 2, TOPK, E])
        slotf = sb("slotf", [P, 2, TOPK])
        ps_y = [ctx.enter_context(nc.psum_tensor(f"ps_y{n}", [P, D], F32)) for n in range(2)]
        ps_h = [ctx.enter_context(nc.psum_tensor(f"ps_h{n}", [P, D], F32)) for n in range(2)]
        ps_r = ctx.enter_context(nc.psum_tensor("ps_r", [P, 2, D // 2], F32))
        ps_p = ctx.enter_context(nc.psum_tensor("ps_p", [P, 2, D // 2], F32))

        s_bp = sem("bproj_loaded")
        s_tb = sem("first_tables_loaded")
        s_tb1 = sem("second_tables_loaded")
        s_bps = sem("bproj_split")
        s_tab = sem("tables_ready")
        s_cst = sem("mid_constants")
        s_ct = [sem("ctx_loaded0"), sem("ctx_loaded1")]
        s_xt = [sem("x_in0"), sem("x_in1")]
        s_cth = sem("ctx_high")
        s_ctl = sem("ctx_low")
        s_py = sem("projected")
        s_x1a = sem("gated")
        s_x1 = sem("x1_ready")
        s_x1s = [sem("x1_stored0"), sem("x1_stored1")]
        s_st = sem("stats2_step")
        s_rstd = sem("rstd2_ready")
        s_xh = sem("xhat2_ready")
        s_h2 = sem("h2_ready")
        s_tr = sem("h2_transposed")
        s_h2t = sem("h2t_ready")
        s_h2h = sem("h2h_ready")
        s_h2l = sem("h2l_ready")
        s_lg = sem("logits_ready")
        s_nm = sem("nmax_ready")
        s_ex = sem("router_exp")
        s_rt = sem("routing_step")
        s_mk = sem("mask_ready")
        s_pos = sem("positions_ready")
        s_sl = sem("slots_ready")
        s_sc = first["s_sc"]

        x_t = x.rearrange("b s d -> (b s) d")
        ctx_v = ctx_t.rearrange("(k p) b s -> p k (b s)", p=P)

        def at(n, size):
            return slice(n, n + size) if isinstance(n, int) else bass.ds(n, size)

        def table(a, b):
            return a[:, b] if isinstance(b, int) else a[:, bass.ds(b, 1), :].rearrange("p o d -> p (o d)")

        def each_pair(eng, body):
            for i in range(2):
                body(i, i, 0)
            with eng.Fori(1, PR // 2 - 1) as j:
                body(2 * j, 0, j - 1)
                body(2 * j + 1, 1, 1)
            for i in range(PR - 2, PR):
                body(i, i % 2, 1)

        def exists(i):
            return not isinstance(i, int) or i < PR

        passed = sem("waits_passed")
        block = ctx.enter_context(nc.Block())

        @block.sync
        def _(eng):
            def load_ct(i):
                for r in range(2):
                    hold(eng, passed, s_ctl, 2 * i + (r - 1))
                    eng.dma_start(ct[:, r], ctx_v[:, :, at((2 * i + r) * P, P)]).then_inc(s_ct[r], 16)

            def load_xt(i, r):
                hold(eng, passed, s_x1, 2 * i + (r - 1))
                eng.dma_start(xt[:, r], x_t[at((2 * i + r) * P, P), :]).then_inc(s_xt[r], 16)

            def store_x1(i, r):
                hold(eng, passed, s_x1, 2 * i + (r + 1))
                eng.dma_start(x1_d[at((2 * i + r) * P, P), :], x1[:, r]).then_inc(s_x1s[r], 16)

            def load_tables(b):
                for src, dst in ((mod_rows[0], ga_t), (mod_rows[2], cb_t), (mod_rows[1], sb_t)):
                    eng.dma_start(dst[:, b], src[b:b + 1, :].to_broadcast([P, D]))\
                        .then_inc((s_tb, s_tb1)[b], 16)

            load_ct(0)
            eng.dma_start(bp_raw[:], bproj).then_inc(s_bp, 16)
            for r in range(2):
                load_xt(0, r)
            load_tables(0)
            eng.dma_start(wrse[:], wr_se).then_inc(s_tb, 16)
            load_ct(1)
            for r in range(2):
                store_x1(0, r)
                load_xt(1, r)

            def body(i, q, b):
                if exists(i + 2):
                    load_ct(i + 2)
                if exists(i + 1):
                    for r in range(2):
                        store_x1(i + 1, r)
                        if exists(i + 2):
                            load_xt(i + 2, r)
                if isinstance(i, int) and i == 0:
                    load_tables(1)
                    for b in range(B):
                        eng.dma_start(gbt[:, b], mod_rows[3][b:b + 1, :].to_broadcast([P, D]))\
                            .then_inc(s_tb1, 16)
                if isinstance(i, int) and i < 2:
                    eng.dma_start(first["w_raw"][:, i], wsh[i]).then_inc(first["s_wl"][i], 16)

            each_pair(eng, body)
            for r in range(2):
                eng.wait_ge(s_x1s[r], 16 * PR)
            eng.wait_ge(s_tb1, 16 * (3 + B))

        @block.gpsimd
        def _(eng):
            eng.memset(mhalf[:], -0.5).then_inc(s_cst, 1)
            eng.memset(lower[:], 1.0).then_inc(s_cst, 1)
            eng.memset(ones[:], 1.0).then_inc(s_cst, 1)
            eng.memset(seen[:], 0.0).then_inc(s_cst, 1)
            eng.wait_ge(s_cst, 2)
            eng.affine_select(out=lower[:], in_=lower[:], compare_op=ALU.is_gt, fill=0.0, base=0,
                              pattern=[[1, P]], channel_multiplier=-1).then_inc(s_cst, 1)
            eng.iota(iota_e[:], pattern=[[0, 2], [0, TOPK], [1, E]], base=0, channel_multiplier=0,
                     allow_small_or_imprecise_dtypes=True).then_inc(s_cst, 1)
            eng.iota(slot_a[:], pattern=[[0, 2], [CAP, E]], base=0, channel_multiplier=0,
                     allow_small_or_imprecise_dtypes=True).then_inc(s_cst, 1)
            eng.iota(slot_b[:], pattern=[[0, 2], [T - CAP, E]], base=2 * SLOTS, channel_multiplier=0,
                     allow_small_or_imprecise_dtypes=True).then_inc(s_cst, 1)
            eng.wait_ge(s_cst, 8)
            eng.wait_ge(s_tb, 16 * 4)
            eng.tensor_scalar(cb_t[:, 0], cb_t[:, 0], 1.0, None, ALU.add).then_inc(s_tab, 1)

            def rsqrt(i):
                hold(eng, passed, s_st, 5 * (i + 1))
                eng.tensor_tensor(rstd[:], veps[:], mhalf[:], ALU.pow).then_inc(s_rstd, 1)

            def send(i, q, r):
                hold(eng, passed, s_sl, i + 1)
                send_rows(eng, xe_d, first, q, r)

            rsqrt(0)

            def body(i, q, b):
                if exists(i + 1):
                    rsqrt(i + 1)
                if not (isinstance(i, int) and i == 0):
                    send(i - 1, 1 - q, 1)
                if exists(i + 1):
                    send(i, q, 0)
                if isinstance(i, int) and i == 0:
                    eng.wait_ge(s_tb1, 16 * (3 + B))
                    eng.tensor_scalar(cb_t[:, 1], cb_t[:, 1], 1.0, None, ALU.add).then_inc(s_tab, 1)

            each_pair(eng, body)

        @block.tensor
        def _(eng):
            def project(i, r):
                ge(eng, s_ctl, 2 * i + (r + 1))
                ge(eng, s_x1a, 2 * i + (r - 1))
                for k in range(KT):
                    for m, (a, w) in enumerate(((ct_h, wp_h), (ct_h, wp_l), (ct_l, wp_h))):
                        eng.matmul(ps_y[r][:], a[:, r, k, :], w[:, k, :],
                                   start=(k == 0 and m == 0), stop=False)
                eng.matmul(ps_y[r][:], one_row[:], bp_h[:], start=False, stop=False)
                eng.matmul(ps_y[r][:], one_row[:], bp_l[:], start=False, stop=True).then_inc(s_py, 1)

            def transposes(i, q):
                for r in range(2):
                    ge(eng, s_h2, 2 * i + (r + 1))
                    ge(eng, s_h2h, 2 * i + (r - 1))
                    for k in range(KT):
                        tr = eng.transpose(ps_h[r][:, k * P:(k + 1) * P], h2[:, q, r, k * P:(k + 1) * P],
                                           ident[:])
                    tr.then_inc(s_tr, 1)

            def logits(i):
                ge(eng, s_ex, 3 * i)
                for r in range(2):
                    ge(eng, s_h2t, 2 * i + (r + 1))
                    for k in range(KT):
                        mm = eng.matmul(ps_r[:, r, 0:E + 1], h2t[:, r, k, :], wrse[:, k, :],
                                        start=(k == 0), stop=(k == KT - 1))
                mm.then_inc(s_lg, 1)

            def positions(i):
                ge(eng, s_mk, 3 * i + 1)
                ge(eng, s_sl, i)
                eng.matmul(ps_p[:, 0, 0:E], lower[:], mask[:, 0], start=True, stop=False)
                eng.matmul(ps_p[:, 0, 0:E], ones[:], seen[:], start=False, stop=True)
                eng.matmul(ps_p[:, 1, 0:E], lower[:], mask[:, 1], start=True, stop=False)
                eng.matmul(ps_p[:, 1, 0:E], ones[:], mask[:, 0], start=False, stop=False)
                eng.matmul(ps_p[:, 1, 0:E], ones[:], seen[:], start=False, stop=True).then_inc(s_pos, 1)

            eng.wait_ge(s_bps, 3)
            for i in range(2):
                for r in range(2):
                    project(i, r)
            eng.wait_ge(s_cst, 8)
            transposes(0, 0)
            eng.wait_ge(s_tb, 16 * 4)
            logits(0)

            def body(i, q, b):
                if exists(i + 2):
                    project(i + 2, 0)
                positions(i)
                if exists(i + 2):
                    project(i + 2, 1)
                if exists(i + 1):
                    transposes(i + 1, 1 - q)
                    logits(i + 1)

            each_pair(eng, body)

        @block.scalar
        def _(eng):
            def split(i):
                for r in range(2):
                    ge(eng, s_ct[r], 16 * (i + 1))
                    ge(eng, s_py, 2 * i + (r - 1))
                    eng.activation(ct_h[:, r], ct[:, r], ACT.Copy).then_inc(s_cth, 1)

            def copies(i):
                for r in range(2):
                    ge(eng, s_tr, 2 * i + (r + 1))
                    ge(eng, s_lg, i)
                    ge(eng, s_h2l, 2 * i)
                    eng.activation(h2t[:, r].rearrange("p k n -> p (k n)"), ps_h[r][:], ACT.Copy)\
                        .then_inc(s_h2t, 1)
                    eng.activation(h2h[:, :, at((2 * i + r) * P, P)],
                                   ps_h[r][:].rearrange("p (k n) -> p k n", k=KT), ACT.Copy)\
                        .then_inc(s_h2h, 1)

            def exps(i):
                ge(eng, s_nm, i + 1)
                for r in range(2):
                    eng.activation(ex[:, r], ps_r[:, r, 0:E], ACT.Exp, bias=nmax[:, r:r + 1],
                                   accum_out=esum[:, r:r + 1]).then_inc(s_ex, 1)
                eng.activation(ese[:], ps_r[:, :, E], ACT.Exp, scale=-1.0).then_inc(s_ex, 1)

            split(0)
            split(1)
            copies(0)

            def body(i, q, b):
                if exists(i + 2):
                    split(i + 2)
                exps(i)
                if exists(i + 1):
                    copies(i + 1)

            each_pair(eng, body)

        @block.vector
        def _(eng):
            STEPS = 14

            def low_ct(i):
                for r in range(2):
                    ge(eng, s_cth, 2 * i + (r + 1))
                    ge(eng, s_py, 2 * i + (r - 1))
                    eng.tensor_tensor(ct_l[:, r], ct[:, r], ct_h[:, r].bitcast(F32), ALU.subtract)\
                        .then_inc(s_ctl, 1)

            def residual(i, b):
                for r in range(2):
                    ge(eng, s_py, 2 * i + (r + 1))
                    ge(eng, s_x1s[r], 16 * i)
                    ge(eng, s_xh, 2 * i)
                    eng.tensor_tensor(x1[:, r], ps_y[r][:], table(ga_t, b), ALU.mult).then_inc(s_x1a, 1)
                for r in range(2):
                    ge(eng, s_xt[r], 16 * (i + 1))
                    ge(eng, s_x1a, 2 * i + (r + 1))
                    eng.tensor_tensor(x1[:, r], x1[:, r], xt[:, r], ALU.add).then_inc(s_x1, 1)
                for r in range(2):
                    ge(eng, s_x1, 2 * i + (r + 1))
                    eng.bn_stats(stats[:, r], x1[:, r]).then_inc(s_st, 1)
                for r in range(2):
                    hold(eng, passed, s_st, 5 * i + (r + 1))
                    eng.bn_aggr(mv[:, r], stats[:, r]).then_inc(s_st, 1)
                ge(eng, s_st, 5 * i + 4)
                ge(eng, s_rstd, i)
                eng.tensor_scalar(veps[:], mv[:, :, 1], EPS, None, ALU.add).then_inc(s_st, 1)

            def modulate(i, q, b):
                for r in range(2):
                    ge(eng, s_h2, 2 * i)
                    eng.scalar_tensor_tensor(out=xhat[:, r], in0=x1[:, r], scalar=mv[:, r, 0:1],
                                             in1=table(cb_t, b), op0=ALU.subtract, op1=ALU.mult)\
                        .then_inc(s_xh, 1)
                ge(eng, s_rstd, i + 1)
                for r in range(2):
                    ge(eng, s_xh, 2 * i + (r + 1))
                    if not (isinstance(i, int) and i < 2):
                        ge(eng, s_tr, 2 * i - 2)
                        ge(eng, s_sc[q][r], (8 * TOPK) * i - 8 * TOPK * q)
                    eng.scalar_tensor_tensor(out=h2[:, q, r], in0=xhat[:, r], scalar=rstd[:, r:r + 1],
                                             in1=table(sb_t, b), op0=ALU.mult, op1=ALU.add)\
                        .then_inc(s_h2, 1)

            def router_max(i):
                ge(eng, s_lg, i + 1)
                ge(eng, s_ex, 3 * i)
                eng.tensor_reduce(nmax[:], ps_r[:, :, 0:E], AX.X, ALU.max, negate=True).then_inc(s_nm, 1)

            def low(i):
                for r in range(2):
                    ge(eng, s_h2h, 2 * i + (r + 1))
                    cols = at((2 * i + r) * P, P)
                    eng.tensor_tensor(h2l[:, :, cols], h2t[:, r], h2h[:, :, cols].bitcast(F32),
                                      ALU.subtract).then_inc(s_h2l, 1)

            def route(i, q):
                def step(n, ins):
                    ins.then_inc(s_rt, 1)

                def after(n, alone=False):
                    if alone:
                        hold(eng, passed, s_rt, STEPS * i + n)
                    else:
                        ge(eng, s_rt, STEPS * i + n)

                ge(eng, s_ex, 3 * i + 3)
                step(1, eng.reciprocal(esum[:], esum[:]))
                step(2, eng.tensor_scalar(ese[:], ese[:], 1.0, None, ALU.add))
                after(1)
                step(3, eng.tensor_tensor(prb[:], ex[:], esum[:].unsqueeze(2).to_broadcast([P, 2, E]),
                                          ALU.mult))
                after(3, alone=True)
                for r in range(2):
                    mxi = eng.max(top8[:, r], prb[:, r])
                step(4, mxi)
                after(4, alone=True)
                for r in range(2):
                    mxi = eng.max_index(idx8[:, r], top8[:, r], prb[:, r])
                step(5, mxi)
                eng.reciprocal(sgate[:, at(2 * i, 2)], ese[:])
                after(5)
                step(6, eng.tensor_copy(idxf[:], idx8[:, :, 0:TOPK]))
                eng.tensor_reduce(wsum[:], top8[:, :, 0:TOPK], AX.X, ALU.add)
                after(6)
                step(7, eng.tensor_tensor(onehot[:], iota_e[:],
                                          idxf[:].unsqueeze(3).to_broadcast([P, 2, TOPK, E]), ALU.is_equal))
                after(7)
                with nc.allow_low_precision(reason="sums of a one and three zeros are exact"):
                    eng.tensor_reduce(mask[:], onehot[:].rearrange("p r k e -> p r e k"), AX.X, ALU.add)\
                        .then_inc(s_mk, 1)
                step(8, eng.reciprocal(wsum[:], wsum[:]))
                after(8)
                step(9, eng.tensor_tensor(wnorm[:], top8[:, :, 0:TOPK],
                                          wsum[:].unsqueeze(2).to_broadcast([P, 2, TOPK]), ALU.mult))
                ge(eng, s_pos, i + 1)
                eng.tensor_tensor(seen[:], seen[:], mask[:, 0], ALU.add).then_inc(s_mk, 1)
                eng.scalar_tensor_tensor(out=over[:], in0=ps_p[:, :, 0:E], scalar=float(CAP),
                                         in1=slot_b[:], op0=ALU.is_ge, op1=ALU.mult)
                step(10, eng.tensor_tensor(slotv[:], ps_p[:, :, 0:E], slot_a[:], ALU.add))
                ge(eng, s_mk, 3 * i + 2)
                eng.tensor_tensor(seen[:], seen[:], mask[:, 1], ALU.add).then_inc(s_mk, 1)
                after(10)
                step(11, eng.tensor_tensor(slotv[:], slotv[:], over[:], ALU.add))
                after(11)
                step(12, eng.tensor_tensor(pick[:], onehot[:],
                                           slotv[:].unsqueeze(2).to_broadcast([P, 2, TOPK, E]), ALU.mult))
                after(12)
                step(13, eng.tensor_reduce(slotf[:], pick[:], AX.X, ALU.add))
                after(13)
                step(14, eng.scalar_tensor_tensor(out=wtop[:, at(2 * i, 2), :], in0=slotf[:],
                                                  scalar=float(SLOTS), in1=wnorm[:],
                                                  op0=ALU.is_lt, op1=ALU.mult))
                if not (isinstance(i, int) and i < 2):
                    for r in range(2):
                        ge(eng, s_sc[q][r], (8 * TOPK) * i - 8 * TOPK * q)
                eng.tensor_copy(slots[:, at(2 * i, 2), :], slotf[:])
                eng.tensor_copy(slot_i[:, q], slotf[:]).then_inc(s_sl, 1)

            eng.memset(one_row[:].bitcast(F32), 1.0).then_inc(s_bps, 1)
            low_ct(0)
            eng.wait_ge(s_bp, 16)
            eng.tensor_copy(bp_h[:], bp_raw[:]).then_inc(s_bps, 1)
            eng.wait_ge(s_bps, 2)
            eng.tensor_tensor(bp_l[:], bp_raw[:], bp_h[:].bitcast(F32), ALU.subtract).then_inc(s_bps, 1)
            eng.wait_ge(s_tb, 16 * 4)
            residual(0, 0)
            low_ct(1)
            eng.wait_ge(s_tab, 1)
            modulate(0, 0, 0)
            eng.wait_ge(s_cst, 8)

            def body(i, q, b):
                if exists(i + 1):
                    residual(i + 1, b)
                if exists(i + 2):
                    low_ct(i + 2)
                router_max(i)
                low(i)
                route(i, q)
                if exists(i + 1):
                    modulate(i + 1, 1 - q, b)
                if isinstance(i, int) and i == 1:
                    eng.wait_ge(s_tab, 2)

            each_pair(eng, body)


def ffn(nc, first, wp_h, wsh, wgu, wd_a, wd_b, x1_d, res_d, xe_d, ye_d, gb_rows, ident, sgate, h2h, h2l,
        slots, wtop, gbt, out):
    QC = HALF // P
    FIRST_POINTS = (2, 5, 8, 12, 15, 18)
    LATER_POINTS = (2, 6, 10, 14, 18)
    SLOT_USES = [len(range(s, FT, 3)) for s in range(3)]
    POINTS = 2 * FT - 2
    HALVES = [0, 0] + [(2 * TT * (p + 1)) // POINTS - (2 * TT * p) // POINTS for p in range(POINTS)]

    def expert_pair(c, q):
        return q if isinstance(c, int) and c == 0 else len(LATER_POINTS) * c + (
            len(FIRST_POINTS) - len(LATER_POINTS) + q)

    def at_point(c, last, p):
        starts = () if last else FIRST_POINTS if isinstance(c, int) and c == 0 else LATER_POINTS
        return [(expert_pair(c, q), p - p0, q, len(starts)) for q, p0 in enumerate(starts)
                if 0 <= p - p0 < 4]

    def before(n, j):
        return n - 3 if j >= 3 else n - (j + 1 + (FT - 1 - j) % 3)

    with ExitStack() as ctx:
        def sb(name, shape, dt=F32):
            return ctx.enter_context(nc.sbuf_tensor(name, shape, dt))

        def sem(name):
            return ctx.enter_context(nc.semaphore(name))

        def psum(name):
            return ctx.enter_context(nc.psum_tensor(name, [P, HALF], F32))

        w_raw = first["w_raw"]
        w_h = sb("ws_h", [P, 3, 3 * D], F32R)
        w_l = sb("ws_l", [P, 3, 3 * D], F32R)
        sil = sb("sil", [P, HALF])
        gu = sb("gu", [P, HALF])
        gu_h, gu_l = wp_h[:, 0:2], wp_h[:, 2:4]
        res = sb("res", [P, QC, D])
        tmp = sb("tmp", [P, D])
        gbc = sb("gbc", [P, D])
        e_gu = sb("e_gu", [P, 2, 2, KT, F])
        e_da = sb("e_da", [P, 2, 2, D])
        e_db = sb("e_db", [F - 2 * P, 2, D])
        e_x = sb("e_x", [P, D])
        e_xt = sb("e_xt", [P, KT, P])
        e_sil = sb("e_sil", [P, F])
        e_h = sb("e_h", [P, F])
        e_ht = sb("e_ht", [P, 3, P])
        e_y = sb("e_y", [P, D])
        free = e_gu[:].rearrange("p a b k f -> p (a b k f)")
        got = [[free[:, (TOPK * g + k) * D:(TOPK * g + k + 1) * D] for k in range(TOPK)] for g in range(2)]
        got.append([e_da[:, k // 2, k % 2, :] for k in range(TOPK)])
        GOT = len(got)
        rest = [free[:, (2 * TOPK + g) * D:(2 * TOPK + g + 1) * D] for g in range(2)]
        total = [e_x, e_y]
        acc = [psum(f"ps_acc{n}") for n in range(QC)]
        ps_g, ps_u, ps_m0, ps_m1 = psum("ps_gate"), psum("ps_up"), psum("ps_m0"), psum("ps_m1")

        s_wl = first["s_wl"]
        s_lgu = sem("expert_gate_up_loaded")
        s_ld = sem("expert_down_loaded")
        s_wh = sem("ws_high")
        s_ws = sem("ws_split")
        s_g = sem("gate_done")
        s_u = sem("up_done")
        s_sil = sem("silu_done")
        s_gu = sem("gu_ready")
        s_guh = sem("gu_high")
        s_gul = sem("gu_low")
        s_dn = sem("down_done")
        s_x1 = sem("x1_chunk_loaded")
        s_gb = sem("gb_loaded")
        s_tmp = sem("shared_gated")
        s_res = sem("res_ready")
        s_rst = sem("res_stored")
        s_lx = sem("expert_tokens_loaded")
        s_e0 = sem("expert_tokens_transposed")
        s_ext = sem("expert_tokens_copied")
        s_e1 = sem("expert_gate_up_done")
        s_esl = sem("expert_silu_done")
        s_eh = sem("expert_hidden_ready")
        s_e2 = sem("expert_hidden_transposed")
        s_eht = sem("expert_hidden_copied")
        s_e3 = sem("expert_down_done")
        s_ey = sem("expert_rows_copied")
        s_yst = sem("expert_rows_stored")
        s_zero = sem("got_zeroed")
        s_got = [sem(f"rows_got{g}") for g in range(GOT)]
        s_rest = [sem("rest_loaded0"), sem("rest_loaded1")]
        s_one = sem("first_rows_weighted")
        s_sum = sem("sum_step")
        s_tot = sem("total_ready")
        s_out = [sem("out_stored0"), sem("out_stored1")]
        s_fin = sem("last_rows_stored")
        out_t = out.rearrange("b s d -> (b s) d")
        REST = TT - QC

        def each_chunk(eng, body):
            body(0, False)
            with eng.Fori(1, CH - 1) as c:
                body(c, False)
            body(CH - 1, True)

        def rows(at, n):
            return slice(at, at + n) if isinstance(at, int) else bass.ds(at, n)

        def at(a, i):
            return a[i] if isinstance(i, int) else a[bass.ds(i, 1)].rearrange("o p n -> (o p) n")

        passed = sem("waits_passed")
        block = ctx.enter_context(nc.Block())

        @block.sync
        def _(eng):
            def load_shared(n, j):
                hold(eng, passed, s_ws, before(n, j) + 1)
                eng.dma_start(w_raw[:, j % 3], wsh[j]).then_inc(s_wl[j % 3], 16)

            def load_gu(e):
                hold(eng, passed, s_e1, e)
                eng.dma_start(e_gu[:].rearrange("p a b k f -> p (a b k f)"), at(wgu, e)).then_inc(s_lgu, 16)

            def load_x(e):
                hold(eng, passed, s_e0, e)
                eng.dma_start(e_x[:], xe_d[rows(e * P, P), :]).then_inc(s_lx, 16)

            def load_down(e):
                hold(eng, passed, s_e3, e)
                eng.dma_start(e_da[:].rearrange("p a b n -> p (a b n)"), at(wd_a, e)).then_inc(s_ld, 16)
                eng.dma_start(e_db[:].rearrange("p a n -> p (a n)"), at(wd_b, e)).then_inc(s_ld, 16)

            def store_y(e):
                hold(eng, passed, s_ey, e + 1)
                eng.dma_start(ye_d[rows(e * P, P), :], e_y[:]).then_inc(s_yst, 16)

            load_shared(2, 2)
            for r in range(2):
                for q in range(2):
                    eng.wait_ge(first["s_sc"][q][r], 16 * TOPK * TT // 4)
            load_x(0)
            load_gu(0)
            load_shared(3, 3)
            load_down(0)

            def store_res(c):
                hold(eng, passed, s_res, QC * (c + 1))
                for q in range(QC):
                    eng.dma_start(res_d[rows(c * HALF + q * P, P), :], res[:, q]).then_inc(s_rst, 16)

            def load_rest(t):
                ge(eng, s_tot, t - 1)
                eng.dma_start(rest[t % 2], res_d[rows(t * P, P), :]).then_inc(s_rest[t % 2], 16)

            def body(c, last):
                first = isinstance(c, int) and c == 0
                if not first:
                    for j in (2, 3):
                        load_shared(FT * c + j, j)
                if last:
                    eng.wait_ge(s_e1, E // 2)
                    for n in range(2):
                        load_rest(n)
                if not (first or last):
                    e = expert_pair(c, 0)
                    load_x(e)
                    load_gu(e)
                    load_down(e)
                if not first:
                    store_res(c - 1)
                hold(eng, passed, s_rst, 16 * QC * c)
                for q in range(QC):
                    eng.dma_start(res[:, q], x1_d[rows(c * HALF + q * P, P), :]).then_inc(s_x1, 16)
                hold(eng, passed, s_tmp, QC * c)
                src = gb_rows[rows(c, 1), :]
                eng.dma_start(gbc[:], src.to_broadcast([P, D])).then_inc(s_gb, 16)
                for j in range(FT):
                    n = FT * c + j
                    if j >= 2 and not (last and j + 2 >= FT):
                        load_shared(n + 2, (j + 2) % FT)
                    for point in (2 * j, 2 * j + 1):
                        for e, stage, q, count in at_point(c, last, point):
                            more = q < count - 1
                            if stage == 0 and more:
                                load_x(e + 1)
                            if stage == 1 and more:
                                load_gu(e + 1)
                            if stage == 3:
                                if more:
                                    load_down(e + 1)
                                store_y(e)
                    for h in range(sum(HALVES[0:2 * j]), sum(HALVES[0:2 * j + 2]) if last else 0):
                        if h % 2 == 1 and h // 2 < REST:
                            t = h // 2
                            ge(eng, s_tot, t + 1)
                            eng.dma_start(out_t[rows(t * P, P), :], total[t % 2][:])\
                                .then_inc(s_out[t % 2], 16)
                            if t + 2 < REST:
                                load_rest(t + 2)

            each_chunk(eng, body)
            for q in range(QC):
                eng.wait_ge(s_res, QC * (CH - 1) + q + 1)
                eng.dma_start(out_t[rows((REST + q) * P, P), :], res[:, q]).then_inc(s_fin, 16)
            for g in range(2):
                eng.wait_ge(s_out[g], 16 * (REST // 2))
            eng.wait_ge(s_fin, 16 * QC)

        @block.gpsimd
        def _(eng):
            for r in range(2):
                send_rows(eng, xe_d, first, 1, r)
            eng.wait_ge(s_e1, E // 2)
            eng.memset(free[:, 0:2 * TOPK * D], 0.0).then_inc(s_zero, 1)
            eng.wait_ge(s_e3, E // 2)
            eng.memset(e_da[:], 0.0).then_inc(s_zero, 1)
            eng.wait_ge(s_zero, 2)
            eng.wait_ge(s_yst, 16 * E // 2)
            for t in range(TT):
                ge(eng, s_tot, t - GOT + 1)
                for k in range(TOPK):
                    eng.indirect_dma_start(
                        out=got[t % GOT][k], out_offset=None, in_=ye_d,
                        in_offset=bass.IndirectOffsetOnAxis(ap=slots[:, t, k:k + 1], axis=0),
                        bounds_check=SLOTS - 1, oob_is_err=False).then_inc(s_got[t % GOT], 16)

        @block.tensor
        def _(eng):
            def gate_up(c, n, j):
                ge(eng, s_ws, n + 1)
                for part, (bank, done, free) in enumerate(((ps_g, s_g, s_sil), (ps_u, s_u, s_gu))):
                    ge(eng, free, n)
                    for k in range(KT):
                        col = part * D + k * P
                        for m, (w, h) in enumerate(((w_h, h2h), (w_l, h2h), (w_h, h2l))):
                            mm = eng.matmul(bank[:], w[:, j % 3, col:col + P],
                                            h[:, k, rows(c * HALF, HALF)],
                                            start=(k == 0 and m == 0), stop=(k == KT - 1 and m == 2))
                    mm.then_inc(done, 1)

            def down(c, n, j):
                ge(eng, s_guh, n + 1)
                ge(eng, s_gul, n + 1)
                if j == 0:
                    ge(eng, s_tmp, QC * c)
                for q in range(QC):
                    for m, (g, w) in enumerate(((gu_h, w_h), (gu_h, w_l), (gu_l, w_h))):
                        mm = eng.matmul(acc[q][:], g[:, j % 2, q * P:(q + 1) * P],
                                        w[:, j % 3, 2 * D:3 * D],
                                        start=(j == 0 and m == 0), stop=(j == FT - 1 and m == 2))
                mm.then_inc(s_dn, 1)

            def stage0(e):
                ge(eng, s_lx, 16 * (e + 1))
                ge(eng, s_eht, 2 * e)
                for k in range(KT):
                    mm = eng.transpose(ps_m0[:, k * P:(k + 1) * P], e_x[:, k * P:(k + 1) * P], ident[:])
                mm.then_inc(s_e0, 1)

            def stage1(e):
                ge(eng, s_ext, e + 1)
                ge(eng, s_lgu, 16 * (e + 1))
                ge(eng, s_ey, e)
                for part, bank in enumerate((ps_m0, ps_m1)):
                    for k in range(KT):
                        for a in range(2):
                            mm = eng.matmul(bank[CAP * a:CAP * (a + 1), 0:F], e_xt[:, k, CAP * a:CAP * (a + 1)],
                                            e_gu[:, part, a, k, :], start=(k == 0), stop=(k == KT - 1))
                mm.then_inc(s_e1, 1)

            def stage2(e):
                ge(eng, s_eh, e + 1)
                for n, (f0, fs) in enumerate(F_TILES):
                    mm = eng.transpose(ps_m0[0:fs, n * P:(n + 1) * P], e_h[:, f0:f0 + fs], ident[:])
                mm.then_inc(s_e2, 1)

            def stage3(e):
                ge(eng, s_eht, 2 * (e + 1))
                ge(eng, s_ld, 32 * (e + 1))
                for n, (f0, fs) in enumerate(F_TILES):
                    for a in range(2):
                        w = e_da[:, a, n, :] if n < 2 else e_db[:, a, :]
                        mm = eng.matmul(ps_m1[CAP * a:CAP * (a + 1), :], e_ht[0:fs, n, CAP * a:CAP * (a + 1)],
                                        w, start=(n == 0), stop=(n == 2))
                mm.then_inc(s_e3, 1)

            stages = (stage0, stage1, stage2, stage3)

            def body(c, last):
                def point(p):
                    for e, stage, _, _ in at_point(c, last, p):
                        stages[stage](e)

                for j in range(FT):
                    n = FT * c + j
                    gate_up(c, n, j)
                    point(2 * j)
                    if j >= 1:
                        down(c, n - 1, j - 1)
                    point(2 * j + 1)
                down(c, FT * c + (FT - 1), FT - 1)

            each_chunk(eng, body)

        @block.scalar
        def _(eng):
            def split(n, j, use):
                ge(eng, s_wl[j % 3], use * 16)
                ge(eng, s_dn, before(n, j) + 1)
                eng.activation(w_h[:, j % 3], w_raw[:, j % 3], ACT.Copy).then_inc(s_wh, 1)

            split(0, 0, 1)

            def first_row(t):
                g = t % 2
                ge(eng, s_got[t % GOT], 16 * TOPK * (t // GOT + 1))
                ge(eng, s_out[g], 16 * min(t // 2, REST // 2))
                ge(eng, s_tot, t - 1)
                eng.activation(total[g][:], got[t % GOT][0], ACT.Copy, scale=wtop[:, t, 0:1]).then_inc(s_one, 1)

            def body(c, last):
                def point(p):
                    for e, stage, _, _ in at_point(c, last, p):
                        expert(e, stage)
                    for h in range(sum(HALVES[0:p]), sum(HALVES[0:p + 1]) if last else 0):
                        if h % 2 == 0:
                            first_row(h // 2)

                def expert(e, stage):
                    if stage == 0:
                        ge(eng, s_e0, e + 1)
                        ge(eng, s_e1, e)
                        eng.activation(e_xt[:].rearrange("p k n -> p (k n)"), ps_m0[:], ACT.Copy)\
                            .then_inc(s_ext, 1)
                    if stage == 1:
                        ge(eng, s_e1, e + 1)
                        ge(eng, s_eh, e)
                        eng.activation(e_sil[:], ps_m0[:, 0:F], ACT.Silu).then_inc(s_esl, 1)
                    if stage == 3:
                        ge(eng, s_e3, e + 1)
                        ge(eng, s_yst, 16 * e)
                        eng.activation(e_y[:], ps_m1[:], ACT.Copy).then_inc(s_ey, 1)

                for j in range(FT):
                    n = FT * c + j
                    if j < FT - 1:
                        split(n + 1, j + 1, SLOT_USES[(j + 1) % 3] * c + ((j + 1) // 3 + 1))
                    ge(eng, s_g, n + 1)
                    ge(eng, s_gu, n)
                    eng.activation(sil[:], ps_g[:], ACT.Silu).then_inc(s_sil, 1)
                    point(2 * j)
                    ge(eng, s_gu, n + 1)
                    ge(eng, s_dn, n if j == 0 else n - 1)
                    eng.activation(gu_h[:, j % 2], gu[:], ACT.Copy).then_inc(s_guh, 1)
                    if j == FT - 1 and not last:
                        split(n + 1, 0, SLOT_USES[0] * c + (SLOT_USES[0] + 1))
                    point(2 * j + 1)

            each_chunk(eng, body)

        @block.vector
        def _(eng):
            def split(n, j):
                ge(eng, s_wh, n + 1)
                eng.tensor_tensor(w_l[:, j % 3], w_raw[:, j % 3], w_h[:, j % 3].bitcast(F32),
                                  ALU.subtract).then_inc(s_ws, 1)

            def combine(t, half):
                g, q = t % 2, t - REST
                STEPS = 4

                def add(k):
                    eng.scalar_tensor_tensor(out=total[g][:], in0=got[t % GOT][k],
                                             scalar=wtop[:, t, k:k + 1], in1=total[g][:],
                                             op0=ALU.mult, op1=ALU.add).then_inc(s_sum, 1)

                if half == 0:
                    ge(eng, s_one, t + 1)
                    add(1)
                    ge(eng, s_sum, STEPS * t + 1)
                    add(2)
                    return
                ge(eng, s_sum, STEPS * t + 2)
                add(3)
                ge(eng, s_sum, STEPS * t + 3)
                eng.tensor_tensor(total[g][:], total[g][:], gbt[:, t // (TT // B)], ALU.mult)\
                    .then_inc(s_sum, 1)
                ge(eng, s_sum, STEPS * t + 4)
                if t < REST:
                    ge(eng, s_rest[g], 16 * (t // 2 + 1))
                    eng.tensor_tensor(total[g][:], total[g][:], rest[g], ALU.add).then_inc(s_tot, 1)
                else:
                    ge(eng, s_x1, 16 * QC * CH)
                    eng.tensor_tensor(res[:, q], total[g][:], res[:, q], ALU.add).then_inc(s_tot, 1)

            split(0, 0)
            split(1, 1)

            def body(c, last):
                def point(p):
                    for e, stage, _, _ in at_point(c, last, p):
                        expert(e, stage)
                    for h in range(sum(HALVES[0:p]), sum(HALVES[0:p + 1]) if last else 0):
                        combine(h // 2, h % 2)

                def expert(e, stage):
                    if stage == 1:
                        ge(eng, s_esl, e + 1)
                        ge(eng, s_e2, e)
                        eng.tensor_tensor(e_h[:], e_sil[:], ps_m1[:, 0:F], ALU.mult).then_inc(s_eh, 1)
                    if stage == 2:
                        ge(eng, s_e2, e + 1)
                        ge(eng, s_e3, e)
                        eng.tensor_copy(e_ht[:, 0:2, :].rearrange("p a n -> p (a n)"), ps_m0[:, 0:2 * P])\
                            .then_inc(s_eht, 1)
                        eng.tensor_copy(e_ht[0:F - 2 * P, 2, :], ps_m0[0:F - 2 * P, 2 * P:3 * P])\
                            .then_inc(s_eht, 1)

                for j in range(FT):
                    n = FT * c + j
                    if 1 <= j < FT - 1:
                        split(n + 1, j + 1)
                    ge(eng, s_sil, n + 1)
                    ge(eng, s_u, n + 1)
                    ge(eng, s_guh, n)
                    ge(eng, s_gul, n)
                    eng.tensor_tensor(gu[:], sil[:], ps_u[:], ALU.mult).then_inc(s_gu, 1)
                    point(2 * j)
                    ge(eng, s_guh, n + 1)
                    eng.tensor_tensor(gu_l[:, j % 2], gu[:], gu_h[:, j % 2].bitcast(F32), ALU.subtract)\
                        .then_inc(s_gul, 1)
                    if j == FT - 1 and not last:
                        split(n + 1, 0)
                    point(2 * j + 1)
                if last:
                    ge(eng, s_tot, TT)
                else:
                    split(FT * c + (FT + 1), 1)
                ge(eng, s_dn, FT * (c + 1))
                ge(eng, s_x1, 16 * QC * (c + 1))
                ge(eng, s_gb, 16 * (c + 1))
                for q in range(QC):
                    t = QC * c + q
                    ge(eng, s_res, t)
                    eng.scalar_tensor_tensor(out=tmp[:], in0=acc[q][:], scalar=sgate[:, rows(t, 1)],
                                             in1=gbc[:], op0=ALU.mult, op1=ALU.mult).then_inc(s_tmp, 1)
                    ge(eng, s_tmp, t + 1)
                    eng.tensor_tensor(res[:, q], res[:, q], tmp[:], ALU.add).then_inc(s_res, 1)

            each_chunk(eng, body)


def kernel(L0_attn_query, L0_attn_key, L0_attn_value, L0_attn_Wqkv, L0_attn_Wproj, L0_attn_bproj,
           L0_ffn_Wr, L0_ffn_Wg, L0_ffn_Wu, L0_ffn_Wd, L0_ffn_Wsg, L0_ffn_Wsu, L0_ffn_Wsd, L0_ffn_Wse,
           L0_c, L0_wmod):
    import numpy as np
    import concourse.bacc as bacc
    from concourse.bass_utils import run_bass_kernel_spmd

    def tiles(w):
        w = np.asarray(w)
        return w.reshape(-1, P, w.shape[1]).transpose(1, 0, 2)

    wqkv = np.asarray(L0_attn_Wqkv).reshape(NH, 3, HN, D)
    qk = np.stack([np.concatenate([wqkv[2 * u, 0], wqkv[2 * u + 1, 0], wqkv[2 * u, 1], wqkv[2 * u + 1, 1]]).T
                   for u in range(NH // 2)])
    arrays = {
        "x": L0_attn_query,
        "wqk": qk.reshape(NH // 2, KT, P, P).transpose(0, 2, 1, 3),
        "wv": tiles(wqkv[:, 2].reshape(D, D).T),
        "wproj": tiles(np.asarray(L0_attn_Wproj).T),
        "bproj": np.asarray(L0_attn_bproj).reshape(1, D),
        "wr_se": tiles(np.concatenate([L0_ffn_Wr, L0_ffn_Wse], axis=1)),
        "c": np.asarray(L0_c).T.reshape(KT, P, B).transpose(1, 0, 2),
        "wmod": L0_wmod,
    }
    wsg = np.asarray(L0_ffn_Wsg).reshape(KT, P, FT, P).transpose(2, 1, 0, 3).reshape(FT, P, D)
    wsu = np.asarray(L0_ffn_Wsu).reshape(KT, P, FT, P).transpose(2, 1, 0, 3).reshape(FT, P, D)
    arrays["wsh"] = np.concatenate([wsg, wsu, np.asarray(L0_ffn_Wsd).reshape(FT, P, D)], axis=2)
    ep = E // 2
    g4 = [np.asarray(w).reshape(ep, 2, KT, P, F).transpose(0, 3, 1, 2, 4) for w in (L0_ffn_Wg, L0_ffn_Wu)]
    arrays["wgu"] = np.stack(g4, axis=2).reshape(ep, P, 2 * 2 * KT * F)
    wd = np.asarray(L0_ffn_Wd).reshape(ep, 2, F, D)
    arrays["wd_a"] = wd[:, :, :2 * P].reshape(ep, 2, 2, P, D).transpose(0, 3, 1, 2, 4).reshape(ep, P, 4 * D)
    arrays["wd_b"] = wd[:, :, 2 * P:].transpose(0, 2, 1, 3).reshape(ep, F - 2 * P, 2 * D)

    nc = bacc.Bacc("TRN2", target_bir_lowering=False, num_devices=1)
    given, aps = {}, {}
    for name, a in arrays.items():
        a = np.ascontiguousarray(a)
        given[f"in_{name}"] = a
        aps[name] = nc.dram_tensor(f"in_{name}", a.shape, mybir.dt.from_np(a.dtype), kind="ExternalInput").ap()
    aps["out"] = nc.dram_tensor("out_0", (B, S, D), F32, kind="ExternalOutput").ap()
    adaln_kernel(nc, **aps)
    r = run_bass_kernel_spmd(nc, [given], core_ids=[0])
    return r.results[0]["out_0"]
```
